# Optimizing a Trainium2 kernel written in Bass

```python
import numpy as np
import jax
import jax.numpy as jnp

def _softmax(x, axis=-1):
    return jax.nn.softmax(x, axis=axis)

def _gelu(x):
    return jax.nn.gelu(x, approximate=True)

def _silu(x):
    return jax.nn.silu(x)

def _sigmoid(x):
    return jax.nn.sigmoid(x)

def _layernorm(x, axis=-1, eps=1e-05):
    m = jnp.mean(x, axis=axis, keepdims=True)
    v = jnp.var(x, axis=axis, keepdims=True)
    return (x - m) / jnp.sqrt(v + eps)

def _scatter_add(tgt, idx, src, axis=0):
    return tgt.at[idx].add(src)

def _segment_sum(src, seg, n):
    return jax.ops.segment_sum(src, seg, n)
kernel_name = 'mk_perceiver_d2_seqx_r4_25954d'

def setup_inputs(seed: int=0):
    np.random.seed(seed)
    _w = jnp.asarray

    def _rec_inputs():
        import jax
        import jax.numpy as jnp
        _rk = jax.random.key(seed)
        x = -0.0002928 + 1 * jax.random.normal(jax.random.fold_in(_rk, 1), (1, 256, 256), jnp.float32)
        _lenS = 256 - jax.random.randint(jax.random.fold_in(_rk, 7), (1,), 0, max(1, 256 // 4) + 1, jnp.int32)
        _lenS2 = 4096 - jax.random.randint(jax.random.fold_in(_rk, 8), (1,), 0, max(1, 4096 // 4) + 1, jnp.int32)
        _ctx_1024P = jax.random.normal(jax.random.fold_in(_rk, 11), (1, 16, 256), jnp.float32)
        _ctx_1024c = jax.random.dirichlet(jax.random.fold_in(_rk, 511), 0.3 * jnp.ones((16,), jnp.float32), (1, 4096))
        _ctx_1024t = jnp.einsum('bsk,bkd->bsd', _ctx_1024c, _ctx_1024P)
        _ctx_1024t = _ctx_1024t * jax.lax.rsqrt(jnp.mean(jnp.square(_ctx_1024t)) + 1e-12) * 0.953939
        ctx_1024 = -1.39393e-06 + 0.999914 * (_ctx_1024t + 0.3 * jax.random.normal(jax.random.fold_in(_rk, 611), (1, 4096, 256), jnp.float32))
        fside_Bx16xSxS2_0 = jax.random.uniform(jax.random.fold_in(_rk, 13), (1, 16, 256, 4096), jnp.float32, 0.0, 1)
        _validS = jnp.arange(256)[None, :] < _lenS[:, None]
        _validS2 = jnp.arange(4096)[None, :] < _lenS2[:, None]
        _causal = jnp.tril(jnp.ones((256, 256), dtype=bool))
        mask_Bx16xSxS2_bk1 = jnp.broadcast_to(_validS2[:, None, None, :], (1, 16, 256, 4096))
        mask_Bx1x1xS2_ff0 = jnp.where(jnp.ones((1, 1, 1, 4096), dtype=bool), 0.0, -1000000000.0).astype(jnp.float32)
        return (x, ctx_1024, fside_Bx16xSxS2_0, mask_Bx16xSxS2_bk1, mask_Bx1x1xS2_ff0)
    x, ctx_1024, fside_Bx16xSxS2_0, mask_Bx16xSxS2_bk1, mask_Bx1x1xS2_ff0 = _rec_inputs()

    def _L0_xattn_setup():
        import jax, jax.numpy as jnp
        import numpy as np
        BS, NQ, NK = (2, 512, 512)
        D_OUT, H, D_K, D_V = (256, 16, 64, 64)

        def _xavier(key, shape):
            fan_in, fan_out = (shape[1], shape[0])
            lim = float(np.sqrt(6.0 / (fan_in + fan_out)))
            return jax.random.uniform(key, shape, jnp.float32, -lim, lim)
        key = jax.random.key(seed)
        ks = jax.random.split(key, 9)
        return {'queries': jax.random.normal(ks[0], (BS, NQ, D_OUT), jnp.float32), 'keys': jax.random.normal(ks[1], (BS, NK, D_OUT), jnp.float32), 'values': jax.random.normal(ks[2], (BS, NK, D_OUT), jnp.float32), 'mask': jax.random.randint(ks[3], (BS, H, NQ, NK), 0, 2).astype(bool), 'weights': jax.random.uniform(ks[4], (BS, H, NQ, NK), jnp.float32), 'Wq': _xavier(ks[5], (H * D_K, D_OUT)), 'bq': jnp.zeros((H * D_K,), jnp.float32), 'Wk': _xavier(ks[6], (H * D_K, D_OUT)), 'bk': jnp.zeros((H * D_K,), jnp.float32), 'Wv': _xavier(ks[7], (H * D_V, D_OUT)), 'bv': jnp.zeros((H * D_V,), jnp.float32), 'Wo': _xavier(ks[8], (D_OUT, H * D_V)), 'bo': jnp.zeros((D_OUT,), jnp.float32)}
    _L0_xattn_all = _L0_xattn_setup()
    _L0_xattn_in = {k: v for k, v in _L0_xattn_all.items() if k in ('Wq', 'bq', 'Wk', 'bk', 'Wv', 'bv', 'Wo', 'bo')}
    del _L0_xattn_all

    def _L0_attn_setup():
        import jax, jax.numpy as jnp
        import numpy as np
        B, T, C = (64, 64, 256)
        N_HEAD, HEAD_SIZE, KV_RANK = (16, 64, 128)
        BLOCK_SIZE = 64
        key = jax.random.key(seed)
        ks = jax.random.split(key, 5)
        HD = N_HEAD * HEAD_SIZE

        def init(k, shape):
            fan_in = shape[0]
            bound = 1.0 / np.sqrt(fan_in)
            return jax.random.uniform(k, shape, jnp.float32, -bound, bound)
        return {'x': jax.random.normal(ks[0], (B, T, C), jnp.float32), 'w_kv_down': init(ks[1], (C, KV_RANK)), 'w_kv_up': init(ks[2], (KV_RANK, 2 * HD)), 'w_q': init(ks[3], (C, HD)), 'w_out': init(ks[4], (HD, C))}
    _L0_attn_all = _L0_attn_setup()
    _L0_attn_in = {k: v for k, v in _L0_attn_all.items() if k in ('w_kv_down', 'w_kv_up', 'w_q', 'w_out')}
    del _L0_attn_all

    def _L0_ffn_setup():
        import jax, jax.numpy as jnp
        import numpy as np
        D_MODEL, D_FF, RANK = (256, 1024, 64)
        B, S = (4, 1024)
        key = jax.random.key(seed)
        ks = jax.random.split(key, 7)
        return {'x': jax.random.normal(ks[0], (B, S, D_MODEL), dtype=jnp.float32), 'U1': jax.random.normal(ks[1], (D_MODEL, RANK), dtype=jnp.float32) * 0.02, 'V1': jax.random.normal(ks[2], (RANK, D_FF), dtype=jnp.float32) * 0.02, 'b1': jnp.zeros((D_FF,), dtype=jnp.float32), 'U2': jax.random.normal(ks[3], (D_FF, RANK), dtype=jnp.float32) * 0.02, 'V2': jax.random.normal(ks[4], (RANK, D_MODEL), dtype=jnp.float32) * 0.02, 'b2': jnp.zeros((D_MODEL,), dtype=jnp.float32)}
    _L0_ffn_all = _L0_ffn_setup()
    _L0_ffn_in = {k: v for k, v in _L0_ffn_all.items() if k in ('U1', 'V1', 'b1', 'U2', 'V2', 'b2')}
    del _L0_ffn_all

    def _L1_xattn_setup():
        import jax, jax.numpy as jnp
        import numpy as np
        H = 16
        D = 256
        F = 1024
        LN_EPS = 1e-05

        def _glorot(key, shape):
            fan_in, fan_out = (shape[0], shape[1])
            lim = np.sqrt(6.0 / (fan_in + fan_out))
            return jax.random.uniform(key, shape, jnp.float32, -lim, lim)

        def _split_heads(x):
            b, l, _ = x.shape
            return x.reshape(b, l, H, D // H)

        def _mha(x, ctx, mask, qw, qb, kw, kb, vw, vb):
            q = _split_heads(x @ qw + qb)
            k = _split_heads(ctx @ kw + kb)
            v = _split_heads(ctx @ vw + vb)
            scores = jnp.einsum('bqhd,bkhd->bhqk', q, k) / np.sqrt(D // H).astype(np.float32)
            if mask is not None:
                scores = scores + mask
            probs = jax.nn.softmax(scores, axis=-1)
            out = jnp.einsum('bhqk,bkhd->bqhd', probs, v)
            return out.reshape(x.shape[0], x.shape[1], D)

        def _self_output(h, residual, w, b, g, be):
            h = h @ w + b
            h = h + residual
            mu = jnp.mean(h, axis=-1, keepdims=True)
            var = jnp.mean(jnp.square(h - mu), axis=-1, keepdims=True)
            return (h - mu) * jax.lax.rsqrt(var + LN_EPS) * g + be
        key = jax.random.key(seed)
        ks = jax.random.split(key, 16)
        inp = {'input_tensor': jax.random.normal(ks[0], (4, 256, D), jnp.float32), 'ctx_tensor': jax.random.normal(ks[1], (4, 512, D), jnp.float32), 'ctx_attn_mask': jnp.zeros((4, 1, 1, 512), jnp.float32), 'cq_w': _glorot(ks[2], (D, D)), 'cq_b': jnp.zeros((D,)), 'ck_w': _glorot(ks[3], (D, D)), 'ck_b': jnp.zeros((D,)), 'cv_w': _glorot(ks[4], (D, D)), 'cv_b': jnp.zeros((D,)), 'co_w': _glorot(ks[5], (D, D)), 'co_b': jnp.zeros((D,)), 'co_g': jnp.ones((D,)), 'co_be': jnp.zeros((D,)), 'sq_w': _glorot(ks[6], (D, D)), 'sq_b': jnp.zeros((D,)), 'sk_w': _glorot(ks[7], (D, D)), 'sk_b': jnp.zeros((D,)), 'sv_w': _glorot(ks[8], (D, D)), 'sv_b': jnp.zeros((D,)), 'so_w': _glorot(ks[9], (D, D)), 'so_b': jnp.zeros((D,)), 'so_g': jnp.ones((D,)), 'so_be': jnp.zeros((D,)), 'fi_w': _glorot(ks[10], (D, F)), 'fi_b': jnp.zeros((F,)), 'fo_w': _glorot(ks[11], (F, D)), 'fo_b': jnp.zeros((D,)), 'fo_g': jnp.ones((D,)), 'fo_be': jnp.zeros((D,))}
        return inp
    _L1_xattn_all = _L1_xattn_setup()
    _L1_xattn_in = {k: v for k, v in _L1_xattn_all.items() if k in ('cq_w', 'cq_b', 'ck_w', 'ck_b', 'cv_w', 'cv_b', 'co_w', 'co_b', 'co_g', 'co_be', 'sq_w', 'sq_b', 'sk_w', 'sk_b', 'sv_w', 'sv_b', 'so_w', 'so_b', 'so_g', 'so_be', 'fi_w', 'fi_b', 'fo_w', 'fo_b', 'fo_g', 'fo_be')}
    del _L1_xattn_all

    def _L1_attn_setup():
        import jax, jax.numpy as jnp
        import numpy as np
        EMBED = 256
        HEADS = 16
        key = jax.random.key(seed)
        ks = jax.random.split(key, 6)
        N, S = (1, 1024)
        half = EMBED // 2
        x = jax.random.normal(ks[0], (N, S, EMBED), dtype=jnp.float32)
        Wq = jax.random.normal(ks[1], (half, half), dtype=jnp.float32) * 0.02
        Wk = jax.random.normal(ks[2], (half, half), dtype=jnp.float32) * 0.02
        Wv = jax.random.normal(ks[3], (half, half), dtype=jnp.float32) * 0.02
        Wo = jax.random.normal(ks[4], (EMBED, half), dtype=jnp.float32) * 0.02
        bo = jnp.zeros((EMBED,), dtype=jnp.float32)
        return {'x': x, 'Wq': Wq, 'Wk': Wk, 'Wv': Wv, 'Wo': Wo, 'bo': bo}
    _L1_attn_all = _L1_attn_setup()
    _L1_attn_in = {k: v for k, v in _L1_attn_all.items() if k in ('Wq', 'Wk', 'Wv', 'Wo', 'bo')}
    del _L1_attn_all

    def _L1_ffn_setup():
        import jax, jax.numpy as jnp
        import numpy as np
        B, S, D = (4, 512, 256)
        E, F = (8, 1024)
        key = jax.random.key(seed)
        ks = jax.random.split(key, 5)
        x = jax.random.normal(ks[0], (B, S, D), dtype=jnp.float32)
        switch_w = jax.random.normal(ks[1], (D, E), dtype=jnp.float32) * D ** (-0.5)
        switch_b = jnp.zeros((E,), dtype=jnp.float32)
        w1 = jax.random.normal(ks[2], (E, D, F), dtype=jnp.float32) * D ** (-0.5)
        b1 = jnp.zeros((E, F), dtype=jnp.float32)
        w2 = jax.random.normal(ks[3], (E, F, D), dtype=jnp.float32) * F ** (-0.5)
        b2 = jnp.zeros((E, D), dtype=jnp.float32)
        return {'x': x, 'switch_w': switch_w, 'switch_b': switch_b, 'w1': w1, 'b1': b1, 'w2': w2, 'b2': b2}
    _L1_ffn_all = _L1_ffn_setup()
    _L1_ffn_in = {k: v for k, v in _L1_ffn_all.items() if k in ('switch_w', 'switch_b', 'w1', 'b1', 'w2', 'b2')}
    del _L1_ffn_all
    return {'x': x, 'ctx_1024': ctx_1024, 'fside_Bx16xSxS2_0': fside_Bx16xSxS2_0, 'mask_Bx16xSxS2_bk1': mask_Bx16xSxS2_bk1, 'mask_Bx1x1xS2_ff0': mask_Bx1x1xS2_ff0, 'L0_xattn_Wq': _L0_xattn_in['Wq'], 'L0_xattn_bq': _L0_xattn_in['bq'], 'L0_xattn_Wk': _L0_xattn_in['Wk'], 'L0_xattn_bk': _L0_xattn_in['bk'], 'L0_xattn_Wv': _L0_xattn_in['Wv'], 'L0_xattn_bv': _L0_xattn_in['bv'], 'L0_xattn_Wo': _L0_xattn_in['Wo'], 'L0_xattn_bo': _L0_xattn_in['bo'], 'L0_attn_w_kv_down': _L0_attn_in['w_kv_down'], 'L0_attn_w_kv_up': _L0_attn_in['w_kv_up'], 'L0_attn_w_q': _L0_attn_in['w_q'], 'L0_attn_w_out': _L0_attn_in['w_out'], 'L0_ffn_U1': _L0_ffn_in['U1'], 'L0_ffn_V1': _L0_ffn_in['V1'], 'L0_ffn_b1': _L0_ffn_in['b1'], 'L0_ffn_U2': _L0_ffn_in['U2'], 'L0_ffn_V2': _L0_ffn_in['V2'], 'L0_ffn_b2': _L0_ffn_in['b2'], 'L1_xattn_cq_w': _L1_xattn_in['cq_w'], 'L1_xattn_cq_b': _L1_xattn_in['cq_b'], 'L1_xattn_ck_w': _L1_xattn_in['ck_w'], 'L1_xattn_ck_b': _L1_xattn_in['ck_b'], 'L1_xattn_cv_w': _L1_xattn_in['cv_w'], 'L1_xattn_cv_b': _L1_xattn_in['cv_b'], 'L1_xattn_co_w': _L1_xattn_in['co_w'], 'L1_xattn_co_b': _L1_xattn_in['co_b'], 'L1_xattn_co_g': _L1_xattn_in['co_g'], 'L1_xattn_co_be': _L1_xattn_in['co_be'], 'L1_xattn_sq_w': _L1_xattn_in['sq_w'], 'L1_xattn_sq_b': _L1_xattn_in['sq_b'], 'L1_xattn_sk_w': _L1_xattn_in['sk_w'], 'L1_xattn_sk_b': _L1_xattn_in['sk_b'], 'L1_xattn_sv_w': _L1_xattn_in['sv_w'], 'L1_xattn_sv_b': _L1_xattn_in['sv_b'], 'L1_xattn_so_w': _L1_xattn_in['so_w'], 'L1_xattn_so_b': _L1_xattn_in['so_b'], 'L1_xattn_so_g': _L1_xattn_in['so_g'], 'L1_xattn_so_be': _L1_xattn_in['so_be'], 'L1_xattn_fi_w': _L1_xattn_in['fi_w'], 'L1_xattn_fi_b': _L1_xattn_in['fi_b'], 'L1_xattn_fo_w': _L1_xattn_in['fo_w'], 'L1_xattn_fo_b': _L1_xattn_in['fo_b'], 'L1_xattn_fo_g': _L1_xattn_in['fo_g'], 'L1_xattn_fo_be': _L1_xattn_in['fo_be'], 'L1_attn_Wq': _L1_attn_in['Wq'], 'L1_attn_Wk': _L1_attn_in['Wk'], 'L1_attn_Wv': _L1_attn_in['Wv'], 'L1_attn_Wo': _L1_attn_in['Wo'], 'L1_attn_bo': _L1_attn_in['bo'], 'L1_ffn_switch_w': _L1_ffn_in['switch_w'], 'L1_ffn_switch_b': _L1_ffn_in['switch_b'], 'L1_ffn_w1': _L1_ffn_in['w1'], 'L1_ffn_b1': _L1_ffn_in['b1'], 'L1_ffn_w2': _L1_ffn_in['w2'], 'L1_ffn_b2': _L1_ffn_in['b2']}

def reference(x, ctx_1024, fside_Bx16xSxS2_0, mask_Bx16xSxS2_bk1, mask_Bx1x1xS2_ff0, L0_xattn_Wq, L0_xattn_bq, L0_xattn_Wk, L0_xattn_bk, L0_xattn_Wv, L0_xattn_bv, L0_xattn_Wo, L0_xattn_bo, L0_attn_w_kv_down, L0_attn_w_kv_up, L0_attn_w_q, L0_attn_w_out, L0_ffn_U1, L0_ffn_V1, L0_ffn_b1, L0_ffn_U2, L0_ffn_V2, L0_ffn_b2, L1_xattn_cq_w, L1_xattn_cq_b, L1_xattn_ck_w, L1_xattn_ck_b, L1_xattn_cv_w, L1_xattn_cv_b, L1_xattn_co_w, L1_xattn_co_b, L1_xattn_co_g, L1_xattn_co_be, L1_xattn_sq_w, L1_xattn_sq_b, L1_xattn_sk_w, L1_xattn_sk_b, L1_xattn_sv_w, L1_xattn_sv_b, L1_xattn_so_w, L1_xattn_so_b, L1_xattn_so_g, L1_xattn_so_be, L1_xattn_fi_w, L1_xattn_fi_b, L1_xattn_fo_w, L1_xattn_fo_b, L1_xattn_fo_g, L1_xattn_fo_be, L1_attn_Wq, L1_attn_Wk, L1_attn_Wv, L1_attn_Wo, L1_attn_bo, L1_ffn_switch_w, L1_ffn_switch_b, L1_ffn_w1, L1_ffn_b1, L1_ffn_w2, L1_ffn_b2):
    import jax
    import jax.numpy as jnp

    def _L0_xattn_ref(queries, keys, values, mask, weights, Wq, bq, Wk, bk, Wv, bv, Wo, bo):
        import jax, jax.numpy as jnp
        import numpy as np
        BS, NQ, NK = (2, 512, 512)
        D_OUT, H, D_K, D_V = (256, 16, 64, 64)

        def _xavier(key, shape):
            fan_in, fan_out = (shape[1], shape[0])
            lim = float(np.sqrt(6.0 / (fan_in + fan_out)))
            return jax.random.uniform(key, shape, jnp.float32, -lim, lim)
        bs, nq, _ = queries.shape
        nk = keys.shape[1]
        q = (queries @ Wq.T + bq).reshape(bs, nq, H, D_K).transpose(0, 2, 1, 3)
        k = (keys @ Wk.T + bk).reshape(bs, nk, H, D_K).transpose(0, 2, 1, 3)
        v = (values @ Wv.T + bv).reshape(bs, nk, H, D_V).transpose(0, 2, 1, 3)
        att = jnp.einsum('bhqd,bhkd->bhqk', q, k) / jnp.sqrt(jnp.float32(D_K))
        att = att * weights
        att = jnp.where(mask, -jnp.inf, att)
        att = jax.nn.softmax(att, axis=-1)
        out = jnp.einsum('bhqk,bhkd->bhqd', att, v)
        out = out.transpose(0, 2, 1, 3).reshape(bs, nq, H * D_V)
        return out @ Wo.T + bo

    def _L0_attn_ref(x, w_kv_down, w_kv_up, w_q, w_out):
        import jax, jax.numpy as jnp
        import numpy as np
        B, T, C = (64, 64, 256)
        N_HEAD, HEAD_SIZE, KV_RANK = (16, 64, 128)
        BLOCK_SIZE = 64
        Bx, Tx, Cx = x.shape
        HD = N_HEAD * HEAD_SIZE
        latent_kv = x @ w_kv_down
        kv = latent_kv @ w_kv_up
        k, v = (kv[..., :HD], kv[..., HD:])
        k = k.reshape(Bx, Tx, N_HEAD, HEAD_SIZE)
        v = v.reshape(Bx, Tx, N_HEAD, HEAD_SIZE)
        q = (x @ w_q).reshape(Bx, Tx, N_HEAD, HEAD_SIZE)
        scale = HEAD_SIZE ** (-0.5)
        att = jnp.einsum('bqhd,bkhd->bhqk', q, k) * scale
        causal = jnp.tril(jnp.ones((Tx, Tx), dtype=bool))
        att = jnp.where(causal, att, -jnp.inf)
        att = jax.nn.softmax(att, axis=-1)
        y = jnp.einsum('bhqk,bkhd->bqhd', att, v)
        y = y.reshape(Bx, Tx, HD)
        return y @ w_out

    def _L0_ffn_ref(x, U1, V1, b1, U2, V2, b2):
        import jax, jax.numpy as jnp
        import numpy as np
        D_MODEL, D_FF, RANK = (256, 1024, 64)
        B, S = (4, 1024)
        P = jnp.einsum('bsd,dr->bsr', x, U1)
        H = jax.nn.gelu(jnp.einsum('bsr,rf->bsf', P, V1) + b1)
        Q = jnp.einsum('bsf,fr->bsr', H, U2)
        return jnp.einsum('bsr,rd->bsd', Q, V2) + b2

    def _L1_xattn_ref(input_tensor, ctx_tensor, ctx_attn_mask, cq_w, cq_b, ck_w, ck_b, cv_w, cv_b, co_w, co_b, co_g, co_be, sq_w, sq_b, sk_w, sk_b, sv_w, sv_b, so_w, so_b, so_g, so_be, fi_w, fi_b, fo_w, fo_b, fo_g, fo_be):
        import jax, jax.numpy as jnp
        import numpy as np
        H = 16
        D = 256
        F = 1024
        LN_EPS = 1e-05

        def _glorot(key, shape):
            fan_in, fan_out = (shape[0], shape[1])
            lim = np.sqrt(6.0 / (fan_in + fan_out))
            return jax.random.uniform(key, shape, jnp.float32, -lim, lim)

        def _split_heads(x):
            b, l, _ = x.shape
            return x.reshape(b, l, H, D // H)

        def _mha(x, ctx, mask, qw, qb, kw, kb, vw, vb):
            q = _split_heads(x @ qw + qb)
            k = _split_heads(ctx @ kw + kb)
            v = _split_heads(ctx @ vw + vb)
            scores = jnp.einsum('bqhd,bkhd->bhqk', q, k) / np.sqrt(D // H).astype(np.float32)
            if mask is not None:
                scores = scores + mask
            probs = jax.nn.softmax(scores, axis=-1)
            out = jnp.einsum('bhqk,bkhd->bqhd', probs, v)
            return out.reshape(x.shape[0], x.shape[1], D)

        def _self_output(h, residual, w, b, g, be):
            h = h @ w + b
            h = h + residual
            mu = jnp.mean(h, axis=-1, keepdims=True)
            var = jnp.mean(jnp.square(h - mu), axis=-1, keepdims=True)
            return (h - mu) * jax.lax.rsqrt(var + LN_EPS) * g + be
        ca = _mha(input_tensor, ctx_tensor, ctx_attn_mask, cq_w, cq_b, ck_w, ck_b, cv_w, cv_b)
        x = _self_output(ca, input_tensor, co_w, co_b, co_g, co_be)
        sa = _mha(x, x, None, sq_w, sq_b, sk_w, sk_b, sv_w, sv_b)
        x = _self_output(sa, x, so_w, so_b, so_g, so_be)
        inter = jax.nn.gelu(x @ fi_w + fi_b, approximate=False)
        x = _self_output(inter, x, fo_w, fo_b, fo_g, fo_be)
        return x

    def _L1_attn_ref(x, Wq, Wk, Wv, Wo, bo):
        import jax, jax.numpy as jnp
        import numpy as np
        EMBED = 256
        HEADS = 16
        N, S, E = x.shape
        H = HEADS
        Dh = E // 2 // H
        scale = float(E // H) ** 0.5
        left = x[..., :E // 2]
        q = (left @ Wq.T).reshape(N, S, H, Dh)
        k = (left @ Wk.T).reshape(N, S, H, Dh)
        v = (left @ Wv.T).reshape(N, S, H, Dh)
        energy = jnp.einsum('nqhd,nkhd->nqkh', q, k)
        att = jax.nn.softmax(energy / scale, axis=2)
        out = jnp.einsum('nqkh,nkhd->nqhd', att, v)
        out = out.reshape(N, S, E // 2)
        return out @ Wo.T + bo

    def _L1_ffn_ref(x, switch_w, switch_b, w1, b1, w2, b2):
        import jax, jax.numpy as jnp
        import numpy as np
        B, S, D = (4, 512, 256)
        E, F = (8, 1024)
        b, s, d = x.shape
        t = x.reshape(-1, d)
        logits = t @ switch_w + switch_b
        route_prob = jax.nn.softmax(logits, axis=-1)
        route_prob_max = jnp.max(route_prob, axis=-1)
        routes = jnp.argmax(route_prob, axis=-1)
        out = jnp.zeros_like(t)
        n_experts = w1.shape[0]
        for e in range(n_experts):
            h = jax.nn.gelu(t @ w1[e] + b1[e])
            y = h @ w2[e] + b2[e]
            mask = (routes == e)[:, None]
            out = jnp.where(mask, y, out)
        out = out * route_prob_max[:, None]
        return out.reshape(b, s, d)
    x = x + _L0_xattn_ref(_layernorm(x, axis=-1), ctx_1024, ctx_1024, mask_Bx16xSxS2_bk1, fside_Bx16xSxS2_0, L0_xattn_Wq, L0_xattn_bq, L0_xattn_Wk, L0_xattn_bk, L0_xattn_Wv, L0_xattn_bv, L0_xattn_Wo, L0_xattn_bo)
    x = x + _L0_attn_ref(_layernorm(x, axis=-1), L0_attn_w_kv_down, L0_attn_w_kv_up, L0_attn_w_q, L0_attn_w_out)
    x = x + _L0_ffn_ref(_layernorm(x, axis=-1), L0_ffn_U1, L0_ffn_V1, L0_ffn_b1, L0_ffn_U2, L0_ffn_V2, L0_ffn_b2)
    x = x + _L1_xattn_ref(_layernorm(x, axis=-1), ctx_1024, mask_Bx1x1xS2_ff0, L1_xattn_cq_w, L1_xattn_cq_b, L1_xattn_ck_w, L1_xattn_ck_b, L1_xattn_cv_w, L1_xattn_cv_b, L1_xattn_co_w, L1_xattn_co_b, L1_xattn_co_g, L1_xattn_co_be, L1_xattn_sq_w, L1_xattn_sq_b, L1_xattn_sk_w, L1_xattn_sk_b, L1_xattn_sv_w, L1_xattn_sv_b, L1_xattn_so_w, L1_xattn_so_b, L1_xattn_so_g, L1_xattn_so_be, L1_xattn_fi_w, L1_xattn_fi_b, L1_xattn_fo_w, L1_xattn_fo_b, L1_xattn_fo_g, L1_xattn_fo_be)
    x = x + _L1_attn_ref(_layernorm(x, axis=-1), L1_attn_Wq, L1_attn_Wk, L1_attn_Wv, L1_attn_Wo, L1_attn_bo)
    x = x + _L1_ffn_ref(_layernorm(x, axis=-1), L1_ffn_switch_w, L1_ffn_switch_b, L1_ffn_w1, L1_ffn_b1, L1_ffn_w2, L1_ffn_b2)
    return x

_drawn_inputs = setup_inputs


def setup_inputs(seed=0):
    import zlib

    import numpy as np

    out = dict(_drawn_inputs(seed))
    spreads = {'L0_xattn_bq': (0.0, 0.8),
     'L0_xattn_bk': (0.0, 0.8),
     'L0_xattn_bv': (0.0, 0.1),
     'L0_xattn_bo': (0.0, 0.1),
     'L0_ffn_b1': (0.0, 0.8),
     'L0_ffn_b2': (0.0, 0.8),
     'L1_xattn_cq_b': (0.0, 2.0),
     'L1_xattn_ck_b': (0.0, 2.0),
     'L1_xattn_cv_b': (0.0, 0.8),
     'L1_xattn_co_b': (0.0, 0.8),
     'L1_xattn_co_g': (1.0, 0.6),
     'L1_xattn_co_be': (0.0, 0.8),
     'L1_xattn_sq_b': (0.0, 2.0),
     'L1_xattn_sk_b': (0.0, 2.0),
     'L1_xattn_sv_b': (0.0, 0.8),
     'L1_xattn_so_b': (0.0, 0.8),
     'L1_xattn_so_g': (1.0, 0.6),
     'L1_xattn_so_be': (0.0, 0.8),
     'L1_xattn_fi_b': (0.0, 0.8),
     'L1_xattn_fo_b': (0.0, 0.8),
     'L1_xattn_fo_g': (1.0, 0.6),
     'L1_xattn_fo_be': (0.0, 0.8),
     'L1_attn_bo': (0.0, 0.8),
     'L1_ffn_switch_b': (0.0, 2.0),
     'L1_ffn_b1': (0.0, 2.0),
     'L1_ffn_b2': (0.0, 2.0)}
    factors = {'fside_Bx16xSxS2_0': 8.0,
     'L0_attn_w_q': 8.0,
     'L0_ffn_U1': 8.0,
     'L0_ffn_V1': 8.0,
     'L0_ffn_U2': 8.0,
     'L0_ffn_V2': 8.0,
     'L1_attn_Wq': 64.0,
     'L1_attn_Wk': 64.0,
     'L1_attn_Wv': 8.397,
     'L1_attn_Wo': 3.109,
     'L1_xattn_cq_w': 5.762,
     'L1_xattn_ck_w': 5.436,
     'L1_xattn_sq_w': 8.0,
     'L1_xattn_sk_w': 8.0,
     'L1_ffn_switch_w': 3.452,
     'L1_ffn_w1': 4.271,
     'L1_ffn_w2': 3.331}
    for name, (base, spread) in spreads.items():
        noise = np.random.default_rng([zlib.crc32(name.encode()), seed]).standard_normal(out[name].shape)
        drawn = base * np.exp(spread * noise) if base else spread * noise
        out[name] = jnp.asarray(drawn.astype(out[name].dtype))
    for name, factor in factors.items():
        out[name] = (out[name] * factor).astype(out[name].dtype)
    return out
```

```python
from contextlib import ExitStack

import numpy as np

import concourse.bass as bass
from concourse import mybir

F32 = mybir.dt.float32
U8 = mybir.dt.uint8
ALU = mybir.AluOpType
ACT = mybir.ActivationFunctionType
AX = mybir.AxisListType

P = 128
TOK = 256
QT = TOK // P
CH = 256
CT = CH // P
KEYS = 4096
HEADS = 16
FF = 1024
FT = FF // P
EXPERTS = 8
BANK = 512
CHUNKS = KEYS // BANK
KT = KEYS // P
PIECES = 4
PIECE = KEYS // PIECES
EPS = 1e-5

TINY = 2.0**-60
D0, D1, DL = 64, 16, 8

COLS = {}
for _name, _n in (("xq", 8), ("xk", 8), ("f1", FT), ("cq", 4), ("ck", 4), ("sq", 4), ("sk", 4),
                  ("sv", 4), ("fi", FT), ("m1", EXPERTS * FT)):
    COLS[_name] = sum(n for _, n in COLS.values()) if not COLS else max(o + n for o, n in COLS.values()), _n
NCOLS = max(o + n for o, n in COLS.values())
ROWS = {}
for _name, _n in (("xv", 1024), ("xo", CH), ("f2", CH), ("cv", CH), ("co_b", CH), ("co_g", CH),
                  ("co_be", CH), ("so_b", CH), ("so_g", CH), ("so_be", CH), ("switch", EXPERTS),
                  ("rank", EXPERTS)):
    ROWS[_name] = max([o + n for o, n in ROWS.values()], default=0), _n
NROWS = max(o + n for o, n in ROWS.values())
LATE = {"fo_b": 0, "fo_g": CH, "fo_be": 2 * CH, "lo": 3 * CH}


def fills_of(cross):
    v = KT // 2 if cross.values_in_loop else 0
    qk = 2 + CHUNKS
    tp = 2 * CHUNKS
    at, k = {"v": 0}, v
    at["t0"] = k
    k += tp
    if cross.tiles_per_turn == 2:
        at["qk"] = k
        k += qk
    at["t1"] = k
    at["t2"] = k + tp
    at["t3_last"] = k + 2 * tp
    at["next"] = k + 2 * tp
    at["t3"] = k + 2 * tp + qk
    return at, k + 3 * tp + qk, k + 3 * tp


class Cross:

    def __init__(self, name, first_fill, head_dim, weighted, tiles_per_turn, values_in_loop):
        self.name, self.d, self.weighted = name, head_dim, weighted
        self.tiles_per_turn, self.values_in_loop = tiles_per_turn, values_in_loop
        self.slot = 64 if head_dim == 64 else 32
        self.heads_per_tile = P // self.slot
        self.at, self.per_turn, last = fills_of(self)
        v_once = 0 if values_in_loop else KT // 2
        self.first_fill = first_fill
        self.f0 = first_fill + v_once + 2 + CHUNKS
        self.turns = 4
        self.end_fill = self.f0 + (self.turns - 1) * self.per_turn + last

    def fill(self, g, what, k=0):
        return g * self.per_turn + (self.f0 + self.at[what] + k)

    def probs_fill(self, g, u, last, t, j):
        return self.fill(g, f"t{u}" + ("_last" if last and u == 3 else ""), 2 * t + j)


class Small:

    def __init__(self, index, name, first_fill, slot, q_from, kv_from, causal, q_scale):
        self.index, self.name, self.slot = index, name, slot
        self.q_tiles, self.kv_tiles, self.causal, self.q_scale = q_from, kv_from, causal, q_scale
        self.per = P // slot
        self.groups = HEADS // self.per
        self.width = HEADS * slot
        self.f_q = first_fill
        self.f_k = self.f_q + self.groups
        self.f_v = self.f_k + self.groups
        self.f_t = self.f_v + QT * self.width // BANK
        self.end_fill = self.f_t + HEADS


def program(nc, a):
    ctx = ExitStack()
    with ctx:
        def sbuf(name, shape, dt=F32):
            return ctx.enter_context(nc.sbuf_tensor(name + "_sb", shape, dt))

        def sem(name):
            return ctx.enter_context(nc.semaphore(name))

        f_hT0 = 0
        X0 = Cross("x0", 1 + 1, D0, True, 2, True)
        f_oT0 = X0.end_fill
        f_hT1 = f_oT0 + 8
        f_lat = f_hT1 + 1
        A0 = Small(0, "a0", f_lat + 1, 64, CT, 1, True, D0**-0.5)
        f_hT2 = A0.end_fill
        f_p = f_hT2 + 1
        f_g0 = f_p + 1
        f_q = f_g0 + FT
        f_hT3 = f_q + 1
        f_pad = f_hT3 + 1
        X1 = Cross("x1", f_pad + f_pad % 2, D1, False, 1, False)
        f_oT1 = X1.end_fill
        f_xT4 = f_oT1 + 1
        A1 = Small(1, "a1", f_xT4 + 1, 32, CT, CT, False, D1**-0.5)
        f_xT5 = A1.end_fill
        f_g1 = f_xT5 + 1
        f_hT6 = f_g1 + FT
        A2 = Small(2, "a2", f_hT6 + 1, 32, 1, 1, False, 0.25)
        f_hT7 = A2.end_fill
        f_moe = f_hT7 + 1 + (f_hT7 + 1) % 2

        w_arena = sbuf("w_arena", [P, 4 * KEYS])
        ck_arena = sbuf("ck_arena", [P, 3 * KEYS])
        v_arena = sbuf("v_arena", [P, KT * 256])
        m_arena = sbuf("m_arena", [P, KEYS])
        o_arena = sbuf("o_arena", [P, 2048])
        p_arena = sbuf("p_arena", [P, 2048])
        rows = sbuf("rows", [P, NROWS])
        cols = sbuf("cols", [P, NCOLS])
        ident = sbuf("ident", [P, P])
        x = sbuf("x", [P, QT, CH])
        h = sbuf("h", [P, QT, CH])
        hT = sbuf("hT", [P, CT, TOK])
        qz_cross = sbuf("qz_cross", [P, 4, TOK])
        wq_stage = sbuf("wq_stage", [P, CT, P])
        wk_stage = sbuf("wk_stage", [P, CT, P])
        wv_stage = sbuf("wv_stage", [P, CT, 256])
        acc_sb = sbuf("acc_sb", [P, P])
        o_cross1 = sbuf("o_cross1", [P, QT, CH])
        row_max = sbuf("row_max", [P, QT, 2])
        chunk_max = sbuf("chunk_max", [P, QT, 2, CHUNKS])
        no_key = sbuf("no_key", [P, 3, 2])
        exp_bias = sbuf("exp_bias", [P, QT, 2])
        row_sum = sbuf("row_sum", [P, 4, 2])
        row_inv = sbuf("row_inv", [P, 4, 2])
        stats = sbuf("stats", [P, QT, 6])
        mean_var = sbuf("mean_var", [P, QT, 2])
        deviation = sbuf("deviation", [P, QT])
        q_bias = sbuf("q_bias", [P, 16])
        s_max = sbuf("s_max", [P, 4, QT])
        s_sum = sbuf("s_sum", [P, 4, QT])
        s_inv = sbuf("s_inv", [P, 4, QT])
        route = sbuf("route", [P, QT, 5, EXPERTS])
        coef = sbuf("coef", [P, QT, EXPERTS])

        def view(arena, at, *shape):
            n = int(np.prod(shape))
            ap = arena[:, at:at + n]
            if len(shape) == 1:
                return ap
            names = "abcd"[:len(shape)]
            return ap.rearrange(f"p ({' '.join(names)}) -> p {' '.join(names)}",
                                **{k: v for k, v in zip(names[1:], shape[1:])})

        side = view(w_arena, 0, QT, 2, KEYS)
        ctxT = view(ck_arena, 0, CT, KEYS)
        keysT = view(ck_arena, 2 * KEYS, KEYS)
        values = view(v_arena, 0, KT, 256)
        masks = m_arena[:, :].bitcast(U8).rearrange("p (q j k) -> p q j k", q=QT, j=2)
        key_mask = view(m_arena, 0, KEYS)
        o_cross0 = view(o_arena, 0, QT, 1024)
        values_turn = view(o_arena, 0, KT, 64)
        probsT = view(p_arena, 0, 2, 2, 4, P)
        xo_w = view(m_arena, 0, FT, CH)
        oT0 = view(w_arena, 0, FT, TOK)
        a0_q, a0_k, a0_v = view(v_arena, 0, CT, 1024), view(v_arena, 2048, 1, 1024), view(v_arena, 3072, 1, 1024)
        a0_o, a0_down = view(v_arena, 4096, 8, CH), view(v_arena, 6144, CT, P)
        f_U1, f_V1 = view(v_arena, 6400, CT, 64), view(v_arena, 6528, FF)
        f_U2, f_V2 = view(v_arena, 7552, FT, 64), view(m_arena, 2048, CH)
        causal = view(m_arena, 2304, QT, TOK)
        latT = view(m_arena, 2816, 1, TOK)
        lowT = view(m_arena, 3072, TOK)
        low2T = view(m_arena, 3328, TOK)
        gT0 = view(w_arena, 2048, FT, TOK)
        co_w = wv_stage[:, :, :]
        a1_q, a1_k, a1_v = (view(v_arena, 1024 * i, CT, 512) for i in range(3))
        a1_o, fi_w, fo_w = view(v_arena, 3072, 4, CH), view(v_arena, 4096, CT, FF), view(v_arena, 6144, FT, CH)
        a2_q, a2_k, a2_v = (view(m_arena, 512 * i, 1, 512) for i in range(3))
        a2_o, switch_w = view(m_arena, 1536, 4, CH), view(m_arena, 2560, CT, EXPERTS)
        gT1 = view(o_arena, 0, FT, TOK)
        b2_rows = view(p_arena, 0, EXPERTS, CH)
        w1 = [view(w_arena, 4096 * k, CT, FF) for k in range(2)]
        w2 = [view(w_arena, 4096 * k + 2048, FT, CH) for k in range(2)]
        moe_hT = [view(ck_arena, 2048 * k, FT, TOK) for k in range(2)]

        def small_views(arena, at, s):
            v = {}
            for name, shape in (("qz", (HEADS, TOK)), ("kT", (s.groups, TOK)), ("v", (QT, s.width)),
                                ("p", (4, QT, TOK)), ("oT", (s.groups, TOK)), ("pT", (2, QT, TOK)),
                                ("masked", (2, QT, TOK) if s.causal else (1, 1))):
                v[name] = view(arena, at, *shape)
                at += int(np.prod(shape))
            return v

        B0 = small_views(w_arena, 0, A0)
        B1 = small_views(ck_arena, 0, A1)
        B2 = small_views(ck_arena, 0, A2)
        SMALL_OPS = {0: (A0, B0, a0_q, a0_k, a0_v, a0_o), 1: (A1, B1, a1_q, a1_k, a1_v, a1_o),
                     2: (A2, B2, a2_q, a2_k, a2_v, a2_o)}

        def row(name):
            at, n = ROWS[name]
            return rows[:, at:at + n]

        def late_row(name):
            return rows[:, LATE[name]:LATE[name] + CH]

        def col(name, i=0):
            return cols[:, bass.ds(COLS[name][0] + i, 1)]

        psum = ctx.enter_context(nc.psum_tensor("psum", [P, 8, BANK], F32))
        ACC, BACK = 6, 7

        def ring(f):
            return psum[:, 4 + f % 2, :]

        x_loaded, cols_loaded, ident_loaded, rows_loaded = map(sem, ("x_loaded", "cols_loaded", "ident_loaded", "rows_loaded"))
        ctx_loaded = [sem(f"ctx_loaded{i}") for i in range(PIECES)]
        side_loaded = [[sem(f"side_loaded{q}_{i}") for i in range(PIECES)] for q in range(QT)]
        mask_loaded = [sem(f"mask_loaded{q}") for q in range(QT)]
        wqk_loaded, wv_loaded = sem("wqk_loaded"), sem("wv_loaded")
        w_block0, w_block0_o, w_co, w_block1, w_attn2, late_loaded, b2_loaded = map(
            sem, ("w_block0", "w_block0_o", "w_co", "w_block1", "w_attn2", "late_loaded", "b2_loaded"))
        key_mask_loaded = sem("key_mask_loaded")
        expert_loaded = [sem(f"expert_loaded{k}") for k in range(2)]
        filled, drained = sem("filled"), sem("drained")
        scores_ready, scores_used = sem("scores_ready"), sem("scores_used")
        masked, bias_ready, exp_done = sem("masked"), sem("bias_ready"), sem("exp_done")
        pv_done, acc_copied, acc_back, normed = sem("pv_done"), sem("acc_copied"), sem("acc_back"), sem("normed")
        cross_link, norm_link, moe_link, link_sem = sem("cross_link"), sem("norm_link"), sem("moe_link"), sem("vector_link")
        values_copied = sem("values_copied")
        ln_var, ln_dev, ln_done = sem("ln_var"), sem("ln_dev"), sem("ln_done")
        q_zeroed = sem("q_zeroed")
        q_bias_ready = sem("q_bias_ready")
        proj_done, x_updated = sem("proj_done"), sem("x_updated")
        sm_scores, sm_masked, sm_max, sm_exp, sm_norm, sm_pv, sm_out = map(
            sem, ("sm_scores", "sm_masked", "sm_max", "sm_exp", "sm_norm", "sm_pv", "sm_out"))
        route_exp, moe_y, moe_added = sem("route_exp"), sem("moe_y"), sem("moe_added")
        out_stored = sem("out_stored")
        sp_passed, act_passed, dve_passed = sem("sp_passed"), sem("act_passed"), sem("dve_passed")

        (PROJ_X0, PROJ_A0, PROJ_F0, PROJ_C, PROJ_A1, PROJ_FI, PROJ_A2, PROJ_ROUTE) = range(8)
        PROJ_BANK = [ACC, BACK, BACK, ACC, BACK, ACC, BACK, ACC]
        LN_X0, LN_A0, LN_F0, LN_X1, LN_CO, LN_SO, LN_FO, LN_A2, LN_MOE = range(9)
        UP_X0, UP_A0, UP_F0, UP_CO, UP_SO, UP_FO, UP_A2 = range(7)

        block = ctx.enter_context(nc.Block())

        @block.sync
        def _(sp):
            def wait_then(sem_, value):
                sp.wait_ge(sem_, value)
                sp.sem_inc(sp_passed)

            def load_side(q, i, pair):
                sp.dma_start(side[:, q, :, i * PIECE:(i + 1) * PIECE],
                             a["side"][bass.ds(pair * 2, 2), q * P:(q + 1) * P, i * PIECE:(i + 1) * PIECE]
                             .rearrange("h p k -> p h k")).then_inc(side_loaded[q][i], 16)

            def load_mask(q, pair):
                sp.dma_start(masks[:, q, :, :], a["mask"][bass.ds(pair * 2, 2), q * P:(q + 1) * P, :]
                             .rearrange("h p k -> p h k")).then_inc(mask_loaded[q], 16)

            def load_qk(wq, wk, m):
                for stage, w in ((wq_stage, wq), (wk_stage, wk)):
                    sp.dma_start(stage[:, :, :], w.rearrange("(c p) n -> p c n", p=P)[:, :, bass.ds(m * P, P)]
                                 ).then_inc(wqk_loaded, 16)

            def load_wv(g):
                sp.dma_start(wv_stage[:, :, :], a["x_wv"].rearrange("(c p) n -> p c n", p=P)[:, :, bass.ds(g * 256, 256)]
                             ).then_inc(wv_loaded, 16)

            def load(dst, src, done):
                sp.dma_start(dst, src).then_inc(done, 16)

            def tiled(name):
                return a[name].rearrange("(c p) n -> p c n", p=P)

            load(x[:, :, :], a["x"].rearrange("(t p) c -> p t c", p=P), x_loaded)
            load(ident[:, :], a["ident"], ident_loaded)
            load(cols[:, :], a["cols"], cols_loaded)
            load_qk(a["x_wq"], a["x_wk"], 0)
            for i in range(PIECES):
                load(ctxT[:, :, i * PIECE:(i + 1) * PIECE], tiled("ctxT")[:, :, i * PIECE:(i + 1) * PIECE], ctx_loaded[i])
                load_side(0, i, 0)
            load_wv(0)
            load_mask(0, 0)
            load(rows[:, :], a["rows"].to_broadcast([P, NROWS]), rows_loaded)
            load_mask(1, 0)
            for i in range(PIECES):
                load_side(1, i, 0)

            def next_unit(g, u, last):
                pair = g * 2 + (u + 2) // 2
                wait_then(masked, g * 4 + (u + 1))
                load_mask(u % 2, pair)
                for i in range(PIECES):
                    wait_then(filled, X0.probs_fill(g, u, last, 2 * i + 1, 1) + 1)
                    load_side(u % 2, i, pair)

            def turn(g, last):
                if not last:
                    wait_then(filled, X0.fill(g, "t0"))
                    load_wv(g + 1)
                next_unit(g, 0, last)
                if not last:
                    wait_then(filled, X0.fill(g, "qk", 2 + CHUNKS))
                    load_qk(a["x_wq"], a["x_wk"], g * 2 + 2)
                next_unit(g, 1, last)
                if not last:
                    next_unit(g, 2, last)
                    wait_then(filled, X0.fill(g, "next", 2 + CHUNKS))
                    load_qk(a["x_wq"], a["x_wk"], g * 2 + 3)
                    next_unit(g, 3, last)

            wait_then(filled, X0.f0)
            load_qk(a["x_wq"], a["x_wk"], 1)
            with sp.Fori(0, X0.turns - 1) as g:
                turn(g, False)
            turn(X0.turns - 1, True)

            wait_then(masked, 16)
            load(xo_w, tiled("x_wo"), w_block0_o)
            load(f_V2[0:64, :], a["f_V2"], w_block0_o)
            load(causal, a["causal"].rearrange("(t p) k -> p t k", p=P), w_block0_o)
            wait_then(pv_done, 16)
            for dst, name in ((a0_down, "a_down"), (a0_q, "a_q"), (a0_k, "a_kup"), (a0_v, "a_vup"),
                              (a0_o, "a_out"), (f_U1, "f_U1"), (f_U2, "f_U2")):
                load(dst, tiled(name), w_block0)
            load(f_V1[0:64, :], a["f_V1"], w_block0)
            load_qk(a["c_wq"], a["c_wk"], 0)
            load(wv_stage[:, :, :], tiled("c_wv"), wv_loaded)
            wait_then(normed, 16)
            load(rows[:, 0:1024], a["late"].to_broadcast([P, 1024]), late_loaded)
            wait_then(x_updated, UP_F0 + 1)
            load(key_mask, a["key_mask"].to_broadcast([P, KEYS]), key_mask_loaded)

            wait_then(filled, X1.first_fill + KT // 2)
            load(co_w, tiled("c_wo"), w_co)
            wait_then(filled, X1.f0)
            load_qk(a["c_wq"], a["c_wk"], 1)
            with sp.Fori(0, X1.turns - 2) as g:
                wait_then(filled, X1.fill(g, "next", 2 + CHUNKS))
                load_qk(a["c_wq"], a["c_wk"], g + 2)
            wait_then(normed, 32)
            for dst, name in ((a1_q, "s_wq"), (a1_k, "s_wk"), (a1_v, "s_wv"), (a1_o, "s_wo"),
                              (fi_w, "fi_w"), (fo_w, "fo_w")):
                load(dst, tiled(name), w_block1)
            for dst, name in ((a2_q, "l_wq"), (a2_k, "l_wk"), (a2_v, "l_wv"), (a2_o, "l_wo"),
                              (switch_w, "switch_w")):
                load(dst, tiled(name), w_attn2)
            load(b2_rows.rearrange("p e c -> p (e c)"), a["b2"].to_broadcast([P, EXPERTS * CH]), b2_loaded)

            def load_expert(k, e):
                sp.dma_start(w1[k], a["w1"][bass.ds(e, 1), :, :].rearrange("o (c p) f -> p (o c) f", p=P)
                             ).then_inc(expert_loaded[k], 16)
                sp.dma_start(w2[k], a["w2"][bass.ds(e, 1), :, :].rearrange("o (f p) c -> p (o f) c", p=P)
                             ).then_inc(expert_loaded[k], 16)

            load_expert(0, 0)
            load_expert(1, 1)
            with sp.Fori(0, EXPERTS // 2 - 1) as i:
                wait_then(moe_y, i * 2 + 1)
                load_expert(0, i * 2 + 2)
                wait_then(moe_y, i * 2 + 2)
                load_expert(1, i * 2 + 3)
            wait_then(moe_added, EXPERTS + 2)
            sp.dma_start(a["out"].rearrange("(t p) c -> p t c", p=P), x[:, :, :]).then_inc(out_stored, 16)
            sp.wait_ge(out_stored, 16)

        @block.gpsimd
        def _(pool):
            nc.gpsimd.memset(qz_cross[:, :, :], 0.0).then_inc(q_zeroed, 1)
            pool.wait_ge(scores_used, 16 * CHUNKS)
            nc.gpsimd.memset(qz_cross[:, :, :], 0.0).then_inc(q_zeroed, 1)
            pool.wait_ge(proj_done, PROJ_X0 + 1)
            nc.gpsimd.memset(B0["qz"], 0.0).then_inc(q_zeroed, 1)
            pool.wait_ge(drained, X1.first_fill + KT // 2)
            nc.gpsimd.tensor_copy(values_turn, values[:, :, 0:64]).then_inc(values_copied, 1)
            with pool.Fori(1, X1.turns) as g:
                pool.wait_ge(pv_done, g * 4 + 16)
                nc.gpsimd.tensor_copy(values_turn, values[:, :, bass.ds(g * 64, 64)]).then_inc(values_copied, 1)
            pool.wait_ge(normed, 32)
            nc.gpsimd.memset(B1["qz"], 0.0).then_inc(q_zeroed, 1)

        @block.scalar
        def _(act):
            def drain(f, dst, src=None, func=ACT.Copy, **kw):
                act.wait_ge(filled, f + 1)
                nc.scalar.activation(dst, src, func, **kw).then_inc(drained, 1)

            def drain_hT(f):
                drain(f, hT[:, :, :], ring(f).rearrange("p (c t) -> p c t", c=CT))

            def deviations(ln):
                act.wait_ge(ln_var, ln + 1)
                nc.scalar.activation(deviation[:, :], mean_var[:, :, 1], ACT.Sqrt).then_inc(ln_dev, 1)

            def q_k(X, f, par, m, qcol, kcol, scale):
                for q in range(QT):
                    act.wait_ge(filled, f + q + 1)
                    act.sem_inc(act_passed)
                    b = psum[:, 4 + (par + q) % 2, :]
                    for j in range(X.heads_per_tile):
                        s = slice(j * X.slot, (j + 1) * X.slot)
                        last = nc.scalar.activation(qz_cross[s, j, q * P:(q + 1) * P], b[s, 0:P], ACT.Identity,
                                                    bias=q_bias[s, bass.ds(qcol + m, 1)], scale=scale)
                    last.then_inc(drained, 1)
                for c in range(CHUNKS):
                    act.wait_ge(filled, f + 2 + c + 1)
                    act.sem_inc(act_passed)
                    nc.scalar.activation(keysT[:, c * BANK:(c + 1) * BANK], psum[:, 4 + (par + c) % 2, :],
                                         ACT.Identity, bias=col(kcol, m)).then_inc(drained, 1)

            def exps(X, n0, g, u):
                act.wait_ge(bias_ready, g * 4 + (n0 + u + 1))
                for j in range(2):
                    nc.scalar.activation(side[:, u % 2, j, :], side[:, u % 2, j, :], ACT.Exp,
                                         bias=exp_bias[:, u % 2, j:j + 1], scale=1.0 / TINY if X.weighted else 1.0,
                                         accum_out=row_sum[:, u, j:j + 1]).then_inc(exp_done, 1)

            def probs(X, n0, g, u, last):
                for t in range(CHUNKS):
                    for j in range(2):
                        f = X.probs_fill(g, u, last, t, j)
                        act.wait_ge(filled, f + 1)
                        nc.scalar.activation(probsT[:, t % 2, j, :, :],
                                             psum[:, 4 + j, :].rearrange("p (i q) -> p i q", i=4),
                                             ACT.Copy).then_inc(drained, 1)
                act.wait_ge(pv_done, g * 4 + (n0 + u + 1))
                if X.d == 64:
                    nc.scalar.activation(acc_sb[:, :], psum[:, ACC, 0:P], ACT.Copy).then_inc(acc_copied, 1)
                else:
                    nc.scalar.activation(acc_sb[0:X.d, :], psum[0:X.d, ACC, 0:P], ACT.Copy)
                    nc.scalar.activation(acc_sb[64:64 + X.d, :], psum[64:64 + X.d, ACC, 0:P], ACT.Copy
                                         ).then_inc(acc_copied, 1)

            def cross(X, n0, qcol, kcol, scale):
                def turn(g, last):
                    if X.values_in_loop:
                        for k in range(KT // 2):
                            act.wait_ge(filled, X.fill(g, "v", k) + 1)
                            nc.scalar.activation(values[:, 2 * k:2 * k + 2, :], psum[:, 4 + k % 2, :]
                                                 .rearrange("p (k n) -> p k n", k=2), ACT.Copy).then_inc(drained, 1)
                    exps(X, n0, g, 0)
                    probs(X, n0, g, 0, last)
                    if X.tiles_per_turn == 2:
                        q_k(X, X.fill(g, "qk"), 0, g * 2 + 1, qcol, kcol, scale)
                    exps(X, n0, g, 1)
                    probs(X, n0, g, 1, last)
                    exps(X, n0, g, 2)
                    probs(X, n0, g, 2, last)
                    if not last:
                        q_k(X, X.fill(g, "next"), 0, g * X.tiles_per_turn + X.tiles_per_turn, qcol, kcol, scale)
                    exps(X, n0, g, 3)
                    probs(X, n0, g, 3, last)

                q_k(X, X.f0 - 2 - CHUNKS, 0, 0, qcol, kcol, scale)
                with act.Fori(0, X.turns - 1) as g:
                    turn(g, False)
                turn(X.turns - 1, True)

            def small(s):
                s, B = SMALL_OPS[s.index][:2]
                act.wait_ge(q_zeroed, 3 if s.index == 0 else 4)
                for g in range(s.groups):
                    f = s.f_q + g
                    act.wait_ge(filled, f + 1)
                    for j in range(s.per):
                        sl = slice(j * s.slot, (j + 1) * s.slot)
                        bias = dict(bias=q_bias[sl, 12 + g:13 + g]) if s.index == 1 else {}
                        last = nc.scalar.activation(B["qz"][sl, g * s.per + j, :], ring(f)[sl, 0:TOK],
                                                    ACT.Identity if bias else ACT.Copy, scale=s.q_scale, **bias)
                    last.then_inc(drained, 1)
                for g in range(s.groups):
                    f = s.f_k + g
                    if s.index == 1:
                        drain(f, B["kT"][:, g, :], ring(f)[:, 0:TOK], ACT.Identity, bias=col("sk", g))
                    else:
                        drain(f, B["kT"][:, g, :], ring(f)[:, 0:TOK])
                for k in range(QT * s.width // BANK):
                    t, c = divmod(k, s.width // BANK)
                    drain(s.f_v + k, B["v"][:, t, c * BANK:(c + 1) * BANK], ring(s.f_v + k))
                for i in range(HEADS + 3):
                    if i < HEADS:
                        act.wait_ge(sm_max, HEADS * s.index + i + 1)
                        for q in range(QT):
                            src = B["masked"][:, i % 2, q, :] if s.causal else psum[:, i % 4, q * TOK:(q + 1) * TOK]
                            nc.scalar.activation(B["p"][:, i % 4, q, :], src, ACT.Exp,
                                                 bias=s_max[:, i % 4, q:q + 1],
                                                 accum_out=s_sum[:, i % 4, q:q + 1]).then_inc(sm_exp, 1)
                    if i >= 3:
                        hd = i - 3
                        drain(s.f_t + hd, B["pT"][:, hd % 2, :, :],
                              ring(s.f_t + hd).rearrange("p (k q) -> p k q", k=QT))

            deviations(LN_X0)
            drain_hT(f_hT0)
            act.wait_ge(filled, 2)
            nc.scalar.activation(deviation[:, :], deviation[:, :], ACT.Copy).then_inc(drained, 1)
            act.wait_ge(q_zeroed, 1)
            act.wait_ge(q_bias_ready, 1)
            act.wait_ge(cols_loaded, 16)
            cross(X0, 0, 0, "xk", TINY * D0**-0.5)
            for k in range(8):
                drain(f_oT0 + k, oT0[:, k, :], ring(f_oT0 + k)[:, 0:TOK])
            deviations(LN_A0)
            drain_hT(f_hT1)
            drain(f_lat, latT[:, 0, :], ring(f_lat)[:, 0:TOK])
            small(A0)
            deviations(LN_F0)
            drain_hT(f_hT2)
            drain(f_p, lowT[0:64, :], ring(f_p)[0:64, 0:TOK])
            for k in range(FT):
                drain(f_g0 + k, gT0[:, k, :], ring(f_g0 + k)[:, 0:TOK], ACT.Gelu_apprx_tanh, bias=col("f1", k))
            drain(f_q, low2T[0:64, :], ring(f_q)[0:64, 0:TOK])
            deviations(LN_X1)
            drain_hT(f_hT3)
            for f in range(f_hT3 + 1, X1.first_fill):
                act.wait_ge(filled, f + 1)
                nc.scalar.activation(deviation[:, :], deviation[:, :], ACT.Copy).then_inc(drained, 1)
            act.wait_ge(q_zeroed, 3)
            for k in range(KT // 2):
                drain(X1.first_fill + k, values[:, 2 * k:2 * k + 2, :],
                      ring(X1.first_fill + k).rearrange("p (k n) -> p k n", k=2))
            cross(X1, 16, 8, "ck", D1**-0.5)
            drain(f_oT1, hT[:, :, :], ring(f_oT1).rearrange("p (c t) -> p c t", c=CT))
            deviations(LN_CO)
            drain_hT(f_xT4)
            small(A1)
            deviations(LN_SO)
            drain_hT(f_xT5)
            for k in range(FT):
                drain(f_g1 + k, gT1[:, k, :], ring(f_g1 + k)[:, 0:TOK], ACT.Gelu, bias=col("fi", k))
            deviations(LN_FO)
            deviations(LN_A2)
            drain_hT(f_hT6)
            small(A2)
            deviations(LN_MOE)
            drain_hT(f_hT7)
            for f in range(f_hT7 + 1, f_moe):
                act.wait_ge(filled, f + 1)
                nc.scalar.activation(deviation[:, :], deviation[:, :], ACT.Copy).then_inc(drained, 1)
            act.wait_ge(sm_max, HEADS * 3 + 1)
            for q in range(QT):
                nc.scalar.activation(route[:, q, 1, :], route[:, q, 0, :], ACT.Exp, bias=s_max[:, 0, q:q + 1],
                                     accum_out=s_sum[:, 0, q:q + 1]).then_inc(route_exp, 1)

            def hidden(k, f, e):
                for t in range(FT):
                    act.wait_ge(filled, f + t + 1)
                    act.sem_inc(act_passed)
                    nc.scalar.activation(moe_hT[k][:, t, :], psum[:, 4 + t % 2, 0:TOK], ACT.Gelu_apprx_tanh,
                                         bias=col("m1", e * FT + t)).then_inc(drained, 1)

            hidden(0, f_moe, 0)
            with act.Fori(0, EXPERTS // 2 - 1) as i:
                hidden(1, i * (2 * FT) + (f_moe + FT), i * 2 + 1)
                hidden(0, i * (2 * FT) + (f_moe + 2 * FT), i * 2 + 2)
            hidden(1, f_moe + (EXPERTS - 1) * FT, EXPERTS - 1)

        @block.tensor
        def _(pe):
            mm, tr = nc.tensor.matmul, nc.tensor.transpose

            def fill(f):
                if not isinstance(f, int) or f >= 2:
                    pe.wait_ge(drained, f - 1)

            def transpose_tokens(f, src):
                fill(f)
                for c in range(CT):
                    for t in range(QT):
                        last = tr(ring(f)[:, c * TOK + t * P:c * TOK + (t + 1) * P], src[:, t, c * P:(c + 1) * P],
                                  ident[:, :])
                last.then_inc(filled, 1)

            def empty_fill(f):
                fill(f)
                tr(ring(f)[:, 0:P], ident[:, :], ident[:, :]).then_inc(filled, 1)

            def q_k(X, f, m, loads_before, first):
                pe.wait_ge(wqk_loaded, m * 32 + (loads_before + 1) * 32)
                for q in range(QT):
                    fill(f + q)
                    for c in range(CT):
                        last = mm(psum[:, 4 + q % 2, 0:P], wq_stage[:, c, :], hT[:, c, q * P:(q + 1) * P],
                                  start=c == 0, stop=c == CT - 1)
                    last.then_inc(filled, 1)
                for ch in range(CHUNKS):
                    fill(f + 2 + ch)
                    if first and ch % 2 == 0:
                        pe.wait_ge(ctx_loaded[ch // 2], 16)
                    for c in range(CT):
                        last = mm(psum[:, 4 + ch % 2, :], wk_stage[:, c, :], ctxT[:, c, ch * BANK:(ch + 1) * BANK],
                                  start=c == 0, stop=c == CT - 1)
                    last.then_inc(filled, 1)

            def value_fills(f, par=0):
                for k in range(KT // 2):
                    fill(f + k)
                    for i in range(2):
                        kt = 2 * k + i
                        for c in range(CT):
                            last = mm(psum[:, 4 + (par + k) % 2, i * 256:(i + 1) * 256], ctxT[:, c, kt * P:(kt + 1) * P],
                                      wv_stage[:, c, :], start=c == 0, stop=c == CT - 1)
                    last.then_inc(filled, 1)

            def scores(X, n0, g, u, new_keys=None):
                for c in range(CHUNKS):
                    if new_keys is not None:
                        pe.wait_ge(drained, new_keys + 2 + c + 1)
                    s = g * (4 * CHUNKS) + ((n0 + u) * CHUNKS + c)
                    if not isinstance(s, int) or s >= 2:
                        pe.wait_ge(scores_used, s - 1)
                    for j in range(2):
                        head = j if X.tiles_per_turn == 2 else 2 * (u // 2 % 2) + j
                        last = mm(psum[:, 2 * (c % 2) + j, :], qz_cross[:, head, (u % 2) * P:(u % 2 + 1) * P],
                                  keysT[:, c * BANK:(c + 1) * BANK], start=True, stop=True)
                    last.then_inc(scores_ready, 1)

            def back(n0, g, u):
                n = g * 4 + (n0 + u)
                pe.wait_ge(acc_copied, n + 1)
                if not isinstance(n, int) or n >= 1:
                    pe.wait_ge(normed, n)
                tr(psum[:, BACK, 0:P], acc_sb[:, :], ident[:, :]).then_inc(acc_back, 1)

            def weigh_values(X, n0, g, u, last):
                vals = values if X.tiles_per_turn == 2 else values_turn

                def transposes(t):
                    for j in range(2):
                        f = X.probs_fill(g, u, last, t, j)
                        fill(f)
                        if t == 0:
                            pe.wait_ge(exp_done, g * 8 + (2 * (n0 + u) + j + 1))
                        for i in range(4):
                            ins = tr(psum[:, 4 + j, i * P:(i + 1) * P],
                                     side[:, u % 2, j, (4 * t + i) * P:(4 * t + i + 1) * P], ident[:, :])
                        ins.then_inc(filled, 1)

                def products(t):
                    pe.wait_ge(drained, X.probs_fill(g, u, last, t, 1) + 1)
                    for i in range(4):
                        for j in range(2):
                            v = (2 * (u // 2) + j) * X.d
                            kt = 4 * t + i
                            ins = mm(psum[64 * j:64 * j + X.d, ACC, 0:P], vals[:, kt, v:v + X.d],
                                     probsT[:, t % 2, j, i, :], start=kt == 0, stop=kt == KT - 1)
                    if t == CHUNKS - 1:
                        ins.then_inc(pv_done, 1)

                transposes(0)
                if not isinstance(g, int) or g * 4 + n0 + u >= 1:
                    pe.wait_ge(acc_copied, g * 4 + (n0 + u))
                for t in range(CHUNKS):
                    if t + 1 < CHUNKS:
                        transposes(t + 1)
                    products(t)

            def cross(X, n0, loads_before):
                first_tile = X.f0 - 2 - CHUNKS

                def turn(g, last):
                    if X.values_in_loop:
                        pe.wait_ge(wv_loaded, g * 16 + 16)
                        value_fills(X.fill(g, "v"))
                    else:
                        pe.wait_ge(values_copied, g + 1)
                    scores(X, n0, g, 1)
                    weigh_values(X, n0, g, 0, last)
                    if X.tiles_per_turn == 2:
                        q_k(X, X.fill(g, "qk"), g * 2 + 1, loads_before, False)
                        scores(X, n0, g, 2, X.fill(g, "qk"))
                    else:
                        scores(X, n0, g, 2)
                    back(n0, g, 0)
                    weigh_values(X, n0, g, 1, last)
                    scores(X, n0, g, 3)
                    back(n0, g, 1)
                    weigh_values(X, n0, g, 2, last)
                    if not last:
                        q_k(X, X.fill(g, "next"), g * X.tiles_per_turn + X.tiles_per_turn, loads_before, False)
                        scores(X, n0, g, 4, X.fill(g, "next"))
                    back(n0, g, 2)
                    weigh_values(X, n0, g, 3, last)
                    back(n0, g, 3)

                q_k(X, first_tile, 0, loads_before, X.weighted)
                scores(X, n0, 0, 0, first_tile)
                with pe.Fori(0, X.turns - 1) as g:
                    turn(g, False)
                turn(X.turns - 1, True)

            def small(s, kvT):
                s, B, wq, wk, wv, wo = SMALL_OPS[s.index]
                for g in range(s.groups):
                    f = s.f_q + g
                    fill(f)
                    for c in range(s.q_tiles):
                        last = mm(ring(f)[:, 0:TOK], wq[:, c, g * P:(g + 1) * P], hT[:, c, :],
                                  start=c == 0, stop=c == s.q_tiles - 1)
                    last.then_inc(filled, 1)
                for g in range(s.groups):
                    f = s.f_k + g
                    fill(f)
                    for c in range(s.kv_tiles):
                        last = mm(ring(f)[:, 0:TOK], wk[:, c, g * P:(g + 1) * P], kvT[:, c, :],
                                  start=c == 0, stop=c == s.kv_tiles - 1)
                    last.then_inc(filled, 1)
                for k in range(QT * s.width // BANK):
                    t, n = divmod(k, s.width // BANK)
                    fill(s.f_v + k)
                    for c in range(s.kv_tiles):
                        last = mm(ring(s.f_v + k), kvT[:, c, t * P:(t + 1) * P], wv[:, c, n * BANK:(n + 1) * BANK],
                                  start=c == 0, stop=c == s.kv_tiles - 1)
                    last.then_inc(filled, 1)
                pe.wait_ge(drained, s.f_v)
                base = HEADS * s.index
                for i in range(HEADS + 4):
                    if i < HEADS:
                        if i >= 4:
                            if s.causal:
                                pe.wait_ge(sm_masked, i - 3)
                            else:
                                pe.wait_ge(sm_exp, 2 * (base + i - 3))
                        for q in range(QT):
                            last = mm(psum[:, i % 4, q * TOK:(q + 1) * TOK], B["qz"][:, i, q * P:(q + 1) * P],
                                      B["kT"][:, i // s.per, :], start=True, stop=True)
                        last.then_inc(sm_scores, 1)
                    if 3 <= i < HEADS + 3:
                        hd = i - 3
                        f = s.f_t + hd
                        fill(f)
                        pe.wait_ge(sm_norm, base + hd + 1)
                        for k in range(QT):
                            for q in range(QT):
                                last = tr(ring(f)[:, k * TOK + q * P:k * TOK + (q + 1) * P],
                                          B["p"][:, hd % 4, q, k * P:(k + 1) * P], ident[:, :])
                        last.then_inc(filled, 1)
                    if i >= 4:
                        hd = i - 4
                        g, j = divmod(hd, s.per)
                        pe.wait_ge(drained, s.f_t + hd + 1)
                        if j == 0 and g >= 2:
                            pe.wait_ge(sm_out, sum(SMALL_OPS[k][0].groups for k in range(s.index)) + g - 1)
                        for k in range(QT):
                            last = mm(psum[j * s.slot:(j + 1) * s.slot, ACC + g % 2, 0:TOK],
                                      B["v"][:, k, hd * s.slot:(hd + 1) * s.slot], B["pT"][:, hd % 2, k, :],
                                      start=k == 0, stop=k == QT - 1)
                        if j == s.per - 1:
                            last.then_inc(sm_pv, 1)
                pe.wait_ge(sm_out, sum(SMALL_OPS[k][0].groups for k in range(s.index + 1)))
                project([B["oT"][:, g, :] for g in range(s.groups)], [wo[:, g, :] for g in range(s.groups)],
                        {0: PROJ_A0, 1: PROJ_A1, 2: PROJ_A2}[s.index])

            def project(lhs, rhs, which):
                n = rhs[0].shape[-1]
                for q in range(QT):
                    for k in range(len(lhs)):
                        last = mm(psum[:, PROJ_BANK[which], q * n:(q + 1) * n], lhs[k][:, q * P:(q + 1) * P], rhs[k],
                                  start=k == 0, stop=k == len(lhs) - 1)
                last.then_inc(proj_done, 1)

            def gelu_fills(f0, w, rhs, n):
                for t in range(FT):
                    f = f0 + t
                    fill(f)
                    for c in range(n):
                        last = mm(ring(f)[:, 0:TOK], w(c, t), rhs(c), start=c == 0, stop=c == n - 1)
                    last.then_inc(filled, 1)

            pe.wait_ge(ident_loaded, 16)
            pe.wait_ge(ln_done, LN_X0 + 1)
            transpose_tokens(f_hT0, h)
            empty_fill(1)
            pe.wait_ge(drained, f_hT0 + 1)
            cross(X0, 0, 0)
            pe.wait_ge(normed, 16)
            for k in range(8):
                fill(f_oT0 + k)
                for t in range(QT):
                    last = tr(ring(f_oT0 + k)[:, t * P:(t + 1) * P], o_cross0[:, t, k * P:(k + 1) * P], ident[:, :])
                last.then_inc(filled, 1)
            pe.wait_ge(drained, f_oT0 + 8)
            pe.wait_ge(w_block0_o, 48)
            project([oT0[:, k, :] for k in range(8)], [xo_w[:, k, :] for k in range(8)], PROJ_X0)

            pe.wait_ge(ln_done, LN_A0 + 1)
            transpose_tokens(f_hT1, h)
            pe.wait_ge(drained, f_hT1 + 1)
            pe.wait_ge(w_block0, 16 * 8)
            fill(f_lat)
            for c in range(CT):
                last = mm(ring(f_lat)[:, 0:TOK], a0_down[:, c, :], hT[:, c, :], start=c == 0, stop=c == CT - 1)
            last.then_inc(filled, 1)
            pe.wait_ge(drained, f_lat + 1)
            small(A0, latT)

            pe.wait_ge(ln_done, LN_F0 + 1)
            transpose_tokens(f_hT2, h)
            pe.wait_ge(drained, f_hT2 + 1)
            fill(f_p)
            for c in range(CT):
                last = mm(ring(f_p)[0:64, 0:TOK], f_U1[:, c, :], hT[:, c, :], start=c == 0, stop=c == CT - 1)
            last.then_inc(filled, 1)
            pe.wait_ge(drained, f_p + 1)
            gelu_fills(f_g0, lambda c, t: f_V1[0:64, t * P:(t + 1) * P], lambda c: lowT[0:64, :], 1)
            fill(f_q)
            pe.wait_ge(drained, f_g0 + FT)
            for t in range(FT):
                last = mm(ring(f_q)[0:64, 0:TOK], f_U2[:, t, :], gT0[:, t, :], start=t == 0, stop=t == FT - 1)
            last.then_inc(filled, 1)
            pe.wait_ge(drained, f_q + 1)
            project([low2T[0:64, :]], [f_V2[0:64, :]], PROJ_F0)

            pe.wait_ge(ln_done, LN_X1 + 1)
            transpose_tokens(f_hT3, h)
            for f in range(f_hT3 + 1, X1.first_fill):
                empty_fill(f)
            pe.wait_ge(drained, f_hT3 + 1)
            pe.wait_ge(wv_loaded, 16 * 5)
            value_fills(X1.first_fill)
            cross(X1, 16, 8)
            pe.wait_ge(normed, 32)
            transpose_tokens(f_oT1, o_cross1)
            pe.wait_ge(drained, f_oT1 + 1)
            pe.wait_ge(w_co, 16)
            project([hT[:, c, :] for c in range(CT)], [co_w[:, c, :] for c in range(CT)], PROJ_C)

            pe.wait_ge(x_updated, UP_CO + 1)
            transpose_tokens(f_xT4, h)
            pe.wait_ge(drained, f_xT4 + 1)
            pe.wait_ge(w_block1, 16 * 6)
            small(A1, hT)

            pe.wait_ge(x_updated, UP_SO + 1)
            transpose_tokens(f_xT5, h)
            pe.wait_ge(drained, f_xT5 + 1)
            gelu_fills(f_g1, lambda c, t: fi_w[:, c, t * P:(t + 1) * P], lambda c: hT[:, c, :], CT)
            pe.wait_ge(drained, f_g1 + FT)
            project([gT1[:, t, :] for t in range(FT)], [fo_w[:, t, :] for t in range(FT)], PROJ_FI)

            pe.wait_ge(ln_done, LN_A2 + 1)
            transpose_tokens(f_hT6, h)
            pe.wait_ge(drained, f_hT6 + 1)
            pe.wait_ge(w_attn2, 16 * 5)
            small(A2, hT)

            pe.wait_ge(ln_done, LN_MOE + 1)
            transpose_tokens(f_hT7, h)
            for f in range(f_hT7 + 1, f_moe):
                empty_fill(f)
            pe.wait_ge(drained, f_hT7 + 1)
            project([hT[:, c, :] for c in range(CT)], [switch_w[:, c, :] for c in range(CT)], PROJ_ROUTE)

            def hidden(k, f, loads):
                pe.wait_ge(expert_loaded[k], loads)
                for t in range(FT):
                    fill(f + t)
                    for c in range(CT):
                        last = mm(psum[:, 4 + t % 2, 0:TOK], w1[k][:, c, t * P:(t + 1) * P], hT[:, c, :],
                                  start=c == 0, stop=c == CT - 1)
                    last.then_inc(filled, 1)

            def output(k, f, added):
                pe.wait_ge(drained, f)
                if added is not None:
                    pe.wait_ge(moe_added, added)
                for q in range(QT):
                    for t in range(FT):
                        last = mm(psum[:, ACC + k, q * CH:(q + 1) * CH], moe_hT[k][:, t, q * P:(q + 1) * P],
                                  w2[k][:, t, :], start=t == 0, stop=t == FT - 1)
                last.then_inc(moe_y, 1)

            hidden(0, f_moe, 32)
            pe.wait_ge(sm_max, HEADS * 3 + 1)
            with pe.Fori(0, EXPERTS // 2 - 1) as i:
                hidden(1, i * (2 * FT) + (f_moe + FT), i * 32 + 32)
                output(0, i * (2 * FT) + (f_moe + FT), i * 2 + 1)
                hidden(0, i * (2 * FT) + (f_moe + 2 * FT), i * 32 + 64)
                output(1, i * (2 * FT) + (f_moe + 2 * FT), i * 2 + 2)
            n = EXPERTS // 2 - 1
            hidden(1, f_moe + (EXPERTS - 1) * FT, 32 * n + 32)
            output(0, f_moe + (EXPERTS - 1) * FT, 2 * n + 1)
            output(1, f_moe + EXPERTS * FT, 2 * n + 2)

        @block.vector
        def _(dve):
            v = nc.vector
            links = [0]

            def link(ins):
                links[0] += 1
                ins.then_inc(link_sem, 1)
                dve.wait_ge(link_sem, links[0])

            def norm(src, dst, ln):
                for t in range(QT):
                    ins = v.bn_stats(stats[:, t, :], src[:, t, :])
                link(ins)
                for t in range(QT):
                    ins = v.bn_aggr(mean_var[:, t, :], stats[:, t, :])
                link(ins)
                v.tensor_scalar(mean_var[:, :, 1], mean_var[:, :, 1], EPS, None, ALU.add).then_inc(ln_var, 1)
                dve.wait_ge(ln_dev, ln + 1)
                link(v.reciprocal(deviation[:, :], deviation[:, :]))
                for t in range(QT):
                    ins = v.tensor_scalar(dst[:, t, :], src[:, t, :], mean_var[:, t, 0:1], deviation[:, t:t + 1],
                                          ALU.subtract, ALU.mult)
                ins.then_inc(ln_done, 1)
                dve.wait_ge(ln_done, ln + 1)

            def both(r):
                return r.unsqueeze(1).to_broadcast([P, QT, CH])

            def add_projection(which, bias, residual, dst, up):
                dve.wait_ge(proj_done, which + 1)
                y = psum[:, PROJ_BANK[which], :].rearrange("p (t c) -> p t c", t=QT)
                if bias is not None:
                    link(v.tensor_tensor(o_cross1[:, :, :], y, both(bias), ALU.add))
                    y = o_cross1[:, :, :]
                ins = v.tensor_tensor(dst, y, residual, ALU.add)
                if up is not None:
                    ins.then_inc(x_updated, 1)
                    dve.wait_ge(x_updated, up + 1)
                else:
                    link(ins)

            def affine(g, b, up):
                link(v.tensor_tensor(h[:, :, :], h[:, :, :], both(g), ALU.mult))
                v.tensor_tensor(h[:, :, :], h[:, :, :], both(b), ALU.add).then_inc(x_updated, 1)
                dve.wait_ge(x_updated, up + 1)

            def cross(X, n0, o, bias_row):
                per_unit = 3

                def unit(g, u):
                    q = u % 2
                    n = g * 4 + (n0 + u)
                    c0 = g * (4 * per_unit) + u * per_unit
                    for c in range(CHUNKS):
                        chunk = side[:, q, :, c * BANK:(c + 1) * BANK]
                        if X.weighted and c % 2 == 0:
                            dve.wait_ge(side_loaded[q][c // 2], g * 32 + 16 * (u // 2 + 1))
                        dve.wait_ge(scores_ready, g * (4 * CHUNKS) + ((n0 + u) * CHUNKS + c + 1))
                        if not X.weighted:
                            dve.sem_inc(dve_passed)
                        if X.weighted:
                            v.tensor_tensor(chunk, psum[:, 2 * (c % 2):2 * (c % 2) + 2, :], chunk, ALU.mult
                                            ).then_inc(scores_used, 1)
                        else:
                            for j in range(2):
                                ins = v.tensor_tensor_reduce(
                                    out=chunk[:, j, :], in0=psum[:, 2 * (c % 2) + j, :],
                                    in1=key_mask[:, c * BANK:(c + 1) * BANK], scale=1.0, scalar=-3.0e38,
                                    op0=ALU.add, op1=ALU.max, accum_out=chunk_max[:, q, j, c:c + 1])
                            ins.then_inc(scores_used, 1)
                    dve.wait_ge(scores_used, g * (4 * CHUNKS) + (n0 + u + 1) * CHUNKS)
                    if X.weighted:
                        dve.wait_ge(mask_loaded[q], g * 32 + 16 * (u // 2 + 1))
                        dve.sem_inc(dve_passed)
                        for j in range(2):
                            ins = v.tensor_tensor_reduce(
                                out=side[:, q, j, :], in0=side[:, q, j, :], in1=masks[:, q, j, :], scale=1.0,
                                scalar=-3.0e38, op0=ALU.subtract, op1=ALU.max, accum_out=row_max[:, q, j:j + 1])
                        ins.then_inc(masked, 1)
                        dve.wait_ge(masked, n + 1)
                        v.tensor_scalar(no_key[:, 0, :], row_max[:, q, :], -0.5, 3.0e38, ALU.is_lt, ALU.mult
                                        ).then_inc(cross_link, 1)
                        dve.wait_ge(cross_link, c0 + 1)
                        v.tensor_scalar(no_key[:, 1, :], no_key[:, 0, :], 10.0, None, ALU.mult).then_inc(cross_link, 1)
                        dve.wait_ge(cross_link, c0 + 2)
                        v.tensor_tensor(no_key[:, 2, :], no_key[:, 1, :], no_key[:, 1, :], ALU.subtract
                                        ).then_inc(cross_link, 1)
                        dve.wait_ge(cross_link, c0 + 3)
                        v.scalar_tensor_tensor(out=exp_bias[:, q, :], in0=row_max[:, q, :], scalar=-1.0 / TINY,
                                               in1=no_key[:, 2, :], op0=ALU.mult, op1=ALU.add).then_inc(bias_ready, 1)
                    else:
                        v.tensor_reduce(exp_bias[:, q, :], chunk_max[:, q, :, :], AX.X, ALU.max, negate=True
                                        ).then_inc(bias_ready, 1)

                def normalise(g, u):
                    n = g * 4 + (n0 + u)
                    dve.wait_ge(exp_done, g * 8 + 2 * (n0 + u + 1))
                    dve.wait_ge(acc_back, n + 1)
                    v.reciprocal(row_inv[:, u, :], row_sum[:, u, :]).then_inc(norm_link, 1)
                    dve.wait_ge(norm_link, n + 1)
                    for j in range(2):
                        at = (g * 4 + (2 * (u // 2) + j)) * X.d
                        ins = v.scalar_tensor_tensor(
                            out=o[:, u % 2, bass.ds(at, X.d)], in0=psum[:, BACK, 64 * j:64 * j + X.d],
                            scalar=row_inv[:, u, j:j + 1], in1=bias_row[:, bass.ds(at, X.d)],
                            op0=ALU.mult, op1=ALU.add)
                    ins.then_inc(normed, 1)

                def turn(g, last):
                    unit(g, 1)
                    unit(g, 2)
                    normalise(g, 0)
                    unit(g, 3)
                    normalise(g, 1)
                    if not last:
                        unit(g, 4)
                    normalise(g, 2)
                    normalise(g, 3)

                unit(0, 0)
                with dve.Fori(0, X.turns - 1) as g:
                    turn(g, False)
                turn(X.turns - 1, True)

            def small(s, v_bias):
                s, B = SMALL_OPS[s.index][:2]
                base = HEADS * s.index
                ot = sum(SMALL_OPS[k][0].groups for k in range(s.index))
                for i in range(HEADS + 4):
                    if i < HEADS:
                        dve.wait_ge(sm_scores, base + i + 1)
                        scores = psum[:, i % 4, :].rearrange("p (q k) -> p q k", q=QT)
                        if s.causal:
                            if i >= 2:
                                dve.wait_ge(sm_exp, 2 * (base + i - 1))
                            v.tensor_tensor(B["masked"][:, i % 2, :, :], scores, causal, ALU.add).then_inc(sm_masked, 1)
                            dve.wait_ge(sm_masked, i + 1)
                            scores = B["masked"][:, i % 2, :, :]
                        v.tensor_reduce(s_max[:, i % 4, :], scores, AX.X, ALU.max, negate=True).then_inc(sm_max, 1)
                    if 2 <= i < HEADS + 2:
                        hd = i - 2
                        dve.wait_ge(sm_exp, 2 * (base + hd + 1))
                        link(v.reciprocal(s_inv[:, hd % 4, :], s_sum[:, hd % 4, :]))
                        for q in range(QT):
                            ins = v.tensor_scalar(B["p"][:, hd % 4, q, :], B["p"][:, hd % 4, q, :],
                                                  s_inv[:, hd % 4, q:q + 1], None, ALU.mult)
                        ins.then_inc(sm_norm, 1)
                    hd = i - 4
                    if hd >= 0 and hd % s.per == s.per - 1:
                        g = hd // s.per
                        dve.wait_ge(sm_pv, ot + g + 1)
                        if v_bias:
                            v.tensor_scalar(B["oT"][:, g, :], psum[:, ACC + g % 2, 0:TOK], col(v_bias, g), None,
                                            ALU.add).then_inc(sm_out, 1)
                        else:
                            v.tensor_copy(B["oT"][:, g, :], psum[:, ACC + g % 2, 0:TOK]).then_inc(sm_out, 1)

            v.memset(acc_sb[:, :], 0.0)
            dve.wait_ge(cols_loaded, 16)
            for at, name, scale in ((0, "xq", TINY * D0**-0.5), (8, "cq", D1**-0.5), (12, "sq", D1**-0.5)):
                n = COLS[name][1]
                ins = v.tensor_scalar(q_bias[:, at:at + n], cols[:, COLS[name][0]:COLS[name][0] + n], scale, None, ALU.mult)
            ins.then_inc(q_bias_ready, 1)
            dve.wait_ge(x_loaded, 16)
            norm(x, h, LN_X0)
            dve.wait_ge(rows_loaded, 16)
            cross(X0, 0, o_cross0, row("xv"))
            add_projection(PROJ_X0, row("xo"), x[:, :, :], x[:, :, :], UP_X0)
            norm(x, h, LN_A0)
            dve.wait_ge(w_block0_o, 48)
            small(A0, None)
            add_projection(PROJ_A0, None, x[:, :, :], x[:, :, :], UP_A0)
            norm(x, h, LN_F0)
            add_projection(PROJ_F0, row("f2"), x[:, :, :], x[:, :, :], UP_F0)
            norm(x, h, LN_X1)
            dve.wait_ge(key_mask_loaded, 16)
            cross(X1, 16, o_cross1, row("cv"))
            add_projection(PROJ_C, row("co_b"), h[:, :, :], h[:, :, :], None)
            norm(h, h, LN_CO)
            affine(row("co_g"), row("co_be"), UP_CO)
            small(A1, "sv")
            add_projection(PROJ_A1, row("so_b"), h[:, :, :], h[:, :, :], None)
            norm(h, h, LN_SO)
            affine(row("so_g"), row("so_be"), UP_SO)
            dve.wait_ge(late_loaded, 16)
            add_projection(PROJ_FI, late_row("fo_b"), h[:, :, :], h[:, :, :], None)
            norm(h, h, LN_FO)
            affine(late_row("fo_g"), late_row("fo_be"), UP_FO)
            link(v.tensor_tensor(x[:, :, :], x[:, :, :], h[:, :, :], ALU.add))
            norm(x, h, LN_A2)
            small(A2, None)
            add_projection(PROJ_A2, late_row("lo"), x[:, :, :], x[:, :, :], UP_A2)
            norm(x, h, LN_MOE)
            dve.wait_ge(proj_done, PROJ_ROUTE + 1)
            logits = psum[:, PROJ_BANK[PROJ_ROUTE], 0:QT * EXPERTS].rearrange("p (q e) -> p q e", q=QT)
            link(v.tensor_tensor(route[:, :, 0, :], logits,
                                 row("switch").unsqueeze(1).to_broadcast([P, QT, EXPERTS]), ALU.add))
            v.tensor_reduce(s_max[:, 0, :], route[:, :, 0, :], AX.X, ALU.max, negate=True).then_inc(sm_max, 1)
            dve.wait_ge(sm_max, HEADS * 3 + 1)
            for q in range(QT):
                ins = v.tensor_scalar(route[:, q, 2, :], route[:, q, 0, :], s_max[:, 0, q:q + 1], 0.0,
                                      ALU.add, ALU.is_equal)
            link(ins)
            link(v.tensor_tensor(route[:, :, 3, :], route[:, :, 2, :],
                                 row("rank").unsqueeze(1).to_broadcast([P, QT, EXPERTS]), ALU.mult))
            link(v.tensor_reduce(s_inv[:, 1, :], route[:, :, 3, :], AX.X, ALU.max))
            for q in range(QT):
                ins = v.tensor_scalar(route[:, q, 4, :], route[:, q, 3, :], s_inv[:, 1, q:q + 1], None, ALU.is_equal)
            link(ins)
            dve.wait_ge(route_exp, QT)
            link(v.reciprocal(s_inv[:, 0, :], s_sum[:, 0, :]))
            for q in range(QT):
                ins = v.tensor_scalar(coef[:, q, :], route[:, q, 4, :], s_inv[:, 0, q:q + 1], None, ALU.mult)
            link(ins)
            dve.wait_ge(b2_loaded, 16)
            v.sem_inc(moe_added, 2)

            def add_expert(k, e, done):
                dve.wait_ge(moe_y, done)
                v.tensor_tensor(h[:, :, :], psum[:, ACC + k, :].rearrange("p (q c) -> p q c", q=QT),
                                b2_rows[:, bass.ds(e, 1), :].to_broadcast([P, QT, CH]), ALU.add).then_inc(moe_link, 1)
                dve.wait_ge(moe_link, done)
                for q in range(QT):
                    ins = v.scalar_tensor_tensor(out=x[:, q, :], in0=h[:, q, :], scalar=coef[:, q, bass.ds(e, 1)],
                                                 in1=x[:, q, :], op0=ALU.mult, op1=ALU.add)
                ins.then_inc(moe_added, 1)
                dve.wait_ge(moe_added, done + 2)

            with dve.Fori(0, EXPERTS // 2) as i:
                add_expert(0, i * 2, i * 2 + 1)
                add_expert(1, i * 2 + 1, i * 2 + 2)


def padded(w, d, slot):
    out = np.zeros((w.shape[0], w.shape[1] // d, slot), w.dtype)
    out[:, :, :d] = w.reshape(w.shape[0], -1, d)
    return out.reshape(w.shape[0], -1)


def tiles(b):
    return b.reshape(-1, P).T


def laid_out(i):
    g = {k: np.asarray(w) for k, w in i.items()}
    pads = lambda b, d: padded(b.reshape(1, -1), d, 32)[0]
    cols = {"xq": g["L0_xattn_bq"], "xk": g["L0_xattn_bk"], "f1": g["L0_ffn_b1"],
            "cq": pads(g["L1_xattn_cq_b"], D1), "ck": pads(g["L1_xattn_ck_b"], D1),
            "sq": pads(g["L1_xattn_sq_b"], D1), "sk": pads(g["L1_xattn_sk_b"], D1),
            "sv": pads(g["L1_xattn_sv_b"], D1), "fi": g["L1_xattn_fi_b"], "m1": g["L1_ffn_b1"].reshape(-1)}
    rows = {"xv": g["L0_xattn_bv"], "xo": g["L0_xattn_bo"], "f2": g["L0_ffn_b2"], "cv": g["L1_xattn_cv_b"],
            "co_b": g["L1_xattn_co_b"], "co_g": g["L1_xattn_co_g"], "co_be": g["L1_xattn_co_be"],
            "so_b": g["L1_xattn_so_b"], "so_g": g["L1_xattn_so_g"], "so_be": g["L1_xattn_so_be"],
            "switch": g["L1_ffn_switch_b"], "rank": np.arange(EXPERTS, 0, -1, dtype=np.float32)}
    causal = np.where(np.tril(np.ones((TOK, TOK), bool)), 0.0, -1e30).astype(np.float32)
    out = {
        "x": g["x"][0], "ctxT": g["ctx_1024"][0].T, "side": g["fside_Bx16xSxS2_0"][0],
        "mask": g["mask_Bx16xSxS2_bk1"][0], "key_mask": g["mask_Bx1x1xS2_ff0"].reshape(1, KEYS),
        "ident": np.eye(P, dtype=np.float32), "causal": causal,
        "cols": np.concatenate([tiles(cols[k]) for k in COLS], 1),
        "rows": np.concatenate([rows[k] for k in ROWS])[None],
        "late": np.concatenate([g["L1_xattn_fo_b"], g["L1_xattn_fo_g"], g["L1_xattn_fo_be"], g["L1_attn_bo"]])[None],
        "x_wq": g["L0_xattn_Wq"].T, "x_wk": g["L0_xattn_Wk"].T, "x_wv": g["L0_xattn_Wv"].T, "x_wo": g["L0_xattn_Wo"].T,
        "a_down": g["L0_attn_w_kv_down"], "a_kup": g["L0_attn_w_kv_up"][:, :1024], "a_vup": g["L0_attn_w_kv_up"][:, 1024:],
        "a_q": g["L0_attn_w_q"], "a_out": g["L0_attn_w_out"],
        "f_U1": g["L0_ffn_U1"], "f_V1": g["L0_ffn_V1"], "f_U2": g["L0_ffn_U2"], "f_V2": g["L0_ffn_V2"],
        "c_wq": padded(g["L1_xattn_cq_w"], D1, 32), "c_wk": padded(g["L1_xattn_ck_w"], D1, 32),
        "c_wv": g["L1_xattn_cv_w"], "c_wo": g["L1_xattn_co_w"],
        "s_wq": padded(g["L1_xattn_sq_w"], D1, 32), "s_wk": padded(g["L1_xattn_sk_w"], D1, 32),
        "s_wv": padded(g["L1_xattn_sv_w"], D1, 32), "s_wo": padded(g["L1_xattn_so_w"].T, D1, 32).T,
        "fi_w": g["L1_xattn_fi_w"], "fo_w": g["L1_xattn_fo_w"],
        "l_wq": padded(g["L1_attn_Wq"].T, DL, 32), "l_wk": padded(g["L1_attn_Wk"].T, DL, 32),
        "l_wv": padded(g["L1_attn_Wv"].T, DL, 32), "l_wo": padded(g["L1_attn_Wo"], DL, 32).T,
        "switch_w": g["L1_ffn_switch_w"], "w1": g["L1_ffn_w1"], "w2": g["L1_ffn_w2"], "b2": g["L1_ffn_b2"].reshape(1, -1),
    }
    return {k: np.ascontiguousarray(w) for k, w in out.items()}


def kernel(**inputs):
    from concourse import bacc as _bacc
    from concourse import mybir as _mybir
    from concourse.bass_utils import run_bass_kernel_spmd as _run

    nc = _bacc.Bacc("TRN2", target_bir_lowering=False, num_devices=1)
    arrays, aps = {}, {}
    for name, w in laid_out(inputs).items():
        arrays[f"in_{name}"] = w
        aps[name] = nc.dram_tensor(f"in_{name}", w.shape, _mybir.dt.from_np(w.dtype), kind="ExternalInput").ap()
    aps["out"] = nc.dram_tensor("out_x", (TOK, CH), _mybir.dt.float32, kind="ExternalOutput").ap()
    program(nc, aps)
    r = _run(nc, [arrays], core_ids=[0])
    return r.results[0]["out_x"][None]
```

```python
from contextlib import ExitStack

import numpy as np

import concourse.bass as bass
from concourse import mybir

F32 = mybir.dt.float32
F32R = mybir.dt.float32r
U8 = mybir.dt.uint8
ALU = mybir.AluOpType
ACT = mybir.ActivationFunctionType
AX = mybir.AxisListType

P = 128
TOK = 256
QT = TOK // P
CH = 256
CT = CH // P
KEYS = 4096
HEADS = 16
FF = 1024
FT = FF // P
EXPERTS = 8
BANK = 512
CHUNKS = KEYS // BANK
KT = KEYS // P
PIECES = 4
PIECE = KEYS // PIECES
EPS = 1e-5

TINY = 2.0**-60
D0, D1, DL = 64, 16, 8

COLS, NCOLS = {}, 0
for _name, _n in (("xq", 8), ("xk", 8), ("f1", FT), ("cq", 16), ("ck", 2), ("pick", 2), ("sq", 4), ("sk", 4),
                  ("sv", 4), ("fi", FT), ("m1", EXPERTS * FT)):
    COLS[_name] = NCOLS, _n
    NCOLS += _n
ROWS, NROWS = {}, 0
for _name, _n in (("xv", 1024), ("xo", CH), ("f2", CH), ("cv", CH), ("co_b", CH), ("co_g", CH),
                  ("co_be", CH), ("so_b", CH), ("so_g", CH), ("so_be", CH), ("switch", EXPERTS),
                  ("rank", EXPERTS)):
    ROWS[_name] = NROWS, _n
    NROWS += _n
LATE = {"fo_b": 0, "fo_g": CH, "fo_be": 2 * CH, "lo": 3 * CH}


PAIRS = HEADS // 2
GROUPS = KT // 2
STEPS = 4 * CHUNKS
LOOKS = [0, 1, 3, 3, 2, 3, 2, 3, 2, 3, 2, 3, 2, 3, 0, 0]


class Weighted:

    TURNS = 4
    QK = 2 + CHUNKS

    def __init__(self, first_fill):
        self.first_fill = first_fill
        self.f0 = first_fill + self.QK
        v, t = KT // 2, 2 * CHUNKS
        self.at = {"v": 0, "t0": v, "qk": v + t}
        self.at["t1"] = self.at["qk"] + self.QK
        self.at["t2"] = self.at["t1"] + t
        self.at["next"] = self.at["t3_last"] = self.at["t2"] + t
        self.at["t3"] = self.at["next"] + self.QK
        self.per_turn = self.at["t3"] + t
        self.end_fill = self.f0 + (self.TURNS - 1) * self.per_turn + self.at["t3_last"] + t

    def fill(self, g, what, k=0):
        return g * self.per_turn + (self.f0 + self.at[what] + k)

    def probs_fill(self, g, u, last, t, j):
        return self.fill(g, f"t{u}" + ("_last" if last and u == 3 else ""), 2 * t + j)


class Small:

    def __init__(self, index, name, first_fill, slot, q_from, kv_from, causal, q_scale):
        self.index, self.name, self.slot = index, name, slot
        self.q_tiles, self.kv_tiles, self.causal, self.q_scale = q_from, kv_from, causal, q_scale
        self.per = P // slot
        self.groups = HEADS // self.per
        self.width = HEADS * slot
        self.f_q = first_fill
        self.f_k = self.f_q + self.groups
        self.f_v = self.f_k + self.groups
        self.f_t = self.f_v + QT * self.width // BANK
        self.end_fill = self.f_t + HEADS


def program(nc, a):
    ctx = ExitStack()
    with ctx:
        starts = {}

        def sbuf(name, shape):
            tensor = ctx.enter_context(nc.sbuf_tensor(name + "_sb", shape, F32))
            starts[name] = nc.sbuf_base - 4 * int(np.prod(shape[1:]))
            return tensor

        def rounded(name, arena, at, shape):
            return nc.alloc_sbuf_tensor_at(name + "_sb", [P, *shape], F32R, offset=starts[arena] + 4 * at)

        def sem(name):
            return ctx.enter_context(nc.semaphore(name))

        f_hT0 = 0
        X0 = Weighted(1 + 1)
        f_oT0 = X0.end_fill
        f_hT1 = f_oT0 + 8
        f_lat = f_hT1 + 1
        A0 = Small(0, "a0", f_lat + 1, 64, CT, 1, True, D0**-0.5)
        f_hT2 = A0.end_fill
        f_p = f_hT2 + 1
        f_g0 = f_p + 1
        f_q = f_g0 + FT
        f_hT3 = f_q + 1
        f_k1 = f_hT3 + 1
        f_v1 = f_k1 + 2 * CHUNKS
        f_oT1 = f_v1 + KT // 2
        f_xT4 = f_oT1 + 1
        A1 = Small(1, "a1", f_xT4 + 1, 32, CT, CT, False, D1**-0.5)
        f_xT5 = A1.end_fill
        f_g1 = f_xT5 + 1
        f_hT6 = f_g1 + FT
        A2 = Small(2, "a2", f_hT6 + 1, 32, 1, 1, False, 0.25)
        f_hT7 = A2.end_fill
        f_moe = f_hT7 + 1 + (f_hT7 + 1) % 2

        w_arena = sbuf("w_arena", [P, 4 * KEYS])
        ck_arena = sbuf("ck_arena", [P, 3 * KEYS])
        v_arena = sbuf("v_arena", [P, KT * 256])
        m_arena = sbuf("m_arena", [P, KEYS])
        o_arena = sbuf("o_arena", [P, 2048])
        p_arena = sbuf("p_arena", [P, 2048])
        rows = sbuf("rows", [P, NROWS])
        cols = sbuf("cols", [P, NCOLS])
        ident = sbuf("ident", [P, P])
        fold = sbuf("fold", [P, 64])
        x = sbuf("x", [P, QT, CH])
        h = sbuf("h", [P, QT, CH])
        hT = sbuf("hT", [P, CT, TOK])
        qz_cross = sbuf("qz_cross", [P, 4, TOK])
        wq_stage = sbuf("wq_stage", [P, CT, P])
        wk_stage = sbuf("wk_stage", [P, CT, P])
        wv_stage = sbuf("wv_stage", [P, CT, 256])
        acc_sb = sbuf("acc_sb", [P, P])
        o_cross1 = sbuf("o_cross1", [P, QT, CH])
        row_max = sbuf("row_max", [P, QT, 2])
        no_key = sbuf("no_key", [P, 3, 2])
        exp_bias = sbuf("exp_bias", [P, QT, 2])
        row_sum = sbuf("row_sum", [P, 4, 2])
        row_inv = sbuf("row_inv", [P, 4, 2])
        stats = sbuf("stats", [P, QT, 6])
        mean_var = sbuf("mean_var", [P, QT, 2])
        deviation = sbuf("deviation", [P, QT])
        q_bias = sbuf("q_bias", [P, 28])
        s_max = sbuf("s_max", [P, 4, QT])
        s_sum = sbuf("s_sum", [P, 4, QT])
        s_inv = sbuf("s_inv", [P, 4, QT])
        route = sbuf("route", [P, QT, 5, EXPERTS])
        coef = sbuf("coef", [P, QT, EXPERTS])

        def view(arena, at, *shape):
            n = int(np.prod(shape))
            ap = arena[:, at:at + n]
            if len(shape) == 1:
                return ap
            names = "abcd"[:len(shape)]
            return ap.rearrange(f"p ({' '.join(names)}) -> p {' '.join(names)}",
                                **{k: v for k, v in zip(names[1:], shape[1:])})

        side = view(w_arena, 0, QT, 2, KEYS)
        ctxT = view(ck_arena, 0, CT, KEYS)
        keysT = view(ck_arena, 2 * KEYS, KEYS)
        values = view(v_arena, 0, KT, 256)
        masks = m_arena[:, :].bitcast(U8).rearrange("p (q j k) -> p q j k", q=QT, j=2)
        o_cross0 = view(o_arena, 0, QT, 1024)
        probsT = view(p_arena, 0, 2, 2, 4, P)
        xo_w = view(m_arena, 0, FT, CH)
        oT0 = view(w_arena, 0, FT, TOK)
        a0_q, a0_k, a0_v = view(v_arena, 0, CT, 1024), view(v_arena, 2048, 1, 1024), view(v_arena, 3072, 1, 1024)
        a0_o, a0_down = view(v_arena, 4096, 8, CH), view(v_arena, 6144, CT, P)
        f_U1, f_V1 = view(v_arena, 6400, CT, 64), view(v_arena, 6528, FF)
        f_U2, f_V2 = view(v_arena, 7552, FT, 64), view(m_arena, 2048, CH)
        causal = view(m_arena, 2304, QT, TOK)
        latT = view(m_arena, 2816, 1, TOK)
        lowT = view(m_arena, 3072, TOK)
        low2T = view(m_arena, 3328, TOK)
        gT0 = view(w_arena, 2048, FT, TOK)
        key_parts = view(w_arena, 0, 2, 2, KEYS).bitcast(F32R)
        stack = [rounded("stack0", "ck_arena", 2 * KEYS, (KEYS,)), rounded("stack1", "m_arena", 0, (KEYS,))]
        q_stack = [rounded(f"q_stack{k}", "qz_cross", 2 * k * TOK, (2, TOK)) for k in range(2)]
        probsT1 = view(p_arena, 0, 2, 2, 2, TOK)
        pair_values = view(ck_arena, 0, 2, KT, 2, 32)
        q_whole = view(o_arena, 0, 2, TOK)
        acc1_sb, scaled = view(o_arena, 512, TOK), view(o_arena, 768, QT, 2, D1)
        sum_inv, pair_max = view(o_arena, 832, QT, 2), view(o_arena, 840, QT, 2, CHUNKS)
        neg_max, neg_parts = view(o_arena, 872, QT, 2), view(o_arena, 880, QT, 2, 2)
        neg_high = view(o_arena, 888, QT, 2).bitcast(F32R)
        MASK_TILE = KEYS // P
        mask_raw, ones = view(o_arena, 900, MASK_TILE), view(o_arena, 1024, BANK)
        mask_parts = view(o_arena, 940, 2, MASK_TILE).bitcast(F32R)
        co_w = wv_stage[:, :, :]
        a1_q, a1_k, a1_v = (view(v_arena, 1024 * i, CT, 512) for i in range(3))
        a1_o, fi_w, fo_w = view(v_arena, 3072, 4, CH), view(v_arena, 4096, CT, FF), view(v_arena, 6144, FT, CH)
        a2_q, a2_k, a2_v = (view(m_arena, 512 * i, 1, 512) for i in range(3))
        a2_o, switch_w = view(m_arena, 1536, 4, CH), view(m_arena, 2560, CT, EXPERTS)
        gT1 = view(o_arena, 0, FT, TOK)
        b2_rows = view(p_arena, 0, EXPERTS, CH)
        w1 = [view(w_arena, 4096 * k, CT, FF) for k in range(2)]
        w2 = [view(w_arena, 4096 * k + 2048, FT, CH) for k in range(2)]
        moe_hT = [view(ck_arena, 2048 * k, FT, TOK) for k in range(2)]

        def small_views(arena, at, s):
            v = {}
            for name, shape in (("qz", (HEADS, TOK)), ("kT", (s.groups, TOK)), ("v", (QT, s.width)),
                                ("p", (4, QT, TOK)), ("oT", (s.groups, TOK)), ("pT", (2, QT, TOK)),
                                ("masked", (2, QT, TOK) if s.causal else (1, 1))):
                v[name] = view(arena, at, *shape)
                at += int(np.prod(shape))
            return v

        B0 = small_views(w_arena, 0, A0)
        B1 = small_views(ck_arena, 0, A1)
        B2 = small_views(ck_arena, 0, A2)
        SMALL_OPS = {0: (A0, B0, a0_q, a0_k, a0_v, a0_o), 1: (A1, B1, a1_q, a1_k, a1_v, a1_o),
                     2: (A2, B2, a2_q, a2_k, a2_v, a2_o)}

        def row(name):
            at, n = ROWS[name]
            return rows[:, at:at + n]

        def late_row(name):
            return rows[:, LATE[name]:LATE[name] + CH]

        def col(name, i=0):
            return cols[:, bass.ds(COLS[name][0] + i, 1)]

        psum = ctx.enter_context(nc.psum_tensor("psum", [P, 8, BANK], F32))
        ACC, BACK = 6, 7
        q_psum = psum[:, BACK, TOK:2 * TOK]

        def ring(f):
            return psum[:, 4 + f % 2, :]

        x_loaded, cols_loaded, ident_loaded, rows_loaded = map(sem, ("x_loaded", "cols_loaded", "ident_loaded", "rows_loaded"))
        ctx_loaded = [sem(f"ctx_loaded{i}") for i in range(PIECES)]
        side_loaded = [[sem(f"side_loaded{q}_{i}") for i in range(PIECES)] for q in range(QT)]
        mask_loaded = [sem(f"mask_loaded{q}") for q in range(QT)]
        wqk_loaded, wv_loaded = sem("wqk_loaded"), sem("wv_loaded")
        w_block0, w_block0_o, w_co, w_block1, w_attn2, late_loaded, b2_loaded = map(
            sem, ("w_block0", "w_block0_o", "w_co", "w_block1", "w_attn2", "late_loaded", "b2_loaded"))
        key_mask_loaded = sem("key_mask_loaded")
        stack_loaded = [[sem(f"stack_loaded{b}_{i}") for i in range(PIECES)] for b in range(2)]
        k_loaded, v_loaded1 = sem("k_loaded"), sem("v_loaded1")
        q_loaded = [sem(f"q_loaded{k}") for k in range(2)]
        keys_high, keys_low, mask_split, mask_placed = map(
            sem, ("keys_high", "keys_low", "mask_split", "mask_placed"))
        q_made, q_high, q_ready, look_ready, look_used = map(
            sem, ("q_made", "q_high", "q_ready", "look_ready", "look_used"))
        neg_ready, neg_turned, neg_placed = sem("neg_ready"), sem("neg_turned"), sem("neg_placed")
        st_ready, st_exp, probs_used = map(sem, ("st_ready", "st_exp", "probs_used"))
        acc1_copied, folded, normed1 = sem("acc1_copied"), sem("folded"), sem("normed1")
        pair_link, norm1_link = sem("pair_link"), sem("norm1_link")
        w1_loaded, w2_loaded = ([sem(f"{w}_loaded{k}") for k in range(2)] for w in ("w1", "w2"))
        filled, drained = sem("filled"), sem("drained")
        scores_ready, scores_used = sem("scores_ready"), sem("scores_used")
        masked, bias_ready, exp_done = sem("masked"), sem("bias_ready"), sem("exp_done")
        pv_done, acc_copied, acc_back, normed = sem("pv_done"), sem("acc_copied"), sem("acc_back"), sem("normed")
        cross_link, norm_link, moe_link, link_sem = sem("cross_link"), sem("norm_link"), sem("moe_link"), sem("vector_link")
        values_copied = sem("values_copied")
        ln_var, ln_dev, ln_done = sem("ln_var"), sem("ln_dev"), sem("ln_done")
        q_zeroed = sem("q_zeroed")
        q_bias_ready = sem("q_bias_ready")
        proj_done, x_updated = sem("proj_done"), sem("x_updated")
        sm_scores, sm_masked, sm_max, sm_exp, sm_norm, sm_pv, sm_out = map(
            sem, ("sm_scores", "sm_masked", "sm_max", "sm_exp", "sm_norm", "sm_pv", "sm_out"))
        route_exp, moe_y, moe_added = sem("route_exp"), sem("moe_y"), sem("moe_added")
        out_stored = sem("out_stored")
        sp_passed, act_passed, dve_passed = sem("sp_passed"), sem("act_passed"), sem("dve_passed")

        (PROJ_X0, PROJ_A0, PROJ_F0, PROJ_C, PROJ_A1, PROJ_FI, PROJ_A2, PROJ_ROUTE) = range(8)
        PROJ_BANK = [ACC, BACK, BACK, ACC, BACK, ACC, BACK, ACC]
        LN_X0, LN_A0, LN_F0, LN_X1, LN_CO, LN_SO, LN_FO, LN_A2, LN_MOE = range(9)
        UP_X0, UP_A0, UP_F0, UP_CO, UP_SO, UP_FO, UP_A2 = range(7)

        block = ctx.enter_context(nc.Block())

        @block.sync
        def _(sp):
            def wait_then(sem_, value):
                sp.wait_ge(sem_, value)
                sp.sem_inc(sp_passed)

            def load_side(q, i, pair):
                sp.dma_start(side[:, q, :, i * PIECE:(i + 1) * PIECE],
                             a["side"][bass.ds(pair * 2, 2), q * P:(q + 1) * P, i * PIECE:(i + 1) * PIECE]
                             .rearrange("h p k -> p h k")).then_inc(side_loaded[q][i], 16)

            def load_mask(q, pair):
                sp.dma_start(masks[:, q, :, :], a["mask"][bass.ds(pair * 2, 2), q * P:(q + 1) * P, :]
                             .rearrange("h p k -> p h k")).then_inc(mask_loaded[q], 16)

            def load_qk(wq, wk, m):
                for stage, w in ((wq_stage, wq), (wk_stage, wk)):
                    sp.dma_start(stage[:, :, :], w.rearrange("(c p) n -> p c n", p=P)[:, :, bass.ds(m * P, P)]
                                 ).then_inc(wqk_loaded, 16)

            def load_wv(g):
                sp.dma_start(wv_stage[:, :, :], a["x_wv"].rearrange("(c p) n -> p c n", p=P)[:, :, bass.ds(g * 256, 256)]
                             ).then_inc(wv_loaded, 16)

            def load(dst, src, done):
                sp.dma_start(dst, src).then_inc(done, 16)

            def tiled(name):
                return a[name].rearrange("(c p) n -> p c n", p=P)

            load(x[:, :, :], a["x"].rearrange("(t p) c -> p t c", p=P), x_loaded)
            load(ident[:, :], a["ident"], ident_loaded)
            load(fold[:, :], a["fold"], ident_loaded)
            load(cols[:, :], a["cols"], cols_loaded)
            load_qk(a["x_wq"], a["x_wk"], 0)
            for i in range(PIECES):
                load(ctxT[:, :, i * PIECE:(i + 1) * PIECE], tiled("ctxT")[:, :, i * PIECE:(i + 1) * PIECE], ctx_loaded[i])
                load_side(0, i, 0)
            load_wv(0)
            load_mask(0, 0)
            load(rows[:, :], a["rows"].to_broadcast([P, NROWS]), rows_loaded)
            load_mask(1, 0)
            for i in range(PIECES):
                load_side(1, i, 0)

            def next_unit(g, u, last):
                pair = g * 2 + (u + 2) // 2
                wait_then(masked, g * 4 + (u + 1))
                load_mask(u % 2, pair)
                for i in range(PIECES):
                    wait_then(filled, X0.probs_fill(g, u, last, 2 * i + 1, 1) + 1)
                    load_side(u % 2, i, pair)

            def turn(g, last):
                if not last:
                    wait_then(filled, X0.fill(g, "t0"))
                    load_wv(g + 1)
                next_unit(g, 0, last)
                if not last:
                    wait_then(filled, X0.fill(g, "qk", 2 + CHUNKS))
                    load_qk(a["x_wq"], a["x_wk"], g * 2 + 2)
                next_unit(g, 1, last)
                if not last:
                    next_unit(g, 2, last)
                    wait_then(filled, X0.fill(g, "next", 2 + CHUNKS))
                    load_qk(a["x_wq"], a["x_wk"], g * 2 + 3)
                    next_unit(g, 3, last)

            wait_then(filled, X0.f0)
            load_qk(a["x_wq"], a["x_wk"], 1)
            with sp.Fori(0, X0.TURNS - 1) as g:
                turn(g, False)
            turn(X0.TURNS - 1, True)

            wait_then(masked, 16)
            load(xo_w, tiled("x_wo"), w_block0_o)
            load(f_V2[0:64, :], a["f_V2"], w_block0_o)
            load(causal, a["causal"].rearrange("(t p) k -> p t k", p=P), w_block0_o)
            wait_then(pv_done, 16)
            for dst, name in ((a0_down, "a_down"), (a0_q, "a_q"), (a0_k, "a_kup"), (a0_v, "a_vup"),
                              (a0_o, "a_out"), (f_U1, "f_U1"), (f_U2, "f_U2")):
                load(dst, tiled(name), w_block0)
            load(f_V1[0:64, :], a["f_V1"], w_block0)
            load(wk_stage[:, :, :], tiled("c_wk")[:, :, 0:P], k_loaded)
            load(wq_stage[:, :, :], tiled("c_wk")[:, :, P:2 * P], k_loaded)
            load(wv_stage[:, :, :], tiled("c_wv"), v_loaded1)
            wait_then(normed, 16)
            load(rows[:, 0:1024], a["late"].to_broadcast([P, 1024]), late_loaded)
            wait_then(proj_done, PROJ_X0 + 1)
            load(mask_raw, a["key_mask"], key_mask_loaded)

            def load_q(n):
                load((wk_stage, wq_stage)[n % 2][:, :, :], tiled("c_wq")[:, :, n * P:(n + 1) * P], q_loaded[n % 2])

            wait_then(filled, f_k1 + CHUNKS)
            load_q(0)
            wait_then(filled, f_k1 + 2 * CHUNKS)
            load_q(1)
            wait_then(filled, f_v1 + KT // 2)
            load(co_w, tiled("c_wo"), w_co)
            for n in range(2, PAIRS):
                wait_then(q_made, n - 1)
                load_q(n)
            for b in range(2):
                for i in range(PIECES):
                    wait_then(stack_loaded[b][i], 48 * (PAIRS // 2))
            wait_then(normed1, PAIRS)
            for dst, name in ((a1_q, "s_wq"), (a1_k, "s_wk"), (a1_v, "s_wv"), (a1_o, "s_wo"),
                              (fi_w, "fi_w"), (fo_w, "fo_w")):
                load(dst, tiled(name), w_block1)
            for dst, name in ((a2_q, "l_wq"), (a2_k, "l_wk"), (a2_v, "l_wv"), (a2_o, "l_wo"),
                              (switch_w, "switch_w")):
                load(dst, tiled(name), w_attn2)
            load(b2_rows.rearrange("p e c -> p (e c)"), a["b2"].to_broadcast([P, EXPERTS * CH]), b2_loaded)

            def load_w1(k, e):
                sp.dma_start(w1[k], a["w1"][bass.ds(e, 1), :, :].rearrange("o (c p) f -> p (o c) f", p=P)
                             ).then_inc(w1_loaded[k], 16)

            def load_w2(k, e):
                sp.dma_start(w2[k], a["w2"][bass.ds(e, 1), :, :].rearrange("o (f p) c -> p (o f) c", p=P)
                             ).then_inc(w2_loaded[k], 16)

            for k in range(2):
                load_w1(k, k)
                load_w2(k, k)
            with sp.Fori(0, EXPERTS // 2 - 1) as i:
                for k in range(2):
                    wait_then(filled, i * (2 * FT) + (f_moe + (k + 1) * FT))
                    load_w1(k, i * 2 + (k + 2))
                    wait_then(moe_y, i * 2 + (k + 1))
                    load_w2(k, i * 2 + (k + 2))
            wait_then(moe_added, EXPERTS + 2)
            sp.dma_start(a["out"].rearrange("(t p) c -> p t c", p=P), x[:, :, :]).then_inc(out_stored, 16)
            sp.wait_ge(out_stored, 16)

        @block.gpsimd
        def _(pool):
            nc.gpsimd.memset(qz_cross[:, :, :], 0.0).then_inc(q_zeroed, 1)
            pool.wait_ge(proj_done, PROJ_X0 + 1)
            nc.gpsimd.memset(B0["qz"], 0.0).then_inc(q_zeroed, 1)

            def load_stack(n, i):
                at = slice(32 * (n % 4), 32 * (n % 4 + 1))
                keys = slice(i * PIECE, (i + 1) * PIECE)
                for b, part in enumerate((0, 1, 0)):
                    pool.dma_start(stack[n % 2][32 * b:32 * (b + 1), keys], key_parts[at, n // 4, part, keys]
                                   ).then_inc(stack_loaded[n % 2][i], 16)

            pool.wait_ge(mask_split, 1)
            for b in range(2):
                for part in range(2):
                    pool.dma_start(stack[b][100 + part:101 + part, :].rearrange("o (p k) -> o p k", p=P),
                                   mask_parts[:, part, :]).then_inc(mask_placed, 16)
            for i in range(PIECES):
                pool.wait_ge(keys_low, 2 * i + 2)
                load_stack(0, i)
            for i in range(PIECES):
                load_stack(1, i)
            pool.wait_ge(filled, f_v1 + KT // 2)
            nc.gpsimd.memset(pair_values[:, :, :, :, D1:32], 0.0).then_inc(values_copied, 1)
            pool.wait_ge(values_copied, 1)
            for b in range(2):
                ins = nc.gpsimd.memset(pair_values[:, b, :, :, D1:D1 + 1], 1.0)
            pool.wait_ge(drained, f_v1 + KT // 2)
            for n in range(PAIRS):
                if n >= 2:
                    if n == PAIRS // 2:
                        pool.wait_ge(keys_low, CHUNKS + 1)
                    for i in range(PIECES):
                        pool.wait_ge(st_ready, GROUPS * (n - 2) + 4 * (i + 1))
                        load_stack(n, i)
                    pool.wait_ge(probs_used, (n - 1) * GROUPS)
                nc.gpsimd.tensor_copy(pair_values[:, n % 2, :, :, 0:D1],
                                      values[:, :, n * 2 * D1:(n + 1) * 2 * D1].rearrange("p k (j d) -> p k j d", j=2)
                                      ).then_inc(values_copied, 1)
            pool.wait_ge(normed1, PAIRS)
            nc.gpsimd.memset(B1["qz"], 0.0).then_inc(q_zeroed, 1)

        @block.scalar
        def _(act):
            def drain(f, dst, src=None, func=ACT.Copy, **kw):
                act.wait_ge(filled, f + 1)
                nc.scalar.activation(dst, src, func, **kw).then_inc(drained, 1)

            def drain_hT(f):
                drain(f, hT[:, :, :], ring(f).rearrange("p (c t) -> p c t", c=CT))

            def deviations(ln):
                act.wait_ge(ln_var, ln + 1)
                nc.scalar.activation(deviation[:, :], mean_var[:, :, 1], ACT.Sqrt).then_inc(ln_dev, 1)

            def q_k(X, f, par, m, qcol, kcol, scale):
                for q in range(QT):
                    act.wait_ge(filled, f + q + 1)
                    act.sem_inc(act_passed)
                    b = psum[:, 4 + (par + q) % 2, :]
                    for j in range(2):
                        s = slice(j * 64, (j + 1) * 64)
                        last = nc.scalar.activation(qz_cross[s, j, q * P:(q + 1) * P], b[s, 0:P], ACT.Identity,
                                                    bias=q_bias[s, bass.ds(qcol + m, 1)], scale=scale)
                    last.then_inc(drained, 1)
                for c in range(CHUNKS):
                    act.wait_ge(filled, f + 2 + c + 1)
                    act.sem_inc(act_passed)
                    nc.scalar.activation(keysT[:, c * BANK:(c + 1) * BANK], psum[:, 4 + (par + c) % 2, :],
                                         ACT.Identity, bias=col(kcol, m)).then_inc(drained, 1)

            def exps(X, n0, g, u):
                act.wait_ge(bias_ready, g * 4 + (n0 + u + 1))
                for j in range(2):
                    nc.scalar.activation(side[:, u % 2, j, :], side[:, u % 2, j, :], ACT.Exp,
                                         bias=exp_bias[:, u % 2, j:j + 1], scale=1.0 / TINY,
                                         accum_out=row_sum[:, u, j:j + 1]).then_inc(exp_done, 1)

            def probs(X, n0, g, u, last):
                for t in range(CHUNKS):
                    for j in range(2):
                        f = X.probs_fill(g, u, last, t, j)
                        act.wait_ge(filled, f + 1)
                        nc.scalar.activation(probsT[:, t % 2, j, :, :],
                                             psum[:, 4 + j, :].rearrange("p (i q) -> p i q", i=4),
                                             ACT.Copy).then_inc(drained, 1)
                act.wait_ge(pv_done, g * 4 + (n0 + u + 1))
                nc.scalar.activation(acc_sb[:, :], psum[:, ACC, 0:P], ACT.Copy).then_inc(acc_copied, 1)

            def cross(X, n0, qcol, kcol, scale):
                def turn(g, last):
                    if True:
                        for k in range(KT // 2):
                            act.wait_ge(filled, X.fill(g, "v", k) + 1)
                            nc.scalar.activation(values[:, 2 * k:2 * k + 2, :], psum[:, 4 + k % 2, :]
                                                 .rearrange("p (k n) -> p k n", k=2), ACT.Copy).then_inc(drained, 1)
                    exps(X, n0, g, 0)
                    probs(X, n0, g, 0, last)
                    if True:
                        q_k(X, X.fill(g, "qk"), 0, g * 2 + 1, qcol, kcol, scale)
                    exps(X, n0, g, 1)
                    probs(X, n0, g, 1, last)
                    exps(X, n0, g, 2)
                    probs(X, n0, g, 2, last)
                    if not last:
                        q_k(X, X.fill(g, "next"), 0, g * 2 + 2, qcol, kcol, scale)
                    exps(X, n0, g, 3)
                    probs(X, n0, g, 3, last)

                q_k(X, X.f0 - 2 - CHUNKS, 0, 0, qcol, kcol, scale)
                with act.Fori(0, X.TURNS - 1) as g:
                    turn(g, False)
                turn(X.TURNS - 1, True)

            def small(s):
                s, B = SMALL_OPS[s.index][:2]
                act.wait_ge(q_zeroed, 2 if s.index == 0 else 3)
                for g in range(s.groups):
                    f = s.f_q + g
                    act.wait_ge(filled, f + 1)
                    for j in range(s.per):
                        sl = slice(j * s.slot, (j + 1) * s.slot)
                        bias = dict(bias=q_bias[sl, 24 + g:25 + g]) if s.index == 1 else {}
                        last = nc.scalar.activation(B["qz"][sl, g * s.per + j, :], ring(f)[sl, 0:TOK],
                                                    ACT.Identity if bias else ACT.Copy, scale=s.q_scale, **bias)
                    last.then_inc(drained, 1)
                for g in range(s.groups):
                    f = s.f_k + g
                    if s.index == 1:
                        drain(f, B["kT"][:, g, :], ring(f)[:, 0:TOK], ACT.Identity, bias=col("sk", g))
                    else:
                        drain(f, B["kT"][:, g, :], ring(f)[:, 0:TOK])
                for k in range(QT * s.width // BANK):
                    t, c = divmod(k, s.width // BANK)
                    drain(s.f_v + k, B["v"][:, t, c * BANK:(c + 1) * BANK], ring(s.f_v + k))
                for i in range(HEADS + 3):
                    if i < HEADS:
                        act.wait_ge(sm_max, HEADS * s.index + i + 1)
                        for q in range(QT):
                            src = B["masked"][:, i % 2, q, :] if s.causal else psum[:, i % 4, q * TOK:(q + 1) * TOK]
                            nc.scalar.activation(B["p"][:, i % 4, q, :], src, ACT.Exp,
                                                 bias=s_max[:, i % 4, q:q + 1],
                                                 accum_out=s_sum[:, i % 4, q:q + 1]).then_inc(sm_exp, 1)
                    if i >= 3:
                        hd = i - 3
                        drain(s.f_t + hd, B["pT"][:, hd % 2, :, :],
                              ring(s.f_t + hd).rearrange("p (k q) -> p k q", k=QT))

            deviations(LN_X0)
            drain_hT(f_hT0)
            act.wait_ge(filled, 2)
            nc.scalar.activation(deviation[:, :], deviation[:, :], ACT.Copy).then_inc(drained, 1)
            act.wait_ge(q_zeroed, 1)
            act.wait_ge(q_bias_ready, 1)
            act.wait_ge(cols_loaded, 16)
            cross(X0, 0, 0, "xk", TINY * D0**-0.5)
            for k in range(8):
                drain(f_oT0 + k, oT0[:, k, :], ring(f_oT0 + k)[:, 0:TOK])
            deviations(LN_A0)
            drain_hT(f_hT1)
            drain(f_lat, latT[:, 0, :], ring(f_lat)[:, 0:TOK])
            small(A0)
            deviations(LN_F0)
            drain_hT(f_hT2)
            drain(f_p, lowT[0:64, :], ring(f_p)[0:64, 0:TOK])
            for k in range(FT):
                drain(f_g0 + k, gT0[:, k, :], ring(f_g0 + k)[:, 0:TOK], ACT.Gelu_apprx_tanh, bias=col("f1", k))
            drain(f_q, low2T[0:64, :], ring(f_q)[0:64, 0:TOK])
            deviations(LN_X1)
            drain_hT(f_hT3)
            for m in range(2):
                for c in range(CHUNKS):
                    act.wait_ge(filled, f_k1 + m * CHUNKS + c + 1)
                    nc.scalar.activation(key_parts[:, m, 0, c * BANK:(c + 1) * BANK], ring(f_k1 + m * CHUNKS + c),
                                         ACT.Identity, bias=col("ck", m)).then_inc(keys_high, 1)

            def split_queries(n, par):
                act.wait_ge(q_made, n + 1)
                act.sem_inc(act_passed)
                for j in range(2):
                    ins = nc.scalar.activation(q_stack[par][:, j, :], q_psum, ACT.Identity, scale=col("pick", j),
                                               bias=q_bias[:, bass.ds(n * 2 + (8 + j), 1)])
                ins.then_inc(q_high, 1)

            def weigh_pair(n, par, first, last):
                for g in range(GROUPS):
                    act.wait_ge(st_ready, n * GROUPS + (g + 1))
                    if not first or g >= 2:
                        act.wait_ge(probs_used, n * GROUPS + (g - 1))
                    nc.scalar.activation(probsT1[:, g % 2, :, :, :].rearrange("p i j q -> p i (j q)"),
                                         psum[:, 2 + 2 * (g % 2):4 + 2 * (g % 2), :], ACT.Exp).then_inc(st_exp, 1)
                    if g == 0 and not first:
                        act.wait_ge(probs_used, n * GROUPS)
                        act.wait_ge(folded, n - 1)
                        nc.scalar.activation(acc1_sb, psum[:, ACC, 0:TOK], ACT.Copy).then_inc(acc1_copied, 1)
                    if g == 0 and not last:
                        split_queries(n + 1, 1 - par)

            act.sem_inc(st_exp, 2)
            act.wait_ge(drained, f_v1)
            split_queries(0, 0)
            for k in range(KT // 2):
                drain(f_v1 + k, values[:, 2 * k:2 * k + 2, :], ring(f_v1 + k).rearrange("p (k n) -> p k n", k=2))
            weigh_pair(0, 0, True, False)
            with act.Fori(0, PAIRS // 2 - 1) as t:
                weigh_pair(t * 2 + 1, 1, False, False)
                weigh_pair(t * 2 + 2, 0, False, False)
            weigh_pair(PAIRS - 1, 1, False, True)
            act.wait_ge(probs_used, PAIRS * GROUPS)
            act.wait_ge(folded, PAIRS - 1)
            nc.scalar.activation(acc1_sb, psum[:, ACC, 0:TOK], ACT.Copy).then_inc(acc1_copied, 1)
            drain(f_oT1, hT[:, :, :], ring(f_oT1).rearrange("p (c t) -> p c t", c=CT))
            deviations(LN_CO)
            drain_hT(f_xT4)
            small(A1)
            deviations(LN_SO)
            drain_hT(f_xT5)
            for k in range(FT):
                drain(f_g1 + k, gT1[:, k, :], ring(f_g1 + k)[:, 0:TOK], ACT.Gelu, bias=col("fi", k))
            deviations(LN_FO)
            deviations(LN_A2)
            drain_hT(f_hT6)
            small(A2)
            deviations(LN_MOE)
            drain_hT(f_hT7)
            for f in range(f_hT7 + 1, f_moe):
                act.wait_ge(filled, f + 1)
                nc.scalar.activation(deviation[:, :], deviation[:, :], ACT.Copy).then_inc(drained, 1)
            act.wait_ge(sm_max, HEADS * 3 + 1)
            for q in range(QT):
                nc.scalar.activation(route[:, q, 1, :], route[:, q, 0, :], ACT.Exp, bias=s_max[:, 0, q:q + 1],
                                     accum_out=s_sum[:, 0, q:q + 1]).then_inc(route_exp, 1)

            def hidden(k, f, e):
                for t in range(FT):
                    act.wait_ge(filled, f + t + 1)
                    act.sem_inc(act_passed)
                    nc.scalar.activation(moe_hT[k][:, t, :], psum[:, 4 + t % 2, 0:TOK], ACT.Gelu_apprx_tanh,
                                         bias=col("m1", e * FT + t)).then_inc(drained, 1)

            hidden(0, f_moe, 0)
            with act.Fori(0, EXPERTS // 2 - 1) as i:
                hidden(1, i * (2 * FT) + (f_moe + FT), i * 2 + 1)
                hidden(0, i * (2 * FT) + (f_moe + 2 * FT), i * 2 + 2)
            hidden(1, f_moe + (EXPERTS - 1) * FT, EXPERTS - 1)

        @block.tensor
        def _(pe):
            mm, tr = nc.tensor.matmul, nc.tensor.transpose

            def fill(f):
                if not isinstance(f, int) or f >= 2:
                    pe.wait_ge(drained, f - 1)

            def transpose_tokens(f, src):
                fill(f)
                for c in range(CT):
                    for t in range(QT):
                        last = tr(ring(f)[:, c * TOK + t * P:c * TOK + (t + 1) * P], src[:, t, c * P:(c + 1) * P],
                                  ident[:, :])
                last.then_inc(filled, 1)

            def empty_fill(f):
                fill(f)
                tr(ring(f)[:, 0:P], ident[:, :], ident[:, :]).then_inc(filled, 1)

            def q_k(X, f, m, loads_before, first):
                pe.wait_ge(wqk_loaded, m * 32 + (loads_before + 1) * 32)
                for q in range(QT):
                    fill(f + q)
                    for c in range(CT):
                        last = mm(psum[:, 4 + q % 2, 0:P], wq_stage[:, c, :], hT[:, c, q * P:(q + 1) * P],
                                  start=c == 0, stop=c == CT - 1)
                    last.then_inc(filled, 1)
                for ch in range(CHUNKS):
                    fill(f + 2 + ch)
                    if first and ch % 2 == 0:
                        pe.wait_ge(ctx_loaded[ch // 2], 16)
                    for c in range(CT):
                        last = mm(psum[:, 4 + ch % 2, :], wk_stage[:, c, :], ctxT[:, c, ch * BANK:(ch + 1) * BANK],
                                  start=c == 0, stop=c == CT - 1)
                    last.then_inc(filled, 1)

            def value_fills(f, par=0):
                for k in range(KT // 2):
                    fill(f + k)
                    for i in range(2):
                        kt = 2 * k + i
                        for c in range(CT):
                            last = mm(psum[:, 4 + (par + k) % 2, i * 256:(i + 1) * 256], ctxT[:, c, kt * P:(kt + 1) * P],
                                      wv_stage[:, c, :], start=c == 0, stop=c == CT - 1)
                    last.then_inc(filled, 1)

            def scores(X, n0, g, u, new_keys=None):
                for c in range(CHUNKS):
                    if new_keys is not None:
                        pe.wait_ge(drained, new_keys + 2 + c + 1)
                    s = g * (4 * CHUNKS) + ((n0 + u) * CHUNKS + c)
                    if not isinstance(s, int) or s >= 2:
                        pe.wait_ge(scores_used, s - 1)
                    for j in range(2):
                        last = mm(psum[:, 2 * (c % 2) + j, :], qz_cross[:, j, (u % 2) * P:(u % 2 + 1) * P],
                                  keysT[:, c * BANK:(c + 1) * BANK], start=True, stop=True)
                    last.then_inc(scores_ready, 1)

            def back(n0, g, u):
                n = g * 4 + (n0 + u)
                pe.wait_ge(acc_copied, n + 1)
                if not isinstance(n, int) or n >= 1:
                    pe.wait_ge(normed, n)
                tr(psum[:, BACK, 0:P], acc_sb[:, :], ident[:, :]).then_inc(acc_back, 1)

            def weigh_values(X, n0, g, u, last):
                def transposes(t):
                    for j in range(2):
                        f = X.probs_fill(g, u, last, t, j)
                        fill(f)
                        if t == 0:
                            pe.wait_ge(exp_done, g * 8 + (2 * (n0 + u) + j + 1))
                        for i in range(4):
                            ins = tr(psum[:, 4 + j, i * P:(i + 1) * P],
                                     side[:, u % 2, j, (4 * t + i) * P:(4 * t + i + 1) * P], ident[:, :])
                        ins.then_inc(filled, 1)

                def products(t):
                    pe.wait_ge(drained, X.probs_fill(g, u, last, t, 1) + 1)
                    for i in range(4):
                        for j in range(2):
                            v = (2 * (u // 2) + j) * D0
                            kt = 4 * t + i
                            ins = mm(psum[64 * j:64 * j + D0, ACC, 0:P], values[:, kt, v:v + D0],
                                     probsT[:, t % 2, j, i, :], start=kt == 0, stop=kt == KT - 1)
                    if t == CHUNKS - 1:
                        ins.then_inc(pv_done, 1)

                transposes(0)
                if not isinstance(g, int) or g * 4 + n0 + u >= 1:
                    pe.wait_ge(acc_copied, g * 4 + (n0 + u))
                for t in range(CHUNKS):
                    if t + 1 < CHUNKS:
                        transposes(t + 1)
                    products(t)

            def cross(X, n0, loads_before):
                first_tile = X.f0 - 2 - CHUNKS

                def turn(g, last):
                    if True:
                        pe.wait_ge(wv_loaded, g * 16 + 16)
                        value_fills(X.fill(g, "v"))
                    else:
                        pe.wait_ge(values_copied, g + 1)
                    scores(X, n0, g, 1)
                    weigh_values(X, n0, g, 0, last)
                    if True:
                        q_k(X, X.fill(g, "qk"), g * 2 + 1, loads_before, False)
                        scores(X, n0, g, 2, X.fill(g, "qk"))
                    else:
                        scores(X, n0, g, 2)
                    back(n0, g, 0)
                    weigh_values(X, n0, g, 1, last)
                    scores(X, n0, g, 3)
                    back(n0, g, 1)
                    weigh_values(X, n0, g, 2, last)
                    if not last:
                        q_k(X, X.fill(g, "next"), g * 2 + 2, loads_before, False)
                        scores(X, n0, g, 4, X.fill(g, "next"))
                    back(n0, g, 2)
                    weigh_values(X, n0, g, 3, last)
                    back(n0, g, 3)

                q_k(X, first_tile, 0, loads_before, True)
                scores(X, n0, 0, 0, first_tile)
                with pe.Fori(0, X.TURNS - 1) as g:
                    turn(g, False)
                turn(X.TURNS - 1, True)

            def small(s, kvT):
                s, B, wq, wk, wv, wo = SMALL_OPS[s.index]
                for g in range(s.groups):
                    f = s.f_q + g
                    fill(f)
                    for c in range(s.q_tiles):
                        last = mm(ring(f)[:, 0:TOK], wq[:, c, g * P:(g + 1) * P], hT[:, c, :],
                                  start=c == 0, stop=c == s.q_tiles - 1)
                    last.then_inc(filled, 1)
                for g in range(s.groups):
                    f = s.f_k + g
                    fill(f)
                    for c in range(s.kv_tiles):
                        last = mm(ring(f)[:, 0:TOK], wk[:, c, g * P:(g + 1) * P], kvT[:, c, :],
                                  start=c == 0, stop=c == s.kv_tiles - 1)
                    last.then_inc(filled, 1)
                for k in range(QT * s.width // BANK):
                    t, n = divmod(k, s.width // BANK)
                    fill(s.f_v + k)
                    for c in range(s.kv_tiles):
                        last = mm(ring(s.f_v + k), kvT[:, c, t * P:(t + 1) * P], wv[:, c, n * BANK:(n + 1) * BANK],
                                  start=c == 0, stop=c == s.kv_tiles - 1)
                    last.then_inc(filled, 1)
                pe.wait_ge(drained, s.f_v)
                base = HEADS * s.index
                for i in range(HEADS + 4):
                    if i < HEADS:
                        if i >= 4:
                            if s.causal:
                                pe.wait_ge(sm_masked, i - 3)
                            else:
                                pe.wait_ge(sm_exp, 2 * (base + i - 3))
                        for q in range(QT):
                            last = mm(psum[:, i % 4, q * TOK:(q + 1) * TOK], B["qz"][:, i, q * P:(q + 1) * P],
                                      B["kT"][:, i // s.per, :], start=True, stop=True)
                        last.then_inc(sm_scores, 1)
                    if 3 <= i < HEADS + 3:
                        hd = i - 3
                        f = s.f_t + hd
                        fill(f)
                        pe.wait_ge(sm_norm, base + hd + 1)
                        for k in range(QT):
                            for q in range(QT):
                                last = tr(ring(f)[:, k * TOK + q * P:k * TOK + (q + 1) * P],
                                          B["p"][:, hd % 4, q, k * P:(k + 1) * P], ident[:, :])
                        last.then_inc(filled, 1)
                    if i >= 4:
                        hd = i - 4
                        g, j = divmod(hd, s.per)
                        pe.wait_ge(drained, s.f_t + hd + 1)
                        if j == 0 and g >= 2:
                            pe.wait_ge(sm_out, sum(SMALL_OPS[k][0].groups for k in range(s.index)) + g - 1)
                        for k in range(QT):
                            last = mm(psum[j * s.slot:(j + 1) * s.slot, ACC + g % 2, 0:TOK],
                                      B["v"][:, k, hd * s.slot:(hd + 1) * s.slot], B["pT"][:, hd % 2, k, :],
                                      start=k == 0, stop=k == QT - 1)
                        if j == s.per - 1:
                            last.then_inc(sm_pv, 1)
                pe.wait_ge(sm_out, sum(SMALL_OPS[k][0].groups for k in range(s.index + 1)))
                project([B["oT"][:, g, :] for g in range(s.groups)], [wo[:, g, :] for g in range(s.groups)],
                        {0: PROJ_A0, 1: PROJ_A1, 2: PROJ_A2}[s.index])

            def project(lhs, rhs, which):
                n = rhs[0].shape[-1]
                for q in range(QT):
                    for k in range(len(lhs)):
                        last = mm(psum[:, PROJ_BANK[which], q * n:(q + 1) * n], lhs[k][:, q * P:(q + 1) * P], rhs[k],
                                  start=k == 0, stop=k == len(lhs) - 1)
                last.then_inc(proj_done, 1)

            def gelu_fills(f0, w, rhs, n):
                for t in range(FT):
                    f = f0 + t
                    fill(f)
                    for c in range(n):
                        last = mm(ring(f)[:, 0:TOK], w(c, t), rhs(c), start=c == 0, stop=c == n - 1)
                    last.then_inc(filled, 1)

            pe.wait_ge(ident_loaded, 32)
            pe.wait_ge(ln_done, LN_X0 + 1)
            transpose_tokens(f_hT0, h)
            empty_fill(1)
            pe.wait_ge(drained, f_hT0 + 1)
            cross(X0, 0, 0)
            pe.wait_ge(normed, 16)
            for k in range(8):
                fill(f_oT0 + k)
                for t in range(QT):
                    last = tr(ring(f_oT0 + k)[:, t * P:(t + 1) * P], o_cross0[:, t, k * P:(k + 1) * P], ident[:, :])
                last.then_inc(filled, 1)
            pe.wait_ge(drained, f_oT0 + 8)
            pe.wait_ge(w_block0_o, 48)
            project([oT0[:, k, :] for k in range(8)], [xo_w[:, k, :] for k in range(8)], PROJ_X0)

            pe.wait_ge(ln_done, LN_A0 + 1)
            transpose_tokens(f_hT1, h)
            pe.wait_ge(drained, f_hT1 + 1)
            pe.wait_ge(w_block0, 16 * 8)
            fill(f_lat)
            for c in range(CT):
                last = mm(ring(f_lat)[:, 0:TOK], a0_down[:, c, :], hT[:, c, :], start=c == 0, stop=c == CT - 1)
            last.then_inc(filled, 1)
            pe.wait_ge(drained, f_lat + 1)
            small(A0, latT)

            pe.wait_ge(ln_done, LN_F0 + 1)
            transpose_tokens(f_hT2, h)
            pe.wait_ge(drained, f_hT2 + 1)
            fill(f_p)
            for c in range(CT):
                last = mm(ring(f_p)[0:64, 0:TOK], f_U1[:, c, :], hT[:, c, :], start=c == 0, stop=c == CT - 1)
            last.then_inc(filled, 1)
            pe.wait_ge(drained, f_p + 1)
            gelu_fills(f_g0, lambda c, t: f_V1[0:64, t * P:(t + 1) * P], lambda c: lowT[0:64, :], 1)
            fill(f_q)
            pe.wait_ge(drained, f_g0 + FT)
            for t in range(FT):
                last = mm(ring(f_q)[0:64, 0:TOK], f_U2[:, t, :], gT0[:, t, :], start=t == 0, stop=t == FT - 1)
            last.then_inc(filled, 1)
            pe.wait_ge(drained, f_q + 1)
            project([low2T[0:64, :]], [f_V2[0:64, :]], PROJ_F0)

            pe.wait_ge(ln_done, LN_X1 + 1)
            transpose_tokens(f_hT3, h)
            pe.wait_ge(drained, f_hT3 + 1)
            pe.wait_ge(k_loaded, 32)
            for m, w in enumerate((wk_stage, wq_stage)):
                for ch in range(CHUNKS):
                    f = f_k1 + m * CHUNKS + ch
                    fill(f)
                    for c in range(CT):
                        last = mm(ring(f), w[:, c, :], ctxT[:, c, ch * BANK:(ch + 1) * BANK],
                                  start=c == 0, stop=c == CT - 1)
                    last.then_inc(filled, 1)

            def make_queries(n, par, loads):
                pe.wait_ge(q_loaded[par], loads)
                if not isinstance(n, int) or n >= 1:
                    pe.wait_ge(q_ready, n)
                if not isinstance(n, int) or n >= 2:
                    pe.wait_ge(normed1, n - 2)
                for c in range(CT):
                    last = mm(q_psum, (wk_stage, wq_stage)[par][:, c, :], hT[:, c, :], start=c == 0, stop=c == CT - 1)
                last.then_inc(q_made, 1)

            def look(n, par, s, loads):
                chunk, q, j = s // 4, s // 2 % 2, s % 2
                if s == 0:
                    pe.wait_ge(q_ready, n + 1)
                if s % 8 == 0:
                    pe.wait_ge(stack_loaded[par][s // 8], loads)
                if s >= 2:
                    pe.wait_ge(look_used, n * STEPS + (s - 1))
                mm(psum[:, s % 2, :], q_stack[par][:, j, q * P:(q + 1) * P],
                   stack[par][:, chunk * BANK:(chunk + 1) * BANK], start=True, stop=True).then_inc(look_ready, 1)

            def turn_maxima(n):
                pe.wait_ge(neg_ready, n + 1)
                for j in range(2):
                    for q in range(QT):
                        last = tr(psum[0:2, 0, j * TOK + q * P:j * TOK + (q + 1) * P], neg_parts[:, q, j, :], ident[:, :])
                last.then_inc(neg_turned, 1)

            def transposed_scores(n, par, g, i):
                if i == 0:
                    if g == 0:
                        pe.wait_ge(neg_placed, n + 1)
                    pe.wait_ge(st_exp, n * GROUPS + (g + 1))
                kt = 2 * g + i
                ins = mm(psum[:, 2 + 2 * (g % 2) + i, :], stack[par][:, kt * P:(kt + 1) * P],
                         q_stack[par][:, :, :].rearrange("p j q -> p (j q)"), start=True, stop=True)
                if i == 1:
                    ins.then_inc(st_ready, 1)

            def sum_values(n, par, g):
                if g == 0:
                    pe.wait_ge(values_copied, n + 2)
                    if not isinstance(n, int) or n >= 1:
                        pe.wait_ge(acc1_copied, n)
                pe.wait_ge(st_exp, n * GROUPS + (g + 3))
                for i in range(2):
                    for j in range(2):
                        at = 32 * (2 * j + i)
                        ins = mm(psum[at:at + 32, ACC, 0:TOK], pair_values[:, par, 2 * g + i, j, :],
                                 probsT1[:, g % 2, i, j, :], start=g == 0, stop=g == GROUPS - 1,
                                 tile_position=(0, at))
                ins.then_inc(probs_used, 1)

            def fold_pair(n, queries):
                pe.wait_ge(acc1_copied, n + 1)
                pe.wait_ge(q_ready, queries)
                for q in range(QT):
                    ins = mm(psum[:, BACK, q * 64:(q + 1) * 64], acc1_sb[:, q * P:(q + 1) * P], fold[:, :],
                             start=True, stop=True)
                ins.then_inc(folded, 1)

            def attend_pair(n, par, first, last, loads):
                s = 0
                for g in range(GROUPS):
                    nxt = (n, par, g + 1) if g + 1 < GROUPS else (n + 1, 1 - par, 0)
                    ahead = not (last and g + 1 == GROUPS)
                    if g == 0 and not last:
                        make_queries(n + 1, 1 - par, loads * 16)
                    if g == GROUPS - 1 and not last:
                        turn_maxima(n + 1)
                    for i in range(2):
                        if ahead:
                            transposed_scores(*nxt, i)
                        if not last:
                            for _ in range((LOOKS[g] + 1 - i) // 2):
                                look(n + 1, 1 - par, s, loads * 48)
                                s += 1
                    if g == 4 and not first:
                        fold_pair(n - 1, PAIRS if last else n + 2)
                    sum_values(n, par, g)

            make_queries(0, 0, 16)
            pe.wait_ge(v_loaded1, 16)
            for k in range(KT // 2):
                f = f_v1 + k
                fill(f)
                for i in range(2):
                    kt = 2 * k + i
                    for c in range(CT):
                        last = mm(ring(f)[:, i * 256:(i + 1) * 256], ctxT[:, c, kt * P:(kt + 1) * P],
                                  wv_stage[:, c, :], start=c == 0, stop=c == CT - 1)
                last.then_inc(filled, 1)
                if k == 0:
                    pe.wait_ge(mask_placed, 64)
                for s in (2 * k, 2 * k + 1):
                    look(0, 0, s, 48)
            pe.wait_ge(drained, f_v1 + KT // 2)
            turn_maxima(0)
            for i in range(2):
                transposed_scores(0, 0, 0, i)
            attend_pair(0, 0, True, False, 1)
            with pe.Fori(0, PAIRS // 2 - 1) as t:
                attend_pair(t * 2 + 1, 1, False, False, t + 2)
                attend_pair(t * 2 + 2, 0, False, False, t + 2)
            attend_pair(PAIRS - 1, 1, False, True, 0)
            pe.wait_ge(normed1, PAIRS - 1)
            fold_pair(PAIRS - 1, PAIRS)
            pe.wait_ge(normed1, PAIRS)
            transpose_tokens(f_oT1, o_cross1)
            pe.wait_ge(drained, f_oT1 + 1)
            pe.wait_ge(w_co, 16)
            project([hT[:, c, :] for c in range(CT)], [co_w[:, c, :] for c in range(CT)], PROJ_C)

            pe.wait_ge(x_updated, UP_CO + 1)
            transpose_tokens(f_xT4, h)
            pe.wait_ge(drained, f_xT4 + 1)
            pe.wait_ge(w_block1, 16 * 6)
            small(A1, hT)

            pe.wait_ge(x_updated, UP_SO + 1)
            transpose_tokens(f_xT5, h)
            pe.wait_ge(drained, f_xT5 + 1)
            gelu_fills(f_g1, lambda c, t: fi_w[:, c, t * P:(t + 1) * P], lambda c: hT[:, c, :], CT)
            pe.wait_ge(drained, f_g1 + FT)
            project([gT1[:, t, :] for t in range(FT)], [fo_w[:, t, :] for t in range(FT)], PROJ_FI)

            pe.wait_ge(ln_done, LN_A2 + 1)
            transpose_tokens(f_hT6, h)
            pe.wait_ge(drained, f_hT6 + 1)
            pe.wait_ge(w_attn2, 16 * 5)
            small(A2, hT)

            pe.wait_ge(ln_done, LN_MOE + 1)
            transpose_tokens(f_hT7, h)
            for f in range(f_hT7 + 1, f_moe):
                empty_fill(f)
            pe.wait_ge(drained, f_hT7 + 1)
            project([hT[:, c, :] for c in range(CT)], [switch_w[:, c, :] for c in range(CT)], PROJ_ROUTE)

            def hidden(k, f, loads):
                pe.wait_ge(w1_loaded[k], loads)
                for t in range(FT):
                    fill(f + t)
                    for c in range(CT):
                        last = mm(psum[:, 4 + t % 2, 0:TOK], w1[k][:, c, t * P:(t + 1) * P], hT[:, c, :],
                                  start=c == 0, stop=c == CT - 1)
                    last.then_inc(filled, 1)

            def output(k, f, added, loads):
                pe.wait_ge(w2_loaded[k], loads)
                pe.wait_ge(drained, f)
                if added is not None:
                    pe.wait_ge(moe_added, added)
                for q in range(QT):
                    for t in range(FT):
                        last = mm(psum[:, ACC + k, q * CH:(q + 1) * CH], moe_hT[k][:, t, q * P:(q + 1) * P],
                                  w2[k][:, t, :], start=t == 0, stop=t == FT - 1)
                last.then_inc(moe_y, 1)

            hidden(0, f_moe, 16)
            pe.wait_ge(sm_max, HEADS * 3 + 1)
            with pe.Fori(0, EXPERTS // 2 - 1) as i:
                hidden(1, i * (2 * FT) + (f_moe + FT), i * 16 + 16)
                output(0, i * (2 * FT) + (f_moe + FT), i * 2 + 1, i * 16 + 16)
                hidden(0, i * (2 * FT) + (f_moe + 2 * FT), i * 16 + 32)
                output(1, i * (2 * FT) + (f_moe + 2 * FT), i * 2 + 2, i * 16 + 16)
            n = EXPERTS // 2 - 1
            hidden(1, f_moe + (EXPERTS - 1) * FT, 16 * n + 16)
            output(0, f_moe + (EXPERTS - 1) * FT, 2 * n + 1, 16 * n + 16)
            output(1, f_moe + EXPERTS * FT, 2 * n + 2, 16 * n + 16)

        @block.vector
        def _(dve):
            v = nc.vector
            links = [0]

            def link(ins):
                links[0] += 1
                ins.then_inc(link_sem, 1)
                dve.wait_ge(link_sem, links[0])

            def norm(src, dst, ln):
                for t in range(QT):
                    ins = v.bn_stats(stats[:, t, :], src[:, t, :])
                link(ins)
                for t in range(QT):
                    ins = v.bn_aggr(mean_var[:, t, :], stats[:, t, :])
                link(ins)
                v.tensor_scalar(mean_var[:, :, 1], mean_var[:, :, 1], EPS, None, ALU.add).then_inc(ln_var, 1)
                dve.wait_ge(ln_dev, ln + 1)
                link(v.reciprocal(deviation[:, :], deviation[:, :]))
                for t in range(QT):
                    ins = v.tensor_scalar(dst[:, t, :], src[:, t, :], mean_var[:, t, 0:1], deviation[:, t:t + 1],
                                          ALU.subtract, ALU.mult)
                ins.then_inc(ln_done, 1)
                dve.wait_ge(ln_done, ln + 1)

            def both(r):
                return r.unsqueeze(1).to_broadcast([P, QT, CH])

            def add_projection(which, bias, residual, dst, up):
                dve.wait_ge(proj_done, which + 1)
                y = psum[:, PROJ_BANK[which], :].rearrange("p (t c) -> p t c", t=QT)
                if bias is not None:
                    link(v.tensor_tensor(o_cross1[:, :, :], y, both(bias), ALU.add))
                    y = o_cross1[:, :, :]
                ins = v.tensor_tensor(dst, y, residual, ALU.add)
                if up is not None:
                    ins.then_inc(x_updated, 1)
                    dve.wait_ge(x_updated, up + 1)
                else:
                    link(ins)

            def affine(g, b, up):
                link(v.tensor_tensor(h[:, :, :], h[:, :, :], both(g), ALU.mult))
                v.tensor_tensor(h[:, :, :], h[:, :, :], both(b), ALU.add).then_inc(x_updated, 1)
                dve.wait_ge(x_updated, up + 1)

            def cross(X, n0, o, bias_row):
                per_unit = 3

                def unit(g, u):
                    q = u % 2
                    n = g * 4 + (n0 + u)
                    c0 = g * (4 * per_unit) + u * per_unit
                    for c in range(CHUNKS):
                        chunk = side[:, q, :, c * BANK:(c + 1) * BANK]
                        if c % 2 == 0:
                            dve.wait_ge(side_loaded[q][c // 2], g * 32 + 16 * (u // 2 + 1))
                        dve.wait_ge(scores_ready, g * (4 * CHUNKS) + ((n0 + u) * CHUNKS + c + 1))
                        v.tensor_tensor(chunk, psum[:, 2 * (c % 2):2 * (c % 2) + 2, :], chunk, ALU.mult
                                        ).then_inc(scores_used, 1)
                    dve.wait_ge(scores_used, g * (4 * CHUNKS) + (n0 + u + 1) * CHUNKS)
                    dve.wait_ge(mask_loaded[q], g * 32 + 16 * (u // 2 + 1))
                    dve.sem_inc(dve_passed)
                    for j in range(2):
                        ins = v.tensor_tensor_reduce(
                            out=side[:, q, j, :], in0=side[:, q, j, :], in1=masks[:, q, j, :], scale=1.0,
                            scalar=-3.0e38, op0=ALU.subtract, op1=ALU.max, accum_out=row_max[:, q, j:j + 1])
                    ins.then_inc(masked, 1)
                    dve.wait_ge(masked, n + 1)
                    v.tensor_scalar(no_key[:, 0, :], row_max[:, q, :], -0.5, 3.0e38, ALU.is_lt, ALU.mult
                                    ).then_inc(cross_link, 1)
                    dve.wait_ge(cross_link, c0 + 1)
                    v.tensor_scalar(no_key[:, 1, :], no_key[:, 0, :], 10.0, None, ALU.mult).then_inc(cross_link, 1)
                    dve.wait_ge(cross_link, c0 + 2)
                    v.tensor_tensor(no_key[:, 2, :], no_key[:, 1, :], no_key[:, 1, :], ALU.subtract
                                    ).then_inc(cross_link, 1)
                    dve.wait_ge(cross_link, c0 + 3)
                    v.scalar_tensor_tensor(out=exp_bias[:, q, :], in0=row_max[:, q, :], scalar=-1.0 / TINY,
                                           in1=no_key[:, 2, :], op0=ALU.mult, op1=ALU.add).then_inc(bias_ready, 1)

                def normalise(g, u):
                    n = g * 4 + (n0 + u)
                    dve.wait_ge(exp_done, g * 8 + 2 * (n0 + u + 1))
                    dve.wait_ge(acc_back, n + 1)
                    v.reciprocal(row_inv[:, u, :], row_sum[:, u, :]).then_inc(norm_link, 1)
                    dve.wait_ge(norm_link, n + 1)
                    for j in range(2):
                        at = (g * 4 + (2 * (u // 2) + j)) * D0
                        ins = v.scalar_tensor_tensor(
                            out=o[:, u % 2, bass.ds(at, D0)], in0=psum[:, BACK, 64 * j:64 * j + D0],
                            scalar=row_inv[:, u, j:j + 1], in1=bias_row[:, bass.ds(at, D0)],
                            op0=ALU.mult, op1=ALU.add)
                    ins.then_inc(normed, 1)

                def turn(g, last):
                    unit(g, 1)
                    unit(g, 2)
                    normalise(g, 0)
                    unit(g, 3)
                    normalise(g, 1)
                    if not last:
                        unit(g, 4)
                    normalise(g, 2)
                    normalise(g, 3)

                unit(0, 0)
                with dve.Fori(0, X.TURNS - 1) as g:
                    turn(g, False)
                turn(X.TURNS - 1, True)

            def small(s, v_bias):
                s, B = SMALL_OPS[s.index][:2]
                base = HEADS * s.index
                ot = sum(SMALL_OPS[k][0].groups for k in range(s.index))
                for i in range(HEADS + 4):
                    if i < HEADS:
                        dve.wait_ge(sm_scores, base + i + 1)
                        scores = psum[:, i % 4, :].rearrange("p (q k) -> p q k", q=QT)
                        if s.causal:
                            if i >= 2:
                                dve.wait_ge(sm_exp, 2 * (base + i - 1))
                            v.tensor_tensor(B["masked"][:, i % 2, :, :], scores, causal, ALU.add).then_inc(sm_masked, 1)
                            dve.wait_ge(sm_masked, i + 1)
                            scores = B["masked"][:, i % 2, :, :]
                        v.tensor_reduce(s_max[:, i % 4, :], scores, AX.X, ALU.max, negate=True).then_inc(sm_max, 1)
                    if 2 <= i < HEADS + 2:
                        hd = i - 2
                        dve.wait_ge(sm_exp, 2 * (base + hd + 1))
                        link(v.reciprocal(s_inv[:, hd % 4, :], s_sum[:, hd % 4, :]))
                        for q in range(QT):
                            ins = v.tensor_scalar(B["p"][:, hd % 4, q, :], B["p"][:, hd % 4, q, :],
                                                  s_inv[:, hd % 4, q:q + 1], None, ALU.mult)
                        ins.then_inc(sm_norm, 1)
                    hd = i - 4
                    if hd >= 0 and hd % s.per == s.per - 1:
                        g = hd // s.per
                        dve.wait_ge(sm_pv, ot + g + 1)
                        if v_bias:
                            v.tensor_scalar(B["oT"][:, g, :], psum[:, ACC + g % 2, 0:TOK], col(v_bias, g), None,
                                            ALU.add).then_inc(sm_out, 1)
                        else:
                            v.tensor_copy(B["oT"][:, g, :], psum[:, ACC + g % 2, 0:TOK]).then_inc(sm_out, 1)

            v.memset(acc_sb[:, :], 0.0)
            dve.wait_ge(cols_loaded, 16)
            for at, name, scale in ((0, "xq", TINY * D0**-0.5), (8, "cq", D1**-0.5), (24, "sq", D1**-0.5)):
                n = COLS[name][1]
                ins = v.tensor_scalar(q_bias[:, at:at + n], cols[:, COLS[name][0]:COLS[name][0] + n], scale, None, ALU.mult)
            ins.then_inc(q_bias_ready, 1)
            dve.wait_ge(x_loaded, 16)
            norm(x, h, LN_X0)
            dve.wait_ge(rows_loaded, 16)
            cross(X0, 0, o_cross0, row("xv"))
            add_projection(PROJ_X0, row("xo"), x[:, :, :], x[:, :, :], UP_X0)
            norm(x, h, LN_A0)
            dve.wait_ge(w_block0_o, 48)
            small(A0, None)
            add_projection(PROJ_A0, None, x[:, :, :], x[:, :, :], UP_A0)
            norm(x, h, LN_F0)
            add_projection(PROJ_F0, row("f2"), x[:, :, :], x[:, :, :], UP_F0)
            norm(x, h, LN_X1)
            dve.wait_ge(key_mask_loaded, 16)
            link(v.memset(ones[96:128, :], 1.0))
            for b in range(2):
                ins = v.tensor_copy(stack[b][96:128, :].rearrange("p (c k) -> p c k", c=CHUNKS),
                                    ones[96:128, :].unsqueeze(1).to_broadcast([32, CHUNKS, BANK]))
            link(ins)
            link(v.tensor_copy(mask_parts[:, 0, :], mask_raw))
            v.tensor_tensor(mask_parts[:, 1, :], mask_raw, mask_parts[:, 0, :], ALU.subtract).then_inc(mask_split, 1)
            for m in range(2):
                for c in range(CHUNKS):
                    dve.wait_ge(keys_high, m * CHUNKS + c + 1)
                    v.scalar_tensor_tensor(out=key_parts[:, m, 1, c * BANK:(c + 1) * BANK],
                                           in0=ring(f_k1 + m * CHUNKS + c), scalar=col("ck", m),
                                           in1=key_parts[:, m, 0, c * BANK:(c + 1) * BANK],
                                           op0=ALU.add, op1=ALU.subtract).then_inc(drained, 1)
                    if m == 0:
                        dve.wait_ge(drained, f_k1 + c + 1)
                        dve.sem_inc(keys_low)
            dve.wait_ge(drained, f_v1)
            dve.sem_inc(keys_low)

            PICK = COLS["pick"][0]
            LINKS = 3

            def pair_linked(ins, n, k):
                ins.then_inc(pair_link, 1)
                dve.wait_ge(pair_link, n * LINKS + k)

            def low_queries(n, par):
                dve.wait_ge(q_high, n + 1)
                dve.sem_inc(dve_passed)
                for j in range(2):
                    ins = v.tensor_scalar(q_whole[64:96, j, :], q_psum[64:96, :], cols[64:96, PICK + j:PICK + j + 1],
                                          q_bias[64:96, bass.ds(n * 2 + (8 + j), 1)], ALU.mult, ALU.add)
                pair_linked(ins, n, 1)
                v.tensor_tensor(q_stack[par][64:96, :, :], q_whole[64:96, :, :], q_stack[par][64:96, :, :],
                                ALU.subtract).then_inc(q_ready, 1)

            def maxima(n, steps):
                for s in steps:
                    dve.wait_ge(look_ready, n * STEPS + (s + 1))
                    v.tensor_reduce(pair_max[:, s // 2 % 2, s % 2, s // 4:s // 4 + 1], psum[:, s % 2, :], AX.X, ALU.max
                                    ).then_inc(look_used, 1)

            def place_maxima(n, par):
                dve.wait_ge(look_used, (n + 1) * STEPS)
                pair_linked(v.tensor_reduce(neg_max, pair_max, AX.X, ALU.max, negate=True), n, 2)
                pair_linked(v.tensor_copy(neg_high, neg_max), n, 3)
                v.tensor_copy(neg_parts[:, :, :, 0], neg_high)
                v.tensor_tensor(neg_parts[:, :, :, 1], neg_max, neg_high, ALU.subtract).then_inc(neg_ready, 1)
                dve.wait_ge(neg_turned, n + 1)
                v.tensor_copy(q_stack[par][96:98, :, :], psum[0:2, 0, :].rearrange("p (j q) -> p j q", j=2)
                              ).then_inc(neg_placed, 1)

            def normalise_pair(n):
                dve.wait_ge(folded, n + 1)
                back = psum[:, BACK, 0:QT * 64].rearrange("p (q j d) -> p q j d", q=QT, j=2)
                v.reciprocal(sum_inv.unsqueeze(3), back[:, :, :, D1:D1 + 1]).then_inc(norm1_link, 1)
                dve.wait_ge(norm1_link, n * 2 + 1)
                v.tensor_tensor(scaled, back[:, :, :, 0:D1], sum_inv.unsqueeze(3).to_broadcast([P, QT, 2, D1]), ALU.mult
                                ).then_inc(norm1_link, 1)
                dve.wait_ge(norm1_link, n * 2 + 2)
                at = ROWS["cv"][0]
                v.tensor_tensor(o_cross1[:, :, bass.ds(n * 2 * D1, 2 * D1)], scaled.rearrange("p q j d -> p q (j d)"),
                                rows[:, bass.ds(n * 2 * D1 + at, 2 * D1)].unsqueeze(1).to_broadcast([P, QT, 2 * D1]),
                                ALU.add).then_inc(normed1, 1)

            def attend_pair(n, par, first):
                low_queries(n + 1, 1 - par)
                before = sum(LOOKS[:6])
                maxima(n + 1, range(before))
                if not first:
                    normalise_pair(n - 1)
                maxima(n + 1, range(before, STEPS))
                place_maxima(n + 1, 1 - par)

            low_queries(0, 0)
            maxima(0, range(STEPS))
            place_maxima(0, 0)
            attend_pair(0, 0, True)
            with dve.Fori(0, PAIRS // 2 - 1) as t:
                attend_pair(t * 2 + 1, 1, False)
                attend_pair(t * 2 + 2, 0, False)
            normalise_pair(PAIRS - 2)
            normalise_pair(PAIRS - 1)
            add_projection(PROJ_C, row("co_b"), h[:, :, :], h[:, :, :], None)
            norm(h, h, LN_CO)
            affine(row("co_g"), row("co_be"), UP_CO)
            small(A1, "sv")
            add_projection(PROJ_A1, row("so_b"), h[:, :, :], h[:, :, :], None)
            norm(h, h, LN_SO)
            affine(row("so_g"), row("so_be"), UP_SO)
            dve.wait_ge(late_loaded, 16)
            add_projection(PROJ_FI, late_row("fo_b"), h[:, :, :], h[:, :, :], None)
            norm(h, h, LN_FO)
            affine(late_row("fo_g"), late_row("fo_be"), UP_FO)
            link(v.tensor_tensor(x[:, :, :], x[:, :, :], h[:, :, :], ALU.add))
            norm(x, h, LN_A2)
            small(A2, None)
            add_projection(PROJ_A2, late_row("lo"), x[:, :, :], x[:, :, :], UP_A2)
            norm(x, h, LN_MOE)
            dve.wait_ge(proj_done, PROJ_ROUTE + 1)
            logits = psum[:, PROJ_BANK[PROJ_ROUTE], 0:QT * EXPERTS].rearrange("p (q e) -> p q e", q=QT)
            link(v.tensor_tensor(route[:, :, 0, :], logits,
                                 row("switch").unsqueeze(1).to_broadcast([P, QT, EXPERTS]), ALU.add))
            v.tensor_reduce(s_max[:, 0, :], route[:, :, 0, :], AX.X, ALU.max, negate=True).then_inc(sm_max, 1)
            dve.wait_ge(sm_max, HEADS * 3 + 1)
            for q in range(QT):
                ins = v.tensor_scalar(route[:, q, 2, :], route[:, q, 0, :], s_max[:, 0, q:q + 1], 0.0,
                                      ALU.add, ALU.is_equal)
            link(ins)
            link(v.tensor_tensor(route[:, :, 3, :], route[:, :, 2, :],
                                 row("rank").unsqueeze(1).to_broadcast([P, QT, EXPERTS]), ALU.mult))
            link(v.tensor_reduce(s_inv[:, 1, :], route[:, :, 3, :], AX.X, ALU.max))
            for q in range(QT):
                ins = v.tensor_scalar(route[:, q, 4, :], route[:, q, 3, :], s_inv[:, 1, q:q + 1], None, ALU.is_equal)
            link(ins)
            dve.wait_ge(route_exp, QT)
            link(v.reciprocal(s_inv[:, 0, :], s_sum[:, 0, :]))
            for q in range(QT):
                ins = v.tensor_scalar(coef[:, q, :], route[:, q, 4, :], s_inv[:, 0, q:q + 1], None, ALU.mult)
            link(ins)
            dve.wait_ge(b2_loaded, 16)
            v.sem_inc(moe_added, 2)

            def add_expert(k, e, done):
                dve.wait_ge(moe_y, done)
                v.tensor_tensor(h[:, :, :], psum[:, ACC + k, :].rearrange("p (q c) -> p q c", q=QT),
                                b2_rows[:, bass.ds(e, 1), :].to_broadcast([P, QT, CH]), ALU.add).then_inc(moe_link, 1)
                dve.wait_ge(moe_link, done)
                for q in range(QT):
                    ins = v.scalar_tensor_tensor(out=x[:, q, :], in0=h[:, q, :], scalar=coef[:, q, bass.ds(e, 1)],
                                                 in1=x[:, q, :], op0=ALU.mult, op1=ALU.add)
                ins.then_inc(moe_added, 1)
                dve.wait_ge(moe_added, done + 2)

            with dve.Fori(0, EXPERTS // 2) as i:
                add_expert(0, i * 2, i * 2 + 1)
                add_expert(1, i * 2 + 1, i * 2 + 2)


def padded(w, d, slot):
    out = np.zeros((w.shape[0], w.shape[1] // d, slot), w.dtype)
    out[:, :, :d] = w.reshape(w.shape[0], -1, d)
    return out.reshape(w.shape[0], -1)


def tiles(b):
    return b.reshape(-1, P).T


def pairs_repeated(w):
    by_pair = w.reshape(w.shape[0], PAIRS, 1, 32)
    return np.concatenate([by_pair] * 3 + [np.zeros_like(by_pair)], 2).reshape(w.shape[0], -1)


def head_bias(b):
    out = np.zeros((P, HEADS), b.dtype)
    for head in range(HEADS):
        for block in range(3):
            at = 32 * block + D1 * (head % 2)
            out[at:at + D1, head] = b[head * D1:(head + 1) * D1]
    out[100:102] = 4.0
    return out


def picks():
    out = np.zeros((P, 2), np.float32)
    for j in range(2):
        for block in range(3):
            out[32 * block + D1 * j:32 * block + D1 * (j + 1), j] = D1**-0.5
    return out


def laid_out(i):
    g = {k: np.asarray(w) for k, w in i.items()}
    pads = lambda b, d: padded(b.reshape(1, -1), d, 32)[0]
    cols = {"xq": tiles(g["L0_xattn_bq"]), "xk": tiles(g["L0_xattn_bk"]), "f1": tiles(g["L0_ffn_b1"]),
            "cq": head_bias(g["L1_xattn_cq_b"]), "ck": tiles(g["L1_xattn_ck_b"]), "pick": picks(),
            "sq": tiles(pads(g["L1_xattn_sq_b"], D1)), "sk": tiles(pads(g["L1_xattn_sk_b"], D1)),
            "sv": tiles(pads(g["L1_xattn_sv_b"], D1)), "fi": tiles(g["L1_xattn_fi_b"]),
            "m1": tiles(g["L1_ffn_b1"].reshape(-1))}
    rows = {"xv": g["L0_xattn_bv"], "xo": g["L0_xattn_bo"], "f2": g["L0_ffn_b2"], "cv": g["L1_xattn_cv_b"],
            "co_b": g["L1_xattn_co_b"], "co_g": g["L1_xattn_co_g"], "co_be": g["L1_xattn_co_be"],
            "so_b": g["L1_xattn_so_b"], "so_g": g["L1_xattn_so_g"], "so_be": g["L1_xattn_so_be"],
            "switch": g["L1_ffn_switch_b"], "rank": np.arange(EXPERTS, 0, -1, dtype=np.float32)}
    causal = np.where(np.tril(np.ones((TOK, TOK), bool)), 0.0, -1e30).astype(np.float32)
    out = {
        "x": g["x"][0], "ctxT": g["ctx_1024"][0].T, "side": g["fside_Bx16xSxS2_0"][0],
        "mask": g["mask_Bx16xSxS2_bk1"][0], "key_mask": g["mask_Bx1x1xS2_ff0"].reshape(P, KEYS // P),
        "ident": np.eye(P, dtype=np.float32),
        "fold": np.kron(np.eye(2), np.tile(np.eye(32), (2, 1))).astype(np.float32), "causal": causal,
        "cols": np.concatenate([cols[k] for k in COLS], 1),
        "rows": np.concatenate([rows[k] for k in ROWS])[None],
        "late": np.concatenate([g["L1_xattn_fo_b"], g["L1_xattn_fo_g"], g["L1_xattn_fo_be"], g["L1_attn_bo"]])[None],
        "x_wq": g["L0_xattn_Wq"].T, "x_wk": g["L0_xattn_Wk"].T, "x_wv": g["L0_xattn_Wv"].T, "x_wo": g["L0_xattn_Wo"].T,
        "a_down": g["L0_attn_w_kv_down"], "a_kup": g["L0_attn_w_kv_up"][:, :1024], "a_vup": g["L0_attn_w_kv_up"][:, 1024:],
        "a_q": g["L0_attn_w_q"], "a_out": g["L0_attn_w_out"],
        "f_U1": g["L0_ffn_U1"], "f_V1": g["L0_ffn_V1"], "f_U2": g["L0_ffn_U2"], "f_V2": g["L0_ffn_V2"],
        "c_wq": pairs_repeated(g["L1_xattn_cq_w"]), "c_wk": g["L1_xattn_ck_w"],
        "c_wv": g["L1_xattn_cv_w"], "c_wo": g["L1_xattn_co_w"],
        "s_wq": padded(g["L1_xattn_sq_w"], D1, 32), "s_wk": padded(g["L1_xattn_sk_w"], D1, 32),
        "s_wv": padded(g["L1_xattn_sv_w"], D1, 32), "s_wo": padded(g["L1_xattn_so_w"].T, D1, 32).T,
        "fi_w": g["L1_xattn_fi_w"], "fo_w": g["L1_xattn_fo_w"],
        "l_wq": padded(g["L1_attn_Wq"].T, DL, 32), "l_wk": padded(g["L1_attn_Wk"].T, DL, 32),
        "l_wv": padded(g["L1_attn_Wv"].T, DL, 32), "l_wo": padded(g["L1_attn_Wo"], DL, 32).T,
        "switch_w": g["L1_ffn_switch_w"], "w1": g["L1_ffn_w1"], "w2": g["L1_ffn_w2"], "b2": g["L1_ffn_b2"].reshape(1, -1),
    }
    return {k: np.ascontiguousarray(w) for k, w in out.items()}


def kernel(**inputs):
    from concourse import bacc as _bacc
    from concourse import mybir as _mybir
    from concourse.bass_utils import run_bass_kernel_spmd as _run

    nc = _bacc.Bacc("TRN2", target_bir_lowering=False, num_devices=1)
    arrays, aps = {}, {}
    for name, w in laid_out(inputs).items():
        arrays[f"in_{name}"] = w
        aps[name] = nc.dram_tensor(f"in_{name}", w.shape, _mybir.dt.from_np(w.dtype), kind="ExternalInput").ap()
    aps["out"] = nc.dram_tensor("out_x", (TOK, CH), _mybir.dt.float32, kind="ExternalOutput").ap()
    program(nc, aps)
    r = _run(nc, [arrays], core_ids=[0])
    return r.results[0]["out_x"][None]
```

```python
from contextlib import ExitStack

import numpy as np

import concourse.bass as bass
from concourse import mybir

F32 = mybir.dt.float32
F32R = mybir.dt.float32r
U8 = mybir.dt.uint8
ALU = mybir.AluOpType
ACT = mybir.ActivationFunctionType
AX = mybir.AxisListType

P = 128
TOK = 256
QT = TOK // P
CH = 256
CT = CH // P
KEYS = 4096
HEADS = 16
FF = 1024
FT = FF // P
EXPERTS = 8
BANK = 512
CHUNKS = KEYS // BANK
KT = KEYS // P
PIECES = 4
PIECE = KEYS // PIECES
EPS = 1e-5

TINY = 2.0**-60
D0, D1, DL = 64, 16, 8

COLS, NCOLS = {}, 0
for _name, _n in (("xq", 8), ("xk", 8), ("f1", FT), ("cq", 16), ("ck", 2), ("pick", 2), ("sq", 4), ("sk", 4),
                  ("sv", 4), ("fi", FT), ("m1", EXPERTS * FT)):
    COLS[_name] = NCOLS, _n
    NCOLS += _n
ROWS, LATE = {}, {}
for _rows, _names in ((ROWS, (("xv", 1024), ("xo", CH), ("f2", CH), ("cv", CH))),
                      (LATE, (("co_b", CH), ("co_g", CH), ("co_be", CH), ("so_b", CH), ("so_g", CH),
                              ("so_be", CH), ("fo_b", CH), ("fo_g", CH), ("fo_be", CH), ("lo", CH),
                              ("switch", EXPERTS), ("rank", EXPERTS)))):
    _at = 0
    for _name, _n in _names:
        _rows[_name] = _at, _n
        _at += _n
NROWS, NLATE = (sum(n for _, n in r.values()) for r in (ROWS, LATE))


PAIRS = HEADS // 2
GROUPS = KT // 2
STEPS = QT * CHUNKS
EXPS_BEHIND = 2
EARLY_VALUES = 3
LOOK_BEHIND = 1
QUERIES_AT = 7
LOOKS = [2, 1, 1, 1, 1, 1, 1, 1, 2, 1, 1, 1, 1, 1, 0, 0]


class Weighted:

    TURNS = 4
    QK = 2 + CHUNKS

    def __init__(self, first_fill):
        self.first_fill = first_fill
        self.f0 = first_fill + self.QK
        v, t = KT // 2, 2 * CHUNKS
        self.at = {"v": 0, "t0": v, "qk": v + t}
        self.at["t1"] = self.at["qk"] + self.QK
        self.at["t2"] = self.at["t1"] + t
        self.at["next"] = self.at["t3_last"] = self.at["t2"] + t
        self.at["t3"] = self.at["next"] + self.QK
        self.per_turn = self.at["t3"] + t
        self.end_fill = self.f0 + (self.TURNS - 1) * self.per_turn + self.at["t3_last"] + t

    def fill(self, g, what, k=0):
        return g * self.per_turn + (self.f0 + self.at[what] + k)

    def probs_fill(self, g, u, last, t, j):
        return self.fill(g, f"t{u}" + ("_last" if last and u == 3 else ""), 2 * t + j)


class Small:

    def __init__(self, index, name, first_fill, slot, q_from, kv_from, causal, q_scale):
        self.index, self.name, self.slot = index, name, slot
        self.q_tiles, self.kv_tiles, self.causal, self.q_scale = q_from, kv_from, causal, q_scale
        self.per = P // slot
        self.groups = HEADS // self.per
        self.width = HEADS * slot
        self.f_q = first_fill
        self.f_k = self.f_q + self.groups
        self.f_v = self.f_k + self.groups
        self.f_t = self.f_v + QT * self.width // BANK
        self.end_fill = self.f_t + HEADS


def program(nc, a):
    ctx = ExitStack()
    with ctx:
        starts = {}

        def sbuf(name, shape):
            tensor = ctx.enter_context(nc.sbuf_tensor(name + "_sb", shape, F32))
            starts[name] = nc.sbuf_base - 4 * int(np.prod(shape[1:]))
            return tensor

        def rounded(name, arena, at, shape):
            return nc.alloc_sbuf_tensor_at(name + "_sb", [P, *shape], F32R, offset=starts[arena] + 4 * at)

        def sem(name):
            return ctx.enter_context(nc.semaphore(name))

        f_hT0 = 0
        X0 = Weighted(1 + 1)
        f_oT0 = X0.end_fill
        f_values = [f_oT0 + 8 + k for k in range(EARLY_VALUES)]
        f_hT1 = f_oT0 + 8 + EARLY_VALUES
        f_lat = f_hT1 + 1
        A0 = Small(0, "a0", f_lat + 1, 64, CT, 1, True, D0**-0.5)
        f_values += [A0.end_fill + k for k in range(EARLY_VALUES)]
        f_hT2 = A0.end_fill + EARLY_VALUES
        f_p = f_hT2 + 1
        f_g0 = f_p + 1
        f_q = f_g0 + FT
        f_values += [f_q + 1 + k for k in range(EARLY_VALUES)]
        f_hT3 = f_q + 1 + EARLY_VALUES
        f_k1 = [f_hT3 + 1]
        f_values += [f_k1[0] + CHUNKS + k for k in range(KT // 2 - 3 * EARLY_VALUES)]
        f_k1.append(f_values[-1] + 1)
        f_oT1 = f_k1[1] + CHUNKS
        f_xT4 = f_oT1 + 1
        A1 = Small(1, "a1", f_xT4 + 1, 32, CT, CT, False, D1**-0.5)
        f_xT5 = A1.end_fill
        f_g1 = f_xT5 + 1
        f_hT6 = f_g1 + FT
        A2 = Small(2, "a2", f_hT6 + 1, 32, 1, 1, False, 0.25)
        f_hT7 = A2.end_fill
        f_moe = f_hT7 + 1 + (f_hT7 + 1) % 2

        w_arena = sbuf("w_arena", [P, 4 * KEYS])
        c_arena = sbuf("c_arena", [P, 2 * KEYS])
        k_arena = sbuf("k_arena", [P, 2 * KEYS])
        v_arena = sbuf("v_arena", [P, KT * 256])
        m_arena = sbuf("m_arena", [P, 2 * KEYS // 4])
        o_arena = sbuf("o_arena", [P, 2048])
        p_arena = sbuf("p_arena", [P, 2048])
        rows = sbuf("rows", [P, NROWS])
        cols = sbuf("cols", [P, NCOLS])
        ident = sbuf("ident", [P, P])
        fold = sbuf("fold", [P, 64])
        x = sbuf("x", [P, QT, CH])
        hT = sbuf("hT", [P, CT, TOK])
        q_arena = sbuf("q_arena", [P, 4 * TOK])
        q_whole0 = sbuf("q_whole0", [P, TOK])
        wq_stage = sbuf("wq_stage", [P, CT, P])
        wk_stage = sbuf("wk_stage", [P, CT, P])
        wv_stage = sbuf("wv_stage", [P, CT, 256])
        acc_sb = sbuf("acc_sb", [P, P])
        row_max = sbuf("row_max", [P, 2])
        no_key = sbuf("no_key", [P, 3, 2])
        exp_bias = sbuf("exp_bias", [P, QT, 2])
        piece_sum = sbuf("piece_sum", [P, 4, 2, PIECES])
        row_sum = sbuf("row_sum", [P, 4, 2])
        row_inv = sbuf("row_inv", [P, 4, 2])
        stats = sbuf("stats", [P, QT, 6])
        mean_var = sbuf("mean_var", [P, QT, 2])
        deviation = sbuf("deviation", [P, QT])
        q_bias = sbuf("q_bias", [P, 28])
        s_max = sbuf("s_max", [P, 4, QT])
        s_sum = sbuf("s_sum", [P, 4, QT])
        s_top = sbuf("s_top", [P, 2, QT])
        s_inv = sbuf("s_inv", [P, 4, QT])
        route = sbuf("route", [P, QT, 5, EXPERTS])
        coef = sbuf("coef", [P, QT, EXPERTS])
        idle_out = sbuf("idle_out", [P, 16])

        def view(arena, at, *shape):
            n = int(np.prod(shape))
            ap = arena[:, at:at + n]
            if len(shape) == 1:
                return ap
            names = "abcd"[:len(shape)]
            return ap.rearrange(f"p ({' '.join(names)}) -> p {' '.join(names)}",
                                **{k: v for k, v in zip(names[1:], shape[1:])})

        side = view(w_arena, 0, QT, 2, KEYS)
        ctxT = view(c_arena, 0, CT, KEYS)
        keys_split = rounded("keys_split", "k_arena", 0, (2, KEYS))
        q_split = rounded("q_split", "q_arena", 0, (2, 2, TOK))
        values = view(v_arena, 0, KT, 256)
        masks = m_arena[:, :].bitcast(U8).rearrange("p (j k) -> p j k", j=2)
        o_cross0 = view(o_arena, 0, QT, 1024)
        probsT = view(p_arena, 0, 2, 2, 4, P)
        o_cross1, h = view(o_arena, 1024, QT, CH), view(o_arena, 1536, QT, CH)
        xo_w = view(k_arena, 0, FT, CH)
        oT0 = view(w_arena, 0, FT, TOK)
        a0_q, a0_k, a0_v = view(m_arena, 0, CT, 1024), view(k_arena, 3584, 1, 1024), view(k_arena, 4608, 1, 1024)
        a0_o, a0_down = view(p_arena, 0, 8, CH), view(k_arena, 5632, CT, P)
        f_U1, f_V1 = view(k_arena, 5888, CT, 64), view(k_arena, 6016, FF)
        f_U2, f_V2 = view(k_arena, 7040, FT, 64), view(k_arena, 2048, CH)
        causal = view(k_arena, 2304, QT, TOK)
        latT = view(k_arena, 2816, 1, TOK)
        lowT = view(k_arena, 3072, TOK)
        low2T = view(k_arena, 3328, TOK)
        gT0 = view(w_arena, 2048, FT, TOK)
        key_parts = view(w_arena, 0, 2, 2, KEYS).bitcast(F32R)
        stack = [rounded(f"stack{k}", "k_arena", k * KEYS, (KEYS,)) for k in range(2)]
        q_stack = [rounded(f"q_stack{k}", "q_arena", 2 * k * TOK, (2, TOK)) for k in range(2)]
        probsT1 = view(p_arena, 0, 2, 2, 2, TOK)
        pair_values = view(c_arena, 0, 2, KT, 2, 32)
        q_next = view(o_arena, 0, 2, TOK)
        q_rounded = view(m_arena, 0, 2, TOK).bitcast(F32R)
        q1_stage = view(m_arena, 512, CT, P)
        acc1_sb, scaled = view(o_arena, 512, TOK), view(o_arena, 768, QT, 2, D1)
        sum_inv, pair_max = view(o_arena, 832, QT, 2), view(o_arena, 840, QT, 2, CHUNKS)
        neg_max, neg_parts = view(o_arena, 872, QT, 2), view(o_arena, 880, QT, 2, 2)
        MASK_TILE = KEYS // P
        mask_raw, ones = view(o_arena, 900, MASK_TILE), view(o_arena, 1024, BANK)
        mask_parts = view(o_arena, 940, 2, MASK_TILE).bitcast(F32R)
        co_w = wv_stage[:, :, :]
        a1_q, a1_k, a1_v = (view(v_arena, 1024 * i, CT, 512) for i in range(3))
        a1_o, fi_w, fo_w = view(v_arena, 3072, 4, CH), view(v_arena, 4096, CT, FF), view(v_arena, 6144, FT, CH)
        a2_q, a2_k, a2_v = (view(w_arena, 8192 + 512 * i, 1, 512) for i in range(3))
        a2_o, switch_w = view(w_arena, 9728, 4, CH), view(w_arena, 10752, CT, EXPERTS)
        late = view(w_arena, 10768, NLATE)
        gT1 = view(w_arena, 14336, FT, TOK)
        x_offset = view(o_arena, 0, QT, CH)
        b2_rows = view(p_arena, 0, EXPERTS, CH)
        w1 = [view(w_arena, 4096 * k, CT, FF) for k in range(2)]
        w2 = [view(w_arena, 4096 * k + 2048, FT, CH) for k in range(2)]
        moe_hT = [view(c_arena, 2048 * k, FT, TOK) for k in range(2)]

        def small_views(arena, at, s):
            v = {}
            for name, shape in (("qz", (HEADS, TOK)), ("kT", (s.groups, TOK)), ("v", (QT, s.width)),
                                ("p", (4, QT, TOK)), ("oT", (s.groups, TOK)), ("pT", (2, QT, TOK)),
                                ("masked", (2, QT, TOK) if s.causal else (1, 1))):
                if at + int(np.prod(shape)) > arena.shape[1]:
                    arena, at = k_arena, 0
                v[name] = view(arena, at, *shape)
                at += int(np.prod(shape))
            return v

        B0 = small_views(w_arena, 0, A0)
        B1 = small_views(c_arena, 0, A1)
        B2 = small_views(c_arena, 0, A2)
        SMALL_OPS = {0: (A0, B0, a0_q, a0_k, a0_v, a0_o), 1: (A1, B1, a1_q, a1_k, a1_v, a1_o),
                     2: (A2, B2, a2_q, a2_k, a2_v, a2_o)}

        def row(name):
            at, n = (ROWS if name in ROWS else LATE)[name]
            return (rows if name in ROWS else late)[:, at:at + n]

        def col(name, i=0):
            return cols[:, bass.ds(COLS[name][0] + i, 1)]

        psum = ctx.enter_context(nc.psum_tensor("psum", [P, 8, BANK], F32))
        ACC, BACK = 6, 7
        LOOK_BANKS, FIRST_LOOK_BANKS = (0, 4), (0, 2)
        q_psum = psum[:, BACK, TOK:2 * TOK]

        def ring(f):
            return psum[:, 4 + f % 2, :]

        x_loaded, cols_loaded, ident_loaded, rows_loaded = map(sem, ("x_loaded", "cols_loaded", "ident_loaded", "rows_loaded"))
        ctx_loaded = [sem(f"ctx_loaded{i}") for i in range(PIECES)]
        side_loaded = [[sem(f"side_loaded{q}_{i}") for i in range(PIECES)] for q in range(QT)]
        mask_loaded = sem("mask_loaded")
        q_high0, q_low0, keys_high0 = sem("q_high0"), sem("q_low0"), sem("keys_high0")
        wqk_loaded, wv_loaded = sem("wqk_loaded"), sem("wv_loaded")
        w_block0, w_block0_o, w_co, w_block1, w_attn2, late_loaded, b2_loaded = map(
            sem, ("w_block0", "w_block0_o", "w_co", "w_block1", "w_attn2", "late_loaded", "b2_loaded"))
        key_mask_loaded = sem("key_mask_loaded")
        stack_loaded = [[sem(f"stack_loaded{b}_{i}") for i in range(PIECES)] for b in range(2)]
        k_loaded, v_loaded1 = sem("k_loaded"), sem("v_loaded1")
        q_loaded = [sem(f"q_loaded{k}") for k in range(2)]
        keys_high, keys_low, mask_split, mask_placed = map(
            sem, ("keys_high", "keys_low", "mask_split", "mask_placed"))
        q_made, q_whole, q_split_done, q_rounding, q_ready, look_ready, look_used = map(
            sem, ("q_made", "q_whole", "q_split_done", "q_rounding", "q_ready", "look_ready", "look_used"))
        neg_ready, neg_turned, neg_placed = sem("neg_ready"), sem("neg_turned"), sem("neg_placed")
        st_ready, st_exp, probs_used = map(sem, ("st_ready", "st_exp", "probs_used"))
        acc1_copied, folded, normed1 = sem("acc1_copied"), sem("folded"), sem("normed1")
        pair_link, norm1_link = sem("pair_link"), sem("norm1_link")
        w1_loaded, w2_loaded = ([sem(f"{w}_loaded{k}") for k in range(2)] for w in ("w1", "w2"))
        filled, drained = sem("filled"), sem("drained")
        scores_ready, scores_used = sem("scores_ready"), sem("scores_used")
        masked, bias_ready, exp_done = sem("masked"), sem("bias_ready"), sem("exp_done")
        pv_done, acc_copied, acc_back, normed = sem("pv_done"), sem("acc_copied"), sem("acc_back"), sem("normed")
        cross_link, norm_link, moe_link, link_sem = sem("cross_link"), sem("norm_link"), sem("moe_link"), sem("vector_link")
        values_copied = sem("values_copied")
        ln_var, ln_dev, ln_done = sem("ln_var"), sem("ln_dev"), sem("ln_done")
        q_zeroed = sem("q_zeroed")
        q_bias_ready = sem("q_bias_ready")
        proj_done, x_updated = sem("proj_done"), sem("x_updated")
        sm_scores, sm_masked, sm_max, sm_exp, sm_norm, sm_pv, sm_out = map(
            sem, ("sm_scores", "sm_masked", "sm_max", "sm_exp", "sm_norm", "sm_pv", "sm_out"))
        route_exp, moe_y, moe_added = sem("route_exp"), sem("moe_y"), sem("moe_added")
        out_stored = sem("out_stored")
        sp_passed, act_passed, dve_passed = sem("sp_passed"), sem("act_passed"), sem("dve_passed")

        (PROJ_X0, PROJ_A0, PROJ_F0, PROJ_C, PROJ_A1, PROJ_FI, PROJ_A2, PROJ_ROUTE) = range(8)
        PROJ_BANK = [ACC, BACK, BACK, ACC, BACK, ACC, BACK, ACC]
        LN_X0, LN_A0, LN_F0, LN_X1, LN_CO, LN_SO, LN_FO, LN_A2, LN_MOE = range(9)
        UP_X0, UP_A0, UP_F0, UP_CO, UP_SO, UP_FO, UP_A2 = range(7)

        block = ctx.enter_context(nc.Block())

        @block.sync
        def _(sp):
            def wait_then(sem_, value):
                sp.wait_ge(sem_, value)
                sp.sem_inc(sp_passed)

            def load_side(q, i, pair):
                sp.dma_start(side[:, q, :, i * PIECE:(i + 1) * PIECE],
                             a["side"][bass.ds(pair * 2, 2), q * P:(q + 1) * P, i * PIECE:(i + 1) * PIECE]
                             .rearrange("h p k -> p h k")).then_inc(side_loaded[q][i], 16)

            def load_mask(q, pair):
                sp.dma_start(masks, a["mask"][bass.ds(pair * 2, 2), q * P:(q + 1) * P, :]
                             .rearrange("h p k -> p h k")).then_inc(mask_loaded, 16)

            def load_qk(wq, wk, m):
                for stage, w in ((wq_stage, wq), (wk_stage, wk)):
                    sp.dma_start(stage[:, :, :], w.rearrange("(c p) n -> p c n", p=P)[:, :, bass.ds(m * P, P)]
                                 ).then_inc(wqk_loaded, 16)

            def load_wv(g):
                sp.dma_start(wv_stage[:, :, :], a["x_wv"].rearrange("(c p) n -> p c n", p=P)[:, :, bass.ds(g * 256, 256)]
                             ).then_inc(wv_loaded, 16)

            def load(dst, src, done):
                sp.dma_start(dst, src).then_inc(done, 16)

            def tiled(name):
                return a[name].rearrange("(c p) n -> p c n", p=P)

            load(x[:, :, :], a["x"].rearrange("(t p) c -> p t c", p=P), x_loaded)
            load(ident[:, :], a["ident"], ident_loaded)
            load(fold[:, :], a["fold"], ident_loaded)
            load(cols[:, :], a["cols"], cols_loaded)
            load_qk(a["x_wq"], a["x_wk"], 0)
            for i in range(PIECES):
                load(ctxT[:, :, i * PIECE:(i + 1) * PIECE], tiled("ctxT")[:, :, i * PIECE:(i + 1) * PIECE], ctx_loaded[i])
                load_side(0, i, 0)
            load_wv(0)
            load_mask(0, 0)
            load(rows[:, :], a["rows"].to_broadcast([P, NROWS]), rows_loaded)
            for i in range(PIECES):
                load_side(1, i, 0)

            def next_unit(g, u, last):
                wait_then(masked, g * 4 + (u + 1))
                if not last or u < 3:
                    load_mask((u + 1) % 2, g * 2 + (u + 1) // 2)
                if last and u >= 2:
                    return
                for i in range(PIECES):
                    wait_then(filled, X0.probs_fill(g, u, last, 2 * i + 1, 1) + 1)
                    load_side(u % 2, i, g * 2 + (u + 2) // 2)

            def turn(g, last):
                if not last:
                    wait_then(filled, X0.fill(g, "t0"))
                    load_wv(g + 1)
                next_unit(g, 0, last)
                if not last:
                    wait_then(filled, X0.fill(g, "qk", 2 + CHUNKS))
                    load_qk(a["x_wq"], a["x_wk"], g * 2 + 2)
                next_unit(g, 1, last)
                next_unit(g, 2, last)
                if not last:
                    wait_then(filled, X0.fill(g, "next", 2 + CHUNKS))
                    load_qk(a["x_wq"], a["x_wk"], g * 2 + 3)
                    next_unit(g, 3, last)

            wait_then(filled, X0.f0)
            load_qk(a["x_wq"], a["x_wk"], 1)
            with sp.Fori(0, X0.TURNS - 1) as g:
                turn(g, False)
            turn(X0.TURNS - 1, True)

            wait_then(masked, 16)
            load(xo_w, tiled("x_wo"), w_block0_o)
            load(f_V2[0:64, :], a["f_V2"], w_block0_o)
            load(causal, a["causal"].rearrange("(t p) k -> p t k", p=P), w_block0_o)
            wait_then(pv_done, 16)
            load(wv_stage[:, :, :], tiled("c_wv"), v_loaded1)
            for dst, name in ((a0_down, "a_down"), (a0_q, "a_q"), (a0_k, "a_kup"), (a0_v, "a_vup"),
                              (a0_o, "a_out"), (f_U1, "f_U1"), (f_U2, "f_U2")):
                load(dst, tiled(name), w_block0)
            load(f_V1[0:64, :], a["f_V1"], w_block0)
            load(wk_stage[:, :, :], tiled("c_wk")[:, :, 0:P], k_loaded)
            load(wq_stage[:, :, :], tiled("c_wk")[:, :, P:2 * P], k_loaded)
            wait_then(proj_done, PROJ_X0 + 1)
            load(mask_raw, a["key_mask"], key_mask_loaded)

            def load_q(n):
                at = n % PAIRS * P
                load(q1_stage if n == 1 else (wk_stage, wq_stage)[n % 2][:, :, :], tiled("c_wq")[:, :, at:at + P], q_loaded[n % 2])

            wait_then(filled, f_k1[0] + CHUNKS)
            load_q(0)
            wait_then(filled, f_values[-1] + 1)
            load(co_w, tiled("c_wo"), w_co)
            load_q(1)
            wait_then(filled, f_k1[1] + CHUNKS)
            for n in range(2, PAIRS + 1):
                wait_then(q_made, n - 1)
                load_q(n)
            for b in range(2):
                for i in range(PIECES):
                    wait_then(stack_loaded[b][i], 48 * (PAIRS // 2))
            load(late, a["late"].to_broadcast([P, NLATE]), late_loaded)
            for dst, name in ((a2_q, "l_wq"), (a2_k, "l_wk"), (a2_v, "l_wv"), (a2_o, "l_wo"),
                              (switch_w, "switch_w")):
                load(dst, tiled(name), w_attn2)
            wait_then(values_copied, PAIRS)
            for dst, name in ((a1_q, "s_wq"), (a1_k, "s_wk"), (a1_v, "s_wv"), (a1_o, "s_wo"),
                              (fi_w, "fi_w"), (fo_w, "fo_w")):
                load(dst, tiled(name), w_block1)

            def load_w1(k, e):
                sp.dma_start(w1[k], a["w1"][bass.ds(e, 1), :, :].rearrange("o (c p) f -> p (o c) f", p=P)
                             ).then_inc(w1_loaded[k], 16)

            def load_w2(k, e):
                sp.dma_start(w2[k], a["w2"][bass.ds(e, 1), :, :].rearrange("o (f p) c -> p (o f) c", p=P)
                             ).then_inc(w2_loaded[k], 16)

            for k in range(2):
                load_w1(k, k)
                load_w2(k, k)
            wait_then(normed1, PAIRS)
            load(b2_rows.rearrange("p e c -> p (e c)"), a["b2"].to_broadcast([P, EXPERTS * CH]), b2_loaded)
            with sp.Fori(0, EXPERTS // 2 - 1) as i:
                for k in range(2):
                    wait_then(filled, i * (2 * FT) + (f_moe + (k + 1) * FT))
                    load_w1(k, i * 2 + (k + 2))
                    wait_then(moe_y, i * 2 + (k + 1))
                    load_w2(k, i * 2 + (k + 2))
            wait_then(moe_added, EXPERTS + 2)
            sp.dma_start(a["out"].rearrange("(t p) c -> p t c", p=P), x[:, :, :]).then_inc(out_stored, 16)
            sp.wait_ge(out_stored, 16)

        @block.gpsimd
        def _(pool):
            pool.wait_ge(proj_done, PROJ_X0 + 1)
            nc.gpsimd.memset(B0["qz"], 0.0).then_inc(q_zeroed, 1)

            def load_stack(n, i):
                at = slice(32 * (n % 4), 32 * (n % 4 + 1))
                keys = slice(i * PIECE, (i + 1) * PIECE)
                for b, part in enumerate((0, 1, 0)):
                    pool.dma_start(stack[n % 2][32 * b:32 * (b + 1), keys], key_parts[at, n // 4, part, keys]
                                   ).then_inc(stack_loaded[n % 2][i], 16)

            for i in range(PIECES):
                pool.wait_ge(keys_low, 2 * i + 2)
                load_stack(0, i)
            pool.wait_ge(mask_split, 1)
            for b in range(2):
                for part in range(2):
                    pool.dma_start(stack[b][100 + part:101 + part, :].rearrange("o (p k) -> o p k", p=P),
                                   mask_parts[:, part, :]).then_inc(mask_placed, 16)
            for i in range(PIECES):
                load_stack(1, i)
            pool.wait_ge(filled, f_oT1)
            for n in range(PAIRS):
                if n < 2:
                    nc.gpsimd.memset(pair_values[:, n, :, :, D1 + 1:32], 0.0)
                    nc.gpsimd.memset(pair_values[:, n, :, :, D1:D1 + 1], 1.0)
                if n >= 2:
                    if n == PAIRS // 2:
                        pool.wait_ge(keys_low, CHUNKS + 1)
                    for i in range(PIECES):
                        pool.wait_ge(st_ready, KT * (n - 2) + KT // PIECES * (i + 1))
                        load_stack(n, i)
                    pool.wait_ge(probs_used, (n - 1) * GROUPS)
                nc.gpsimd.tensor_copy(pair_values[:, n % 2, :, :, 0:D1],
                                      values[:, :, n * 2 * D1:(n + 1) * 2 * D1].rearrange("p k (j d) -> p k j d", j=2)
                                      ).then_inc(values_copied, 1)
            pool.wait_ge(normed1, PAIRS)
            nc.gpsimd.memset(B1["qz"], 0.0).then_inc(q_zeroed, 1)

        @block.scalar
        def _(act):
            def drain(f, dst, src=None, func=ACT.Copy, **kw):
                act.wait_ge(filled, f + 1)
                nc.scalar.activation(dst, src, func, **kw).then_inc(drained, 1)

            def drain_hT(f):
                drain(f, hT[:, :, :], ring(f).rearrange("p (c t) -> p c t", c=CT))

            idle_columns = iter(range(16))

            def bring(func):
                at = next(idle_columns)
                nc.scalar.activation(idle_out[:, at:at + 1], ident[:, 0:1], func)

            def deviations(ln):
                if ln > 0:
                    bring(ACT.Sqrt)
                act.wait_ge(ln_var, ln + 1)
                nc.scalar.activation(deviation[:, :], mean_var[:, :, 1], ACT.Sqrt).then_inc(ln_dev, 1)

            def q_k(f, m, beside=None):
                for q in range(QT):
                    act.wait_ge(filled, f + q + 1)
                    act.sem_inc(act_passed)
                    nc.scalar.activation(q_whole0[:, q * P:(q + 1) * P], psum[:, 4 + q % 2, 0:P], ACT.Identity,
                                         bias=q_bias[:, bass.ds(m, 1)], scale=TINY * D0**-0.5).then_inc(drained, 1)
                act.wait_ge(drained, f + 2)
                for j in range(2):
                    own = slice(64 * j, 64 * (j + 1))
                    for part in range(2):
                        to = own if part == 0 else slice(64 * (1 - j), 64 * (2 - j))
                        ins = nc.scalar.activation(q_split[to, j, part, :], q_whole0[own, :], ACT.Copy)
                ins.then_inc(q_high0, 1)
                for c in range(CHUNKS + EXPS_BEHIND):
                    if c < CHUNKS:
                        act.wait_ge(filled, f + 2 + c + 1)
                        act.sem_inc(act_passed)
                        for j in range(2):
                            own = slice(64 * j, 64 * (j + 1))
                            nc.scalar.activation(keys_split[own, j, c * BANK:(c + 1) * BANK], psum[own, 4 + c % 2, :],
                                                 ACT.Identity, bias=cols[own, bass.ds(m + COLS["xk"][0], 1)]
                                                 ).then_inc(keys_high0, 1)
                    if beside is not None and c == EXPS_BEHIND:
                        act.wait_ge(bias_ready, beside[0] * 4 + (beside[1] + 1))
                        act.sem_inc(act_passed)
                    if beside is not None and c >= EXPS_BEHIND:
                        exp_piece(beside[1], (c - EXPS_BEHIND) // 2, (c - EXPS_BEHIND) % 2)
                act.wait_ge(drained, f + 2 + CHUNKS)

            def exp_piece(u, i, j):
                keys = slice(i * PIECE, (i + 1) * PIECE)
                nc.scalar.activation(side[:, u % 2, j, keys], side[:, u % 2, j, keys], ACT.Exp,
                                     bias=exp_bias[:, u % 2, j:j + 1], scale=1.0 / TINY,
                                     accum_out=piece_sum[:, u, j, i:i + 1]).then_inc(exp_done, 1)

            def exps(g, u, ks=range(2 * PIECES)):
                for k in ks:
                    if k == 0:
                        act.wait_ge(bias_ready, g * 4 + (u + 1))
                    exp_piece(u, k // 2, k % 2)

            def probs(g, u, last, beside=None, own=False):
                for t in range(CHUNKS):
                    if own and t % 2 == 0:
                        exps(g, u, (t, t + 1))
                    for j in range(2):
                        f = X0.probs_fill(g, u, last, t, j)
                        act.wait_ge(filled, f + 1)
                        nc.scalar.activation(probsT[:, t % 2, j, :, :],
                                             psum[:, 4 + j, :].rearrange("p (i q) -> p i q", i=4),
                                             ACT.Copy).then_inc(drained, 1)
                    if beside is not None and t >= CHUNKS // 2:
                        exps(g, beside, (t - CHUNKS // 2,))
                act.wait_ge(pv_done, g * 4 + (u + 1))
                nc.scalar.activation(acc_sb[:, :], psum[:, ACC, 0:P], ACT.Copy).then_inc(acc_copied, 1)

            def cross(X):
                def turn(g, last):
                    for k in range(KT // 2):
                        act.wait_ge(filled, X.fill(g, "v", k) + 1)
                        nc.scalar.activation(values[:, 2 * k:2 * k + 2, :], psum[:, 4 + k % 2, :]
                                             .rearrange("p (k n) -> p k n", k=2), ACT.Copy).then_inc(drained, 1)
                        if k >= KT // 4:
                            exps(g, 0, (k - KT // 4,))
                    probs(g, 0, last)
                    q_k(X.fill(g, "qk"), g * 2 + 1, (g, 1))
                    probs(g, 1, last, 2)
                    exps(g, 2, range(PIECES, 2 * PIECES))
                    probs(g, 2, last)
                    if not last:
                        q_k(X.fill(g, "next"), g * 2 + 2, (g, 3))
                    probs(g, 3, last, own=last)

                q_k(X.first_fill, 0)
                with act.Fori(0, X.TURNS - 1) as g:
                    turn(g, False)
                turn(X.TURNS - 1, True)

            def small(s):
                s, B = SMALL_OPS[s.index][:2]
                bring(ACT.Exp)
                act.wait_ge(q_zeroed, 1 if s.index == 0 else 2)
                for g in range(s.groups):
                    f = s.f_q + g
                    act.wait_ge(filled, f + 1)
                    for j in range(s.per):
                        sl = slice(j * s.slot, (j + 1) * s.slot)
                        bias = dict(bias=q_bias[sl, 24 + g:25 + g]) if s.index == 1 else {}
                        last = nc.scalar.activation(B["qz"][sl, g * s.per + j, :], ring(f)[sl, 0:TOK],
                                                    ACT.Identity if bias else ACT.Copy, scale=s.q_scale, **bias)
                    last.then_inc(drained, 1)
                for g in range(s.groups):
                    f = s.f_k + g
                    if s.index == 1:
                        drain(f, B["kT"][:, g, :], ring(f)[:, 0:TOK], ACT.Identity, bias=col("sk", g))
                    else:
                        drain(f, B["kT"][:, g, :], ring(f)[:, 0:TOK])
                for k in range(QT * s.width // BANK):
                    t, c = divmod(k, s.width // BANK)
                    drain(s.f_v + k, B["v"][:, t, c * BANK:(c + 1) * BANK], ring(s.f_v + k))
                for i in range(HEADS + 3):
                    if i < HEADS:
                        act.wait_ge(sm_max, HEADS * s.index + i + 1)
                        for q in range(QT):
                            src = B["masked"][:, i % 2, q, :] if s.causal else psum[:, i % 4, q * TOK:(q + 1) * TOK]
                            nc.scalar.activation(B["p"][:, i % 4, q, :], src, ACT.Exp,
                                                 bias=s_max[:, i % 4, q:q + 1],
                                                 accum_out=s_sum[:, i % 4, q:q + 1]).then_inc(sm_exp, 1)
                    if i >= 3:
                        hd = i - 3
                        drain(s.f_t + hd, B["pT"][:, hd % 2, :, :],
                              ring(s.f_t + hd).rearrange("p (k q) -> p k q", k=QT))

            def drain_value(k):
                drain(f_values[k], values[:, 2 * k:2 * k + 2, :], ring(f_values[k]).rearrange("p (k n) -> p k n", k=2))

            def layer_norm_beside(ln, k):
                drain_value(k)
                deviations(ln)
                for i in range(1, EARLY_VALUES):
                    drain_value(k + i)

            deviations(LN_X0)
            act.wait_ge(ident_loaded, 32)
            drain_hT(f_hT0)
            act.wait_ge(filled, 2)
            nc.scalar.activation(deviation[:, :], deviation[:, :], ACT.Copy).then_inc(drained, 1)
            act.wait_ge(q_bias_ready, 1)
            act.wait_ge(cols_loaded, 16)
            cross(X0)
            for k in range(8):
                drain(f_oT0 + k, oT0[:, k, :], ring(f_oT0 + k)[:, 0:TOK])
            layer_norm_beside(LN_A0, 0)
            drain_hT(f_hT1)
            drain(f_lat, latT[:, 0, :], ring(f_lat)[:, 0:TOK])
            small(A0)
            layer_norm_beside(LN_F0, EARLY_VALUES)
            drain_hT(f_hT2)
            drain(f_p, lowT[0:64, :], ring(f_p)[0:64, 0:TOK])
            bring(ACT.Gelu_apprx_tanh)
            for k in range(FT):
                drain(f_g0 + k, gT0[:, k, :], ring(f_g0 + k)[:, 0:TOK], ACT.Gelu_apprx_tanh, bias=col("f1", k))
            drain(f_q, low2T[0:64, :], ring(f_q)[0:64, 0:TOK])
            layer_norm_beside(LN_X1, 2 * EARLY_VALUES)
            drain_hT(f_hT3)

            def high_keys(m):
                for c in range(CHUNKS):
                    if m == 1 and c == 3:
                        whole_queries(1)
                    if m == 1 and c == 5:
                        place_queries(1, 1)
                    act.wait_ge(filled, f_k1[m] + c + 1)
                    nc.scalar.activation(key_parts[:, m, 0, c * BANK:(c + 1) * BANK], ring(f_k1[m] + c),
                                         ACT.Identity, bias=col("ck", m)).then_inc(keys_high, 1)
                act.wait_ge(drained, f_k1[m] + CHUNKS)

            def whole_queries(n):
                act.wait_ge(q_made, n + 1)
                if not isinstance(n, int) or n >= 1:
                    act.wait_ge(q_ready, n)
                act.sem_inc(act_passed)
                for j in range(2):
                    ins = nc.scalar.activation(q_next[:, j, :], q_psum, ACT.Identity, scale=col("pick", j),
                                               bias=q_bias[:, bass.ds(n * 2 + (8 + j), 1)])
                ins.then_inc(q_whole, 1)
                act.wait_ge(q_whole, n + 1)
                nc.scalar.activation(q_rounded[64:96, :, :], q_next[64:96, :, :], ACT.Copy).then_inc(q_rounding, 1)

            def place_queries(n, par):
                act.wait_ge(q_split_done, n + 1)
                nc.scalar.activation(q_stack[par][:, :, :], q_next, ACT.Copy).then_inc(q_ready, 1)

            def weigh_pair(n, par, first, last):
                for g in range(GROUPS):
                    for i in range(2):
                        act.wait_ge(st_ready, n * KT + (2 * g + i + 1))
                        if g == GROUPS - 1 and i == 1 and not last:
                            act.sem_inc(act_passed)
                            place_queries(n + 2, par)
                        if i == 0 and (not first or g >= 2):
                            act.wait_ge(probs_used, n * GROUPS + (g - 1))
                        nc.scalar.activation(probsT1[:, g % 2, i, :, :].rearrange("p j q -> p (j q)"),
                                             psum[:, 2 + i, :], ACT.Exp).then_inc(st_exp, 1)
                    if g == 0 and not first:
                        act.wait_ge(probs_used, n * GROUPS)
                        act.wait_ge(folded, n - 1)
                        nc.scalar.activation(acc1_sb, psum[:, ACC, 0:TOK], ACT.Copy).then_inc(acc1_copied, 1)
                    if g == QUERIES_AT and not last:
                        whole_queries(n + 2)

            act.sem_inc(st_exp, 2)
            high_keys(0)
            for k in range(3 * EARLY_VALUES, KT // 2):
                drain_value(k)
            whole_queries(0)
            place_queries(0, 0)
            high_keys(1)
            weigh_pair(0, 0, True, False)
            with act.Fori(0, PAIRS // 2 - 1) as t:
                weigh_pair(t * 2 + 1, 1, False, False)
                weigh_pair(t * 2 + 2, 0, False, False)
            weigh_pair(PAIRS - 1, 1, False, True)
            act.wait_ge(probs_used, PAIRS * GROUPS)
            act.wait_ge(folded, PAIRS - 1)
            nc.scalar.activation(acc1_sb, psum[:, ACC, 0:TOK], ACT.Copy).then_inc(acc1_copied, 1)
            drain(f_oT1, hT[:, :, :], ring(f_oT1).rearrange("p (c t) -> p c t", c=CT))
            deviations(LN_CO)
            drain_hT(f_xT4)
            small(A1)
            deviations(LN_SO)
            drain_hT(f_xT5)
            bring(ACT.Gelu)
            for k in range(FT):
                drain(f_g1 + k, gT1[:, k, :], ring(f_g1 + k)[:, 0:TOK], ACT.Gelu, bias=col("fi", k))
            deviations(LN_FO)
            deviations(LN_A2)
            drain_hT(f_hT6)
            small(A2)
            deviations(LN_MOE)
            drain_hT(f_hT7)
            for f in range(f_hT7 + 1, f_moe):
                act.wait_ge(filled, f + 1)
                nc.scalar.activation(deviation[:, :], deviation[:, :], ACT.Copy).then_inc(drained, 1)
            bring(ACT.Exp)
            act.wait_ge(sm_max, HEADS * 3 + 1)
            for q in range(QT):
                nc.scalar.activation(route[:, q, 1, :], route[:, q, 0, :], ACT.Exp, bias=s_max[:, 0, q:q + 1],
                                     accum_out=s_sum[:, 0, q:q + 1]).then_inc(route_exp, 1)

            def hidden(k, f, e):
                for t in range(FT):
                    act.wait_ge(filled, f + t + 1)
                    act.sem_inc(act_passed)
                    nc.scalar.activation(moe_hT[k][:, t, :], psum[:, 4 + t % 2, 0:TOK], ACT.Gelu_apprx_tanh,
                                         bias=col("m1", e * FT + t)).then_inc(drained, 1)

            hidden(0, f_moe, 0)
            with act.Fori(0, EXPERTS // 2 - 1) as i:
                hidden(1, i * (2 * FT) + (f_moe + FT), i * 2 + 1)
                hidden(0, i * (2 * FT) + (f_moe + 2 * FT), i * 2 + 2)
            hidden(1, f_moe + (EXPERTS - 1) * FT, EXPERTS - 1)

        @block.tensor
        def _(pe):
            mm, tr = nc.tensor.matmul, nc.tensor.transpose

            def fill(f):
                if not isinstance(f, int) or f >= 2:
                    pe.wait_ge(drained, f - 1)

            def transpose_tokens(f, src):
                fill(f)
                for c in range(CT):
                    for t in range(QT):
                        last = tr(ring(f)[:, c * TOK + t * P:c * TOK + (t + 1) * P], src[:, t, c * P:(c + 1) * P],
                                  ident[:, :])
                last.then_inc(filled, 1)

            def empty_fill(f):
                fill(f)
                tr(ring(f)[:, 0:P], ident[:, :], ident[:, :]).then_inc(filled, 1)

            def q_k_scores(f, m, g, u):
                pe.wait_ge(wqk_loaded, m * 32 + 32)
                for q in range(QT):
                    fill(f + q)
                    for c in range(CT):
                        last = mm(psum[:, 4 + q % 2, 0:P], wq_stage[:, c, :], hT[:, c, q * P:(q + 1) * P],
                                  start=c == 0, stop=c == CT - 1)
                    last.then_inc(filled, 1)
                for ch in range(CHUNKS):
                    fill(f + 2 + ch)
                    if isinstance(m, int) and m == 0 and ch % 2 == 0:
                        pe.wait_ge(ctx_loaded[ch // 2], 16)
                    for c in range(CT):
                        last = mm(psum[:, 4 + ch % 2, :], wk_stage[:, c, :], ctxT[:, c, ch * BANK:(ch + 1) * BANK],
                                  start=c == 0, stop=c == CT - 1)
                    last.then_inc(filled, 1)
                    if ch == 0:
                        pe.wait_ge(q_low0, m + 1)
                    else:
                        pe.wait_ge(drained, f + 2 + ch)
                        score_chunk(g, u, ch - 1)
                pe.wait_ge(drained, f + 2 + CHUNKS)
                score_chunk(g, u, CHUNKS - 1)

            def value_fill(f, k):
                fill(f + k)
                for i in range(2):
                    kt = 2 * k + i
                    for c in range(CT):
                        last = mm(psum[:, 4 + k % 2, i * 256:(i + 1) * 256], ctxT[:, c, kt * P:(kt + 1) * P],
                                  wv_stage[:, c, :], start=c == 0, stop=c == CT - 1)
                last.then_inc(filled, 1)

            def score_chunk(g, u, c):
                s = g * (4 * CHUNKS) + (u * CHUNKS + c)
                if not isinstance(s, int) or s >= 2:
                    pe.wait_ge(scores_used, s - 1)
                for j in range(2):
                    for part in range(2):
                        last = mm(psum[:, 2 * (c % 2) + j, :], q_split[:, j, part, (u % 2) * P:(u % 2 + 1) * P],
                                  keys_split[:, j, c * BANK:(c + 1) * BANK], start=part == 0, stop=part == 1)
                last.then_inc(scores_ready, 1)

            def back(g, u):
                n = g * 4 + u
                pe.wait_ge(acc_copied, n + 1)
                if not isinstance(n, int) or n >= 1:
                    pe.wait_ge(normed, n)
                tr(psum[:, BACK, 0:P], acc_sb[:, :], ident[:, :]).then_inc(acc_back, 1)

            def weigh_values(g, u, last, beside=()):
                def transposes(t):
                    for j in range(2):
                        f = X0.probs_fill(g, u, last, t, j)
                        fill(f)
                        if t % 2 == 0:
                            pe.wait_ge(exp_done, g * (8 * PIECES) + (2 * PIECES * u + t + j + 1))
                        for i in range(4):
                            ins = tr(psum[:, 4 + j, i * P:(i + 1) * P],
                                     side[:, u % 2, j, (4 * t + i) * P:(4 * t + i + 1) * P], ident[:, :])
                        ins.then_inc(filled, 1)

                def products(t):
                    pe.wait_ge(drained, X0.probs_fill(g, u, last, t, 1) + 1)
                    for i in range(4):
                        for j in range(2):
                            v = (2 * (u // 2) + j) * D0
                            kt = 4 * t + i
                            ins = mm(psum[64 * j:64 * j + D0, ACC, 0:P], values[:, kt, v:v + D0],
                                     probsT[:, t % 2, j, i, :], start=kt == 0, stop=kt == KT - 1)
                    if t == CHUNKS - 1:
                        ins.then_inc(pv_done, 1)

                transposes(0)
                if not isinstance(g, int) or g * 4 + u >= 1:
                    pe.wait_ge(acc_copied, g * 4 + u)
                for t in range(CHUNKS):
                    if t + 1 < CHUNKS:
                        transposes(t + 1)
                    products(t)
                    if CHUNKS // 2 <= t < CHUNKS // 2 + len(beside):
                        score_chunk(g, u + 2, beside[t - CHUNKS // 2])

            def cross(X):
                def turn(g, last):
                    pe.wait_ge(wv_loaded, g * 16 + 16)
                    for k in range(KT // 2):
                        value_fill(X.fill(g, "v"), k)
                        if k >= KT // 4:
                            score_chunk(g, 1, k - KT // 4)
                    weigh_values(g, 0, last)
                    q_k_scores(X.fill(g, "qk"), g * 2 + 1, g, 2)
                    back(g, 0)
                    weigh_values(g, 1, last, (0, 1, 2, 3))
                    for c in range(4, CHUNKS):
                        score_chunk(g, 3, c)
                    back(g, 1)
                    weigh_values(g, 2, last)
                    if not last:
                        q_k_scores(X.fill(g, "next"), g * 2 + 2, g, 4)
                    back(g, 2)
                    weigh_values(g, 3, last)
                    back(g, 3)

                q_k_scores(X.first_fill, 0, 0, 0)
                with pe.Fori(0, X.TURNS - 1) as g:
                    turn(g, False)
                turn(X.TURNS - 1, True)

            def small(s, kvT):
                s, B, wq, wk, wv, wo = SMALL_OPS[s.index]
                for g in range(s.groups):
                    f = s.f_q + g
                    fill(f)
                    for c in range(s.q_tiles):
                        last = mm(ring(f)[:, 0:TOK], wq[:, c, g * P:(g + 1) * P], hT[:, c, :],
                                  start=c == 0, stop=c == s.q_tiles - 1)
                    last.then_inc(filled, 1)
                for g in range(s.groups):
                    f = s.f_k + g
                    fill(f)
                    for c in range(s.kv_tiles):
                        last = mm(ring(f)[:, 0:TOK], wk[:, c, g * P:(g + 1) * P], kvT[:, c, :],
                                  start=c == 0, stop=c == s.kv_tiles - 1)
                    last.then_inc(filled, 1)
                for k in range(QT * s.width // BANK):
                    t, n = divmod(k, s.width // BANK)
                    fill(s.f_v + k)
                    for c in range(s.kv_tiles):
                        last = mm(ring(s.f_v + k), kvT[:, c, t * P:(t + 1) * P], wv[:, c, n * BANK:(n + 1) * BANK],
                                  start=c == 0, stop=c == s.kv_tiles - 1)
                    last.then_inc(filled, 1)
                pe.wait_ge(drained, s.f_v)
                base = HEADS * s.index
                for i in range(HEADS + 5):
                    if i < HEADS:
                        if i >= 4:
                            if s.causal:
                                pe.wait_ge(sm_masked, i - 3)
                            else:
                                pe.wait_ge(sm_exp, 2 * (base + i - 3))
                        for q in range(QT):
                            last = mm(psum[:, i % 4, q * TOK:(q + 1) * TOK], B["qz"][:, i, q * P:(q + 1) * P],
                                      B["kT"][:, i // s.per, :], start=True, stop=True)
                        last.then_inc(sm_scores, 1)
                    if i >= 5:
                        hd = i - 5
                        g, j = divmod(hd, s.per)
                        pe.wait_ge(drained, s.f_t + hd + 1)
                        if j == 0 and g >= 2:
                            pe.wait_ge(sm_out, sum(SMALL_OPS[k][0].groups for k in range(s.index)) + g - 1)
                        for k in range(QT):
                            last = mm(psum[j * s.slot:(j + 1) * s.slot, ACC + g % 2, 0:TOK],
                                      B["v"][:, k, hd * s.slot:(hd + 1) * s.slot], B["pT"][:, hd % 2, k, :],
                                      start=k == 0, stop=k == QT - 1)
                        if j == s.per - 1:
                            last.then_inc(sm_pv, 1)
                    if 3 <= i < HEADS + 3:
                        hd = i - 3
                        f = s.f_t + hd
                        fill(f)
                        pe.wait_ge(sm_norm, base + hd + 1)
                        for k in range(QT):
                            for q in range(QT):
                                last = tr(ring(f)[:, k * TOK + q * P:k * TOK + (q + 1) * P],
                                          B["p"][:, hd % 4, q, k * P:(k + 1) * P], ident[:, :])
                        last.then_inc(filled, 1)
                pe.wait_ge(sm_out, sum(SMALL_OPS[k][0].groups for k in range(s.index + 1)))
                project([B["oT"][:, g, :] for g in range(s.groups)], [wo[:, g, :] for g in range(s.groups)],
                        {0: PROJ_A0, 1: PROJ_A1, 2: PROJ_A2}[s.index])

            def project(lhs, rhs, which):
                n = rhs[0].shape[-1]
                for q in range(QT):
                    for k in range(len(lhs)):
                        last = mm(psum[:, PROJ_BANK[which], q * n:(q + 1) * n], lhs[k][:, q * P:(q + 1) * P], rhs[k],
                                  start=k == 0, stop=k == len(lhs) - 1)
                last.then_inc(proj_done, 1)

            def gelu_fills(f0, w, rhs, n):
                for t in range(FT):
                    f = f0 + t
                    fill(f)
                    for c in range(n):
                        last = mm(ring(f)[:, 0:TOK], w(c, t), rhs(c), start=c == 0, stop=c == n - 1)
                    last.then_inc(filled, 1)

            def value_fill1(k):
                f = f_values[k]
                fill(f)
                for i in range(2):
                    kt = 2 * k + i
                    for c in range(CT):
                        last = mm(ring(f)[:, i * 256:(i + 1) * 256], ctxT[:, c, kt * P:(kt + 1) * P],
                                  wv_stage[:, c, :], start=c == 0, stop=c == CT - 1)
                last.then_inc(filled, 1)

            pe.wait_ge(ident_loaded, 32)
            pe.wait_ge(ln_done, LN_X0 + 1)
            transpose_tokens(f_hT0, h)
            empty_fill(1)
            pe.wait_ge(drained, f_hT0 + 1)
            cross(X0)
            pe.wait_ge(normed, 16)
            for k in range(8):
                fill(f_oT0 + k)
                for t in range(QT):
                    last = tr(ring(f_oT0 + k)[:, t * P:(t + 1) * P], o_cross0[:, t, k * P:(k + 1) * P], ident[:, :])
                last.then_inc(filled, 1)
            pe.wait_ge(drained, f_oT0 + 8)
            pe.wait_ge(w_block0_o, 48)
            project([oT0[:, k, :] for k in range(8)], [xo_w[:, k, :] for k in range(8)], PROJ_X0)
            pe.wait_ge(v_loaded1, 16)
            for k in range(EARLY_VALUES):
                value_fill1(k)

            pe.wait_ge(ln_done, LN_A0 + 1)
            transpose_tokens(f_hT1, h)
            pe.wait_ge(drained, f_hT1 + 1)
            pe.wait_ge(w_block0, 16 * 8)
            fill(f_lat)
            for c in range(CT):
                last = mm(ring(f_lat)[:, 0:TOK], a0_down[:, c, :], hT[:, c, :], start=c == 0, stop=c == CT - 1)
            last.then_inc(filled, 1)
            pe.wait_ge(drained, f_lat + 1)
            small(A0, latT)

            for k in range(EARLY_VALUES, 2 * EARLY_VALUES):
                value_fill1(k)
            pe.wait_ge(ln_done, LN_F0 + 1)
            transpose_tokens(f_hT2, h)
            pe.wait_ge(drained, f_hT2 + 1)
            fill(f_p)
            for c in range(CT):
                last = mm(ring(f_p)[0:64, 0:TOK], f_U1[:, c, :], hT[:, c, :], start=c == 0, stop=c == CT - 1)
            last.then_inc(filled, 1)
            pe.wait_ge(drained, f_p + 1)
            gelu_fills(f_g0, lambda c, t: f_V1[0:64, t * P:(t + 1) * P], lambda c: lowT[0:64, :], 1)
            fill(f_q)
            pe.wait_ge(drained, f_g0 + FT)
            for t in range(FT):
                last = mm(ring(f_q)[0:64, 0:TOK], f_U2[:, t, :], gT0[:, t, :], start=t == 0, stop=t == FT - 1)
            last.then_inc(filled, 1)
            pe.wait_ge(drained, f_q + 1)
            project([low2T[0:64, :]], [f_V2[0:64, :]], PROJ_F0)

            for k in range(2 * EARLY_VALUES, 3 * EARLY_VALUES):
                value_fill1(k)
            pe.wait_ge(ln_done, LN_X1 + 1)
            transpose_tokens(f_hT3, h)
            pe.wait_ge(drained, f_hT3 + 1)
            pe.wait_ge(k_loaded, 32)

            def key_fill1(m, ch, beside=()):
                f = f_k1[m] + ch
                fill(f)
                for c in range(CT):
                    last = mm(ring(f), (wk_stage, wq_stage)[m][:, c, :], ctxT[:, c, ch * BANK:(ch + 1) * BANK],
                              start=c == 0, stop=c == CT - 1)
                    if c == CT - 1:
                        last.then_inc(filled, 1)
                    for s in beside[c:c + 1]:
                        look(0, 0, s, 48, FIRST_LOOK_BANKS)

            def make_queries(n, par, loads, stage=None):
                pe.wait_ge(q_loaded[par], loads)
                if not isinstance(n, int) or n >= 1:
                    pe.wait_ge(q_whole, n)
                if not isinstance(n, int) or n >= 3:
                    pe.wait_ge(normed1, n - 2)
                stage = (wk_stage, wq_stage)[par] if stage is None else stage
                for c in range(CT):
                    last = mm(q_psum, stage[:, c, :], hT[:, c, :], start=c == 0, stop=c == CT - 1)
                last.then_inc(q_made, 1)

            def look(n, par, s, loads, banks):
                chunk, q = divmod(s, QT)
                if s == 0:
                    pe.wait_ge(q_ready, n + 1)
                if s % (STEPS // PIECES) == 0:
                    pe.wait_ge(stack_loaded[par][s // (STEPS // PIECES)], loads)
                if s >= 2:
                    pe.wait_ge(look_used, n * STEPS + (s - 1))
                for j in range(2):
                    last = mm(psum[:, banks[s % 2] + j, :], q_stack[par][:, j, q * P:(q + 1) * P],
                              stack[par][:, chunk * BANK:(chunk + 1) * BANK], start=True, stop=True)
                last.then_inc(look_ready, 1)

            def turn_maxima(n):
                pe.wait_ge(neg_ready, n + 1)
                for j in range(2):
                    for q in range(QT):
                        last = tr(psum[0:2, 0, j * TOK + q * P:j * TOK + (q + 1) * P], neg_parts[:, q, j, :], ident[:, :])
                last.then_inc(neg_turned, 1)

            def transposed_scores(n, par, g, i):
                if g == 0 and i == 0:
                    pe.wait_ge(neg_placed, n + 1)
                kt = 2 * g + i
                pe.wait_ge(st_exp, n * KT + (kt + 1))
                ins = mm(psum[:, 2 + i, :], stack[par][:, kt * P:(kt + 1) * P],
                         q_stack[par][:, :, :].rearrange("p j q -> p (j q)"), start=True, stop=True)
                ins.then_inc(st_ready, 1)

            def sum_values(n, par, g):
                if g == 0:
                    pe.wait_ge(values_copied, n + 1)
                    if not isinstance(n, int) or n >= 1:
                        pe.wait_ge(acc1_copied, n)
                pe.wait_ge(st_exp, n * KT + (2 * g + 4))
                for i in range(2):
                    for j in range(2):
                        at = 32 * (2 * j + i)
                        ins = mm(psum[at:at + 32, ACC, 0:TOK], pair_values[:, par, 2 * g + i, j, :],
                                 probsT1[:, g % 2, i, j, :], start=g == 0, stop=g == GROUPS - 1,
                                 tile_position=(0, at))
                ins.then_inc(probs_used, 1)

            def fold_pair(n, queries):
                pe.wait_ge(acc1_copied, n + 1)
                pe.wait_ge(q_whole, queries)
                for q in range(QT):
                    ins = mm(psum[:, BACK, q * 64:(q + 1) * 64], acc1_sb[:, q * P:(q + 1) * P], fold[:, :],
                             start=True, stop=True)
                ins.then_inc(folded, 1)

            def attend_pair(n, par, first, last, loads):
                s = 0
                for g in range(GROUPS):
                    if g == QUERIES_AT and not last:
                        make_queries(n + 2, par, (loads + 1 if par == 0 else loads) * 16)
                    if not last:
                        for _ in range(LOOKS[g]):
                            look(n + 1, 1 - par, s, loads * 48, LOOK_BANKS)
                            s += 1
                    if g == GROUPS - 1 and not last:
                        turn_maxima(n + 1)
                    if g > 0:
                        sum_values(n, par, g - 1)
                    elif not first:
                        sum_values(n - 1, 1 - par, GROUPS - 1)
                    for i in range(2):
                        if g + 1 < GROUPS:
                            transposed_scores(n, par, g + 1, i)
                        elif not last:
                            transposed_scores(n + 1, 1 - par, 0, i)
                    if g == 4 and not first:
                        fold_pair(n - 1, PAIRS + 1 if last else n + 2)
                if last:
                    sum_values(n, par, GROUPS - 1)

            for ch in range(CHUNKS):
                key_fill1(0, ch)
            for k in range(3 * EARLY_VALUES, KT // 2):
                value_fill1(k)
            make_queries(0, 0, 16)
            for ch in range(CHUNKS):
                if ch == LOOK_BEHIND:
                    pe.wait_ge(mask_placed, 64)
                at = QT * (ch - LOOK_BEHIND)
                key_fill1(1, ch, range(at, at + QT) if at >= 0 else ())
                if ch == 2:
                    make_queries(1, 1, 16, q1_stage)
            for s in range(STEPS - QT * LOOK_BEHIND, STEPS):
                look(0, 0, s, 48, FIRST_LOOK_BANKS)
            pe.wait_ge(drained, f_oT1)
            turn_maxima(0)
            for i in range(2):
                transposed_scores(0, 0, 0, i)
            attend_pair(0, 0, True, False, 1)
            with pe.Fori(0, PAIRS // 2 - 1) as t:
                attend_pair(t * 2 + 1, 1, False, False, t + 2)
                attend_pair(t * 2 + 2, 0, False, False, t + 2)
            attend_pair(PAIRS - 1, 1, False, True, 0)
            pe.wait_ge(normed1, PAIRS - 1)
            fold_pair(PAIRS - 1, PAIRS + 1)
            pe.wait_ge(normed1, PAIRS)
            transpose_tokens(f_oT1, o_cross1)
            pe.wait_ge(drained, f_oT1 + 1)
            pe.wait_ge(w_co, 16)
            project([hT[:, c, :] for c in range(CT)], [co_w[:, c, :] for c in range(CT)], PROJ_C)

            pe.wait_ge(x_updated, UP_CO + 1)
            transpose_tokens(f_xT4, h)
            pe.wait_ge(drained, f_xT4 + 1)
            pe.wait_ge(w_block1, 16 * 6)
            small(A1, hT)

            pe.wait_ge(x_updated, UP_SO + 1)
            transpose_tokens(f_xT5, h)
            pe.wait_ge(drained, f_xT5 + 1)
            gelu_fills(f_g1, lambda c, t: fi_w[:, c, t * P:(t + 1) * P], lambda c: hT[:, c, :], CT)
            pe.wait_ge(drained, f_g1 + FT)
            project([gT1[:, t, :] for t in range(FT)], [fo_w[:, t, :] for t in range(FT)], PROJ_FI)

            pe.wait_ge(ln_done, LN_A2 + 1)
            transpose_tokens(f_hT6, h)
            pe.wait_ge(drained, f_hT6 + 1)
            pe.wait_ge(w_attn2, 16 * 5)
            small(A2, hT)

            pe.wait_ge(ln_done, LN_MOE + 1)
            transpose_tokens(f_hT7, h)
            for f in range(f_hT7 + 1, f_moe):
                empty_fill(f)
            pe.wait_ge(drained, f_hT7 + 1)
            project([hT[:, c, :] for c in range(CT)], [switch_w[:, c, :] for c in range(CT)], PROJ_ROUTE)

            def hidden(k, f, loads):
                pe.wait_ge(w1_loaded[k], loads)
                for t in range(FT):
                    fill(f + t)
                    for c in range(CT):
                        last = mm(psum[:, 4 + t % 2, 0:TOK], w1[k][:, c, t * P:(t + 1) * P], hT[:, c, :],
                                  start=c == 0, stop=c == CT - 1)
                    last.then_inc(filled, 1)

            def output(k, f, added, loads):
                pe.wait_ge(w2_loaded[k], loads)
                pe.wait_ge(drained, f)
                if added is not None:
                    pe.wait_ge(moe_added, added)
                for q in range(QT):
                    for t in range(FT):
                        last = mm(psum[:, ACC + k, q * CH:(q + 1) * CH], moe_hT[k][:, t, q * P:(q + 1) * P],
                                  w2[k][:, t, :], start=t == 0, stop=t == FT - 1)
                last.then_inc(moe_y, 1)

            hidden(0, f_moe, 16)
            pe.wait_ge(sm_max, HEADS * 3 + 1)
            with pe.Fori(0, EXPERTS // 2 - 1) as i:
                hidden(1, i * (2 * FT) + (f_moe + FT), i * 16 + 16)
                output(0, i * (2 * FT) + (f_moe + FT), i * 2 + 1, i * 16 + 16)
                hidden(0, i * (2 * FT) + (f_moe + 2 * FT), i * 16 + 32)
                output(1, i * (2 * FT) + (f_moe + 2 * FT), i * 2 + 2, i * 16 + 16)
            n = EXPERTS // 2 - 1
            hidden(1, f_moe + (EXPERTS - 1) * FT, 16 * n + 16)
            output(0, f_moe + (EXPERTS - 1) * FT, 2 * n + 1, 16 * n + 16)
            output(1, f_moe + EXPERTS * FT, 2 * n + 2, 16 * n + 16)

        @block.vector
        def _(dve):
            v = nc.vector
            links = [0]

            def link(ins):
                links[0] += 1
                ins.then_inc(link_sem, 1)
                dve.wait_ge(link_sem, links[0])

            def norm(src, dst, ln, gain=None, offset=None, up=None):
                for t in range(QT):
                    ins = v.bn_stats(stats[:, t, :], src[:, t, :])
                link(ins)
                for t in range(QT):
                    ins = v.bn_aggr(mean_var[:, t, :], stats[:, t, :])
                link(ins)
                v.tensor_scalar(mean_var[:, :, 1], mean_var[:, :, 1], EPS, None, ALU.add).then_inc(ln_var, 1)
                dve.wait_ge(ln_dev, ln + 1)
                link(v.reciprocal(deviation[:, :], deviation[:, :]))
                for t in range(QT):
                    if gain is None:
                        ins = v.tensor_scalar(dst[:, t, :], src[:, t, :], mean_var[:, t, 0:1], deviation[:, t:t + 1],
                                              ALU.subtract, ALU.mult)
                    else:
                        ins = v.scalar_tensor_tensor(out=src[:, t, :], in0=src[:, t, :], scalar=mean_var[:, t, 0:1],
                                                     in1=gain, op0=ALU.subtract, op1=ALU.mult)
                ins.then_inc(ln_done, 1)
                dve.wait_ge(ln_done, ln + 1)
                if gain is not None:
                    for t in range(QT):
                        ins = v.scalar_tensor_tensor(out=dst[:, t, :], in0=src[:, t, :], scalar=deviation[:, t:t + 1],
                                                     in1=offset[t], op0=ALU.mult, op1=ALU.add)
                    ins.then_inc(x_updated, 1)
                    dve.wait_ge(x_updated, up + 1)

            def both(r):
                return r.unsqueeze(1).to_broadcast([P, QT, CH])

            def add_projection(which, bias, residual, dst, up, transposed=None):
                y = psum[:, PROJ_BANK[which], :].rearrange("p (t c) -> p t c", t=QT)
                if bias is not None:
                    if transposed is not None:
                        dve.wait_ge(filled, transposed + 1)
                    link(v.tensor_tensor(o_cross1[:, :, :], residual, both(bias), ALU.add))
                    residual = o_cross1[:, :, :]
                dve.wait_ge(proj_done, which + 1)
                ins = v.tensor_tensor(dst, y, residual, ALU.add)
                if up is not None:
                    ins.then_inc(x_updated, 1)
                    dve.wait_ge(x_updated, up + 1)
                else:
                    link(ins)

            def cross(X, o, bias_row):
                per_unit = 3

                def low_queries0(m):
                    dve.wait_ge(q_high0, m + 1)
                    for j in range(2):
                        own, other = slice(64 * j, 64 * (j + 1)), slice(64 * (1 - j), 64 * (2 - j))
                        for part, to in ((0, other), (1, own)):
                            ins = v.tensor_tensor(q_split[to, j, part, :], q_whole0[own, :], q_split[own, j, 0, :],
                                                  ALU.subtract)
                    ins.then_inc(q_low0, 1)

                def low_keys0(m, c):
                    for j in range(2):
                        own, other = slice(64 * j, 64 * (j + 1)), slice(64 * (1 - j), 64 * (2 - j))
                        dve.wait_ge(keys_high0, m * (2 * CHUNKS) + (2 * c + j + 1))
                        dve.sem_inc(dve_passed)
                        ins = v.scalar_tensor_tensor(
                            out=keys_split[other, j, c * BANK:(c + 1) * BANK], in0=psum[own, 4 + c % 2, :],
                            scalar=cols[own, bass.ds(m + COLS["xk"][0], 1)],
                            in1=keys_split[own, j, c * BANK:(c + 1) * BANK], op0=ALU.add, op1=ALU.subtract)
                    ins.then_inc(drained, 1)

                def unit(g, u, tile=None):
                    q = u % 2
                    n = g * 4 + u
                    c0 = g * (4 * per_unit) + u * per_unit
                    if tile is not None:
                        low_queries0(tile)
                        low_keys0(tile, 0)
                    for c in range(CHUNKS):
                        if tile is not None and c + 1 < CHUNKS:
                            low_keys0(tile, c + 1)
                        chunk = side[:, q, :, c * BANK:(c + 1) * BANK]
                        if c % 2 == 0:
                            dve.wait_ge(side_loaded[q][c // 2], g * 32 + 16 * (u // 2 + 1))
                        dve.wait_ge(scores_ready, g * (4 * CHUNKS) + (u * CHUNKS + c + 1))
                        v.tensor_tensor(chunk, psum[:, 2 * (c % 2):2 * (c % 2) + 2, :], chunk, ALU.mult
                                        ).then_inc(scores_used, 1)
                    dve.wait_ge(scores_used, g * (4 * CHUNKS) + (u + 1) * CHUNKS)
                    dve.wait_ge(mask_loaded, g * 64 + 16 * (u + 1))
                    dve.sem_inc(dve_passed)
                    for j in range(2):
                        ins = v.tensor_tensor_reduce(
                            out=side[:, q, j, :], in0=side[:, q, j, :], in1=masks[:, j, :], scale=1.0,
                            scalar=-3.0e38, op0=ALU.subtract, op1=ALU.max, accum_out=row_max[:, j:j + 1])
                    ins.then_inc(masked, 1)
                    dve.wait_ge(masked, n + 1)
                    v.tensor_scalar(no_key[:, 0, :], row_max[:, :], -0.5, 3.0e38, ALU.is_lt, ALU.mult
                                    ).then_inc(cross_link, 1)
                    dve.wait_ge(cross_link, c0 + 1)
                    v.tensor_scalar(no_key[:, 1, :], no_key[:, 0, :], 10.0, None, ALU.mult).then_inc(cross_link, 1)
                    dve.wait_ge(cross_link, c0 + 2)
                    v.tensor_tensor(no_key[:, 2, :], no_key[:, 1, :], no_key[:, 1, :], ALU.subtract
                                    ).then_inc(cross_link, 1)
                    dve.wait_ge(cross_link, c0 + 3)
                    v.scalar_tensor_tensor(out=exp_bias[:, q, :], in0=row_max[:, :], scalar=-1.0 / TINY,
                                           in1=no_key[:, 2, :], op0=ALU.mult, op1=ALU.add).then_inc(bias_ready, 1)

                def normalise(g, u):
                    n = g * 4 + u
                    dve.wait_ge(exp_done, g * (8 * PIECES) + 2 * PIECES * (u + 1))
                    v.tensor_reduce(row_sum[:, u, :], piece_sum[:, u, :, :], AX.X, ALU.add).then_inc(norm_link, 1)
                    dve.wait_ge(norm_link, n * 2 + 1)
                    dve.wait_ge(acc_back, n + 1)
                    v.reciprocal(row_inv[:, u, :], row_sum[:, u, :]).then_inc(norm_link, 1)
                    dve.wait_ge(norm_link, n * 2 + 2)
                    for j in range(2):
                        at = (g * 4 + (2 * (u // 2) + j)) * D0
                        ins = v.scalar_tensor_tensor(
                            out=o[:, u % 2, bass.ds(at, D0)], in0=psum[:, BACK, 64 * j:64 * j + D0],
                            scalar=row_inv[:, u, j:j + 1], in1=bias_row[:, bass.ds(at, D0)],
                            op0=ALU.mult, op1=ALU.add)
                    ins.then_inc(normed, 1)

                def turn(g, last):
                    unit(g, 1)
                    unit(g, 2, g * 2 + 1)
                    normalise(g, 0)
                    unit(g, 3)
                    normalise(g, 1)
                    if not last:
                        unit(g, 4, g * 2 + 2)
                    normalise(g, 2)
                    normalise(g, 3)

                unit(0, 0, 0)
                dve.wait_ge(rows_loaded, 16)
                with dve.Fori(0, X.TURNS - 1) as g:
                    turn(g, False)
                turn(X.TURNS - 1, True)

            def small(s, v_bias):
                s, B = SMALL_OPS[s.index][:2]
                base = HEADS * s.index
                ot = sum(SMALL_OPS[k][0].groups for k in range(s.index))
                for i in range(HEADS + 5):
                    if i < HEADS:
                        dve.wait_ge(sm_scores, base + i + 1)
                        scores = psum[:, i % 4, :].rearrange("p (q k) -> p q k", q=QT)
                        if s.causal:
                            if i >= 2:
                                dve.wait_ge(sm_exp, 2 * (base + i - 1))
                            for q in range(QT):
                                ins = v.tensor_tensor_reduce(
                                    out=B["masked"][:, i % 2, q, :], in0=scores[:, q, :], in1=causal[:, q, :],
                                    scale=1.0, scalar=-3.0e38, op0=ALU.add, op1=ALU.max,
                                    accum_out=s_top[:, i % 2, q:q + 1])
                            ins.then_inc(sm_masked, 1)
                            dve.wait_ge(sm_masked, i + 1)
                            v.tensor_scalar(s_max[:, i % 4, :], s_top[:, i % 2, :], -1.0, None, ALU.mult
                                            ).then_inc(sm_max, 1)
                        else:
                            v.tensor_reduce(s_max[:, i % 4, :], scores, AX.X, ALU.max, negate=True).then_inc(sm_max, 1)
                    if 2 <= i < HEADS + 2:
                        hd = i - 2
                        dve.wait_ge(sm_exp, 2 * (base + hd + 1))
                        link(v.reciprocal(s_inv[:, hd % 4, :], s_sum[:, hd % 4, :]))
                        for q in range(QT):
                            ins = v.tensor_scalar(B["p"][:, hd % 4, q, :], B["p"][:, hd % 4, q, :],
                                                  s_inv[:, hd % 4, q:q + 1], None, ALU.mult)
                        ins.then_inc(sm_norm, 1)
                    hd = i - 5
                    if hd >= 0 and hd % s.per == s.per - 1:
                        g = hd // s.per
                        dve.wait_ge(sm_pv, ot + g + 1)
                        if v_bias:
                            v.tensor_scalar(B["oT"][:, g, :], psum[:, ACC + g % 2, 0:TOK], col(v_bias, g), None,
                                            ALU.add).then_inc(sm_out, 1)
                        else:
                            v.tensor_copy(B["oT"][:, g, :], psum[:, ACC + g % 2, 0:TOK]).then_inc(sm_out, 1)

            v.memset(acc_sb[:, :], 0.0)
            dve.wait_ge(cols_loaded, 16)
            for at, name, scale in ((0, "xq", TINY * D0**-0.5), (8, "cq", D1**-0.5), (24, "sq", D1**-0.5)):
                n = COLS[name][1]
                ins = v.tensor_scalar(q_bias[:, at:at + n], cols[:, COLS[name][0]:COLS[name][0] + n], scale, None, ALU.mult)
            ins.then_inc(q_bias_ready, 1)
            dve.wait_ge(x_loaded, 16)
            norm(x, h, LN_X0)
            cross(X0, o_cross0, row("xv"))
            add_projection(PROJ_X0, row("xo"), x[:, :, :], x[:, :, :], UP_X0, f_oT0 + 7)
            norm(x, h, LN_A0)
            dve.wait_ge(w_block0_o, 48)
            small(A0, None)
            add_projection(PROJ_A0, None, x[:, :, :], x[:, :, :], UP_A0)
            norm(x, h, LN_F0)
            add_projection(PROJ_F0, row("f2"), x[:, :, :], x[:, :, :], UP_F0)
            norm(x, h, LN_X1)

            def low_key1(m, c):
                dve.wait_ge(keys_high, m * CHUNKS + c + 1)
                v.scalar_tensor_tensor(out=key_parts[:, m, 1, c * BANK:(c + 1) * BANK],
                                       in0=ring(f_k1[m] + c), scalar=col("ck", m),
                                       in1=key_parts[:, m, 0, c * BANK:(c + 1) * BANK],
                                       op0=ALU.add, op1=ALU.subtract).then_inc(drained, 1)

            for c in range(CHUNKS):
                low_key1(0, c)
                dve.wait_ge(drained, f_k1[0] + c + 1)
                dve.sem_inc(keys_low)
            dve.wait_ge(key_mask_loaded, 16)
            link(v.memset(ones[96:128, :], 1.0))
            for b in range(2):
                ins = v.tensor_copy(stack[b][96:128, :].rearrange("p (c k) -> p c k", c=CHUNKS),
                                    ones[96:128, :].unsqueeze(1).to_broadcast([32, CHUNKS, BANK]))
            link(ins)
            link(v.tensor_scalar(mask_raw, mask_raw, -3.0e38, None, ALU.max))
            link(v.tensor_copy(mask_parts[:, 0, :], mask_raw))
            v.tensor_tensor(mask_parts[:, 1, :], mask_raw, mask_parts[:, 0, :], ALU.subtract).then_inc(mask_split, 1)
            LINKS = 2

            def pair_linked(ins, n, k):
                ins.then_inc(pair_link, 1)
                dve.wait_ge(pair_link, n * LINKS + k)

            def low_queries(n):
                dve.wait_ge(q_rounding, n + 1)
                dve.sem_inc(dve_passed)
                v.tensor_tensor(q_next[64:96, :, :], q_next[64:96, :, :], q_rounded[64:96, :, :], ALU.subtract
                                ).then_inc(q_split_done, 1)

            def maxima(n, steps, banks):
                for s in steps:
                    chunk, q = divmod(s, QT)
                    dve.wait_ge(look_ready, n * STEPS + (s + 1))
                    v.tensor_reduce(pair_max[:, q, :, chunk], psum[:, banks[s % 2]:banks[s % 2] + 2, :], AX.X, ALU.max
                                    ).then_inc(look_used, 1)

            def place_maxima(n, par):
                dve.wait_ge(look_used, (n + 1) * STEPS)
                pair_linked(v.tensor_reduce(neg_max, pair_max, AX.X, ALU.max, negate=True), n, 1)
                pair_linked(v.tensor_copy(neg_parts[:, :, :, 0].bitcast(F32R), neg_max), n, 2)
                v.tensor_tensor(neg_parts[:, :, :, 1], neg_max, neg_parts[:, :, :, 0], ALU.subtract
                                ).then_inc(neg_ready, 1)
                dve.wait_ge(neg_turned, n + 1)
                v.tensor_copy(q_stack[par][96:98, :, :], psum[0:2, 0, :].rearrange("p (j q) -> p j q", j=2)
                              ).then_inc(neg_placed, 1)

            def normalise_pair(n):
                dve.wait_ge(folded, n + 1)
                back = psum[:, BACK, 0:QT * 64].rearrange("p (q j d) -> p q j d", q=QT, j=2)
                v.reciprocal(sum_inv.unsqueeze(3), back[:, :, :, D1:D1 + 1]).then_inc(norm1_link, 1)
                dve.wait_ge(norm1_link, n * 2 + 1)
                v.tensor_tensor(scaled, back[:, :, :, 0:D1], sum_inv.unsqueeze(3).to_broadcast([P, QT, 2, D1]), ALU.mult
                                ).then_inc(norm1_link, 1)
                dve.wait_ge(norm1_link, n * 2 + 2)
                at = ROWS["cv"][0]
                v.tensor_tensor(o_cross1[:, :, bass.ds(n * 2 * D1, 2 * D1)], scaled.rearrange("p q j d -> p q (j d)"),
                                rows[:, bass.ds(n * 2 * D1 + at, 2 * D1)].unsqueeze(1).to_broadcast([P, QT, 2 * D1]),
                                ALU.add).then_inc(normed1, 1)

            def attend_pair(n, par, first):
                at = [sum(LOOKS[:6]), sum(LOOKS[:QUERIES_AT + 4])]
                maxima(n + 1, range(at[0]), LOOK_BANKS)
                if not first:
                    normalise_pair(n - 1)
                maxima(n + 1, range(at[0], at[1]), LOOK_BANKS)
                low_queries(n + 2)
                maxima(n + 1, range(at[1], STEPS), LOOK_BANKS)
                place_maxima(n + 1, 1 - par)

            low_queries(0)
            for c in range(CHUNKS):
                if c >= LOOK_BEHIND:
                    maxima(0, range(QT * (c - LOOK_BEHIND), QT * (c - LOOK_BEHIND + 1)), FIRST_LOOK_BANKS)
                low_key1(1, c)
                if c == 3:
                    low_queries(1)
            dve.wait_ge(drained, f_oT1)
            dve.sem_inc(keys_low)
            maxima(0, range(STEPS - QT * LOOK_BEHIND, STEPS), FIRST_LOOK_BANKS)
            place_maxima(0, 0)
            attend_pair(0, 0, True)
            with dve.Fori(0, PAIRS // 2 - 1) as t:
                attend_pair(t * 2 + 1, 1, False)
                attend_pair(t * 2 + 2, 0, False)
            normalise_pair(PAIRS - 2)
            normalise_pair(PAIRS - 1)
            dve.wait_ge(late_loaded, 16)
            add_projection(PROJ_C, row("co_b"), h[:, :, :], h[:, :, :], None, f_oT1)
            norm(h, h, LN_CO, row("co_g"), [row("co_be")] * QT, UP_CO)
            small(A1, "sv")
            add_projection(PROJ_A1, row("so_b"), h[:, :, :], h[:, :, :], None)
            norm(h, h, LN_SO, row("so_g"), [row("so_be")] * QT, UP_SO)
            link(v.tensor_tensor(x_offset, x[:, :, :], both(row("fo_be")), ALU.add))
            add_projection(PROJ_FI, row("fo_b"), h[:, :, :], h[:, :, :], None)
            norm(h, x, LN_FO, row("fo_g"), [x_offset[:, t, :] for t in range(QT)], UP_FO)
            norm(x, h, LN_A2)
            small(A2, None)
            add_projection(PROJ_A2, row("lo"), x[:, :, :], x[:, :, :], UP_A2)
            norm(x, h, LN_MOE)
            dve.wait_ge(proj_done, PROJ_ROUTE + 1)
            logits = psum[:, PROJ_BANK[PROJ_ROUTE], 0:QT * EXPERTS].rearrange("p (q e) -> p q e", q=QT)
            link(v.tensor_tensor(route[:, :, 0, :], logits,
                                 row("switch").unsqueeze(1).to_broadcast([P, QT, EXPERTS]), ALU.add))
            v.tensor_reduce(s_max[:, 0, :], route[:, :, 0, :], AX.X, ALU.max, negate=True).then_inc(sm_max, 1)
            dve.wait_ge(sm_max, HEADS * 3 + 1)
            for q in range(QT):
                ins = v.tensor_scalar(route[:, q, 2, :], route[:, q, 0, :], s_max[:, 0, q:q + 1], 0.0,
                                      ALU.add, ALU.is_equal)
            link(ins)
            link(v.tensor_tensor(route[:, :, 3, :], route[:, :, 2, :],
                                 row("rank").unsqueeze(1).to_broadcast([P, QT, EXPERTS]), ALU.mult))
            link(v.tensor_reduce(s_inv[:, 1, :], route[:, :, 3, :], AX.X, ALU.max))
            for q in range(QT):
                ins = v.tensor_scalar(route[:, q, 4, :], route[:, q, 3, :], s_inv[:, 1, q:q + 1], None, ALU.is_equal)
            link(ins)
            dve.wait_ge(route_exp, QT)
            link(v.reciprocal(s_inv[:, 0, :], s_sum[:, 0, :]))
            for q in range(QT):
                ins = v.tensor_scalar(coef[:, q, :], route[:, q, 4, :], s_inv[:, 0, q:q + 1], None, ALU.mult)
            link(ins)
            dve.wait_ge(b2_loaded, 16)
            v.sem_inc(moe_added, 2)

            def add_expert(k, e, done):
                dve.wait_ge(moe_y, done)
                v.tensor_tensor(h[:, :, :], psum[:, ACC + k, :].rearrange("p (q c) -> p q c", q=QT),
                                b2_rows[:, bass.ds(e, 1), :].to_broadcast([P, QT, CH]), ALU.add).then_inc(moe_link, 1)
                dve.wait_ge(moe_link, done)
                for q in range(QT):
                    ins = v.scalar_tensor_tensor(out=x[:, q, :], in0=h[:, q, :], scalar=coef[:, q, bass.ds(e, 1)],
                                                 in1=x[:, q, :], op0=ALU.mult, op1=ALU.add)
                ins.then_inc(moe_added, 1)
                dve.wait_ge(moe_added, done + 2)

            with dve.Fori(0, EXPERTS // 2) as i:
                add_expert(0, i * 2, i * 2 + 1)
                add_expert(1, i * 2 + 1, i * 2 + 2)


def padded(w, d, slot):
    out = np.zeros((w.shape[0], w.shape[1] // d, slot), w.dtype)
    out[:, :, :d] = w.reshape(w.shape[0], -1, d)
    return out.reshape(w.shape[0], -1)


def tiles(b):
    return b.reshape(-1, P).T


def pairs_repeated(w):
    by_pair = w.reshape(w.shape[0], PAIRS, 1, 32)
    return np.concatenate([by_pair] * 3 + [np.zeros_like(by_pair)], 2).reshape(w.shape[0], -1)


def head_bias(b):
    out = np.zeros((P, HEADS), b.dtype)
    for head in range(HEADS):
        for block in range(3):
            at = 32 * block + D1 * (head % 2)
            out[at:at + D1, head] = b[head * D1:(head + 1) * D1]
    out[100:102] = 4.0
    return out


def picks():
    out = np.zeros((P, 2), np.float32)
    for j in range(2):
        for block in range(3):
            out[32 * block + D1 * j:32 * block + D1 * (j + 1), j] = D1**-0.5
    return out


def laid_out(i):
    g = {k: np.asarray(w) for k, w in i.items()}
    pads = lambda b, d: padded(b.reshape(1, -1), d, 32)[0]
    cols = {"xq": tiles(g["L0_xattn_bq"]), "xk": tiles(g["L0_xattn_bk"]), "f1": tiles(g["L0_ffn_b1"]),
            "cq": head_bias(g["L1_xattn_cq_b"]), "ck": tiles(g["L1_xattn_ck_b"]), "pick": picks(),
            "sq": tiles(pads(g["L1_xattn_sq_b"], D1)), "sk": tiles(pads(g["L1_xattn_sk_b"], D1)),
            "sv": tiles(pads(g["L1_xattn_sv_b"], D1)), "fi": tiles(g["L1_xattn_fi_b"]),
            "m1": tiles(g["L1_ffn_b1"].reshape(-1))}
    rows = {"xv": g["L0_xattn_bv"], "xo": g["L0_xattn_bo"], "f2": g["L0_ffn_b2"], "cv": g["L1_xattn_cv_b"],
            **{f"{s}_{p}": g[f"L1_xattn_{s}_{p}"] for s in ("co", "so", "fo") for p in ("b", "g", "be")},
            "lo": g["L1_attn_bo"], "switch": g["L1_ffn_switch_b"],
            "rank": np.arange(EXPERTS, 0, -1, dtype=np.float32)}
    causal = np.where(np.tril(np.ones((TOK, TOK), bool)), 0.0, -1e30).astype(np.float32)
    out = {
        "x": g["x"][0], "ctxT": g["ctx_1024"][0].T, "side": g["fside_Bx16xSxS2_0"][0],
        "mask": g["mask_Bx16xSxS2_bk1"][0], "key_mask": g["mask_Bx1x1xS2_ff0"].reshape(P, KEYS // P),
        "ident": np.eye(P, dtype=np.float32),
        "fold": np.kron(np.eye(2), np.tile(np.eye(32), (2, 1))).astype(np.float32), "causal": causal,
        "cols": np.concatenate([cols[k] for k in COLS], 1),
        "rows": np.concatenate([rows[k] for k in ROWS])[None], "late": np.concatenate([rows[k] for k in LATE])[None],
        "x_wq": g["L0_xattn_Wq"].T, "x_wk": g["L0_xattn_Wk"].T, "x_wv": g["L0_xattn_Wv"].T, "x_wo": g["L0_xattn_Wo"].T,
        "a_down": g["L0_attn_w_kv_down"], "a_kup": g["L0_attn_w_kv_up"][:, :1024], "a_vup": g["L0_attn_w_kv_up"][:, 1024:],
        "a_q": g["L0_attn_w_q"], "a_out": g["L0_attn_w_out"],
        "f_U1": g["L0_ffn_U1"], "f_V1": g["L0_ffn_V1"], "f_U2": g["L0_ffn_U2"], "f_V2": g["L0_ffn_V2"],
        "c_wq": pairs_repeated(g["L1_xattn_cq_w"]), "c_wk": g["L1_xattn_ck_w"],
        "c_wv": g["L1_xattn_cv_w"], "c_wo": g["L1_xattn_co_w"],
        "s_wq": padded(g["L1_xattn_sq_w"], D1, 32), "s_wk": padded(g["L1_xattn_sk_w"], D1, 32),
        "s_wv": padded(g["L1_xattn_sv_w"], D1, 32), "s_wo": padded(g["L1_xattn_so_w"].T, D1, 32).T,
        "fi_w": g["L1_xattn_fi_w"], "fo_w": g["L1_xattn_fo_w"],
        "l_wq": padded(g["L1_attn_Wq"].T, DL, 32), "l_wk": padded(g["L1_attn_Wk"].T, DL, 32),
        "l_wv": padded(g["L1_attn_Wv"].T, DL, 32), "l_wo": padded(g["L1_attn_Wo"], DL, 32).T,
        "switch_w": g["L1_ffn_switch_w"], "w1": g["L1_ffn_w1"], "w2": g["L1_ffn_w2"], "b2": g["L1_ffn_b2"].reshape(1, -1),
    }
    return {k: np.ascontiguousarray(w) for k, w in out.items()}


def kernel(**inputs):
    from concourse import bacc as _bacc
    from concourse import mybir as _mybir
    from concourse.bass_utils import run_bass_kernel_spmd as _run

    nc = _bacc.Bacc("TRN2", target_bir_lowering=False, num_devices=1)
    arrays, aps = {}, {}
    for name, w in laid_out(inputs).items():
        arrays[f"in_{name}"] = w
        aps[name] = nc.dram_tensor(f"in_{name}", w.shape, _mybir.dt.from_np(w.dtype), kind="ExternalInput").ap()
    aps["out"] = nc.dram_tensor("out_x", (TOK, CH), _mybir.dt.float32, kind="ExternalOutput").ap()
    program(nc, aps)
    r = _run(nc, [arrays], core_ids=[0])
    return r.results[0]["out_x"][None]
```
